# Optimizing a Trainium2 kernel written in Bass

```python
import numpy as np
import jax
import jax.numpy as jnp

def _softmax(x, axis=-1):
    return jax.nn.softmax(x, axis=axis)

def _gelu(x):
    return jax.nn.gelu(x, approximate=True)

def _silu(x):
    return jax.nn.silu(x)

def _sigmoid(x):
    return jax.nn.sigmoid(x)

def _layernorm(x, axis=-1, eps=1e-05):
    m = jnp.mean(x, axis=axis, keepdims=True)
    v = jnp.var(x, axis=axis, keepdims=True)
    return (x - m) / jnp.sqrt(v + eps)

def _scatter_add(tgt, idx, src, axis=0):
    return tgt.at[idx].add(src)

def _segment_sum(src, seg, n):
    return jax.ops.segment_sum(src, seg, n)
kernel_name = 'mk_gnn_resnorm_d4_gnn_r8_306404'

def setup_inputs(seed: int=0):
    np.random.seed(seed)
    _w = jnp.asarray

    def _rec_inputs():
        import jax
        import jax.numpy as jnp
        _gk = jax.random.key(seed)
        x = -0.0005121 + 1.001 * jax.random.normal(jax.random.fold_in(_gk, 1), (6250, 64), jnp.float32)
        _s = jax.random.randint(jax.random.fold_in(_gk, 2), (100000,), 0, 6250, jnp.int32)
        _d = jax.random.randint(jax.random.fold_in(_gk, 3), (100000,), 0, 6250, jnp.int32)
        _loop = jnp.arange(6250, dtype=jnp.int32)
        src = jnp.concatenate([_s, _d, _loop])
        dst = jnp.concatenate([_d, _s, _loop])
        _o = jnp.argsort(dst, stable=True)
        src = src[_o]
        dst = dst[_o]
        edge_attr_16 = 0.000196303 + 1.00016 * jax.random.normal(jax.random.fold_in(_gk, 11), (206250, 16), jnp.float32)
        edge_attr_32 = 0.000196303 + 1.00016 * jax.random.normal(jax.random.fold_in(_gk, 12), (206250, 32), jnp.float32)
        edge_attr_64 = -2.25437e-05 + 0.999858 * jax.random.normal(jax.random.fold_in(_gk, 13), (206250, 64), jnp.float32)
        edge_type_8 = jax.random.randint(jax.random.fold_in(_gk, 15), (206250,), 0, 8, jnp.int32)
        return (x, src, dst, edge_attr_16, edge_attr_32, edge_attr_64, edge_type_8)
    x, src, dst, edge_attr_16, edge_attr_32, edge_attr_64, edge_type_8 = _rec_inputs()

    def _L0_gnn_setup():
        import jax, jax.numpy as jnp
        import numpy as np
        N = 6250
        E = 100000
        D = 64
        H = 64
        DE = 32

        def _transformer_conv(x, src, dst, edge_attr, wq, bq, wk, bk, wv, bv, we, ws, bs, n_nodes):
            q = x @ wq + bq
            k = x @ wk + bk
            v = x @ wv + bv
            e = edge_attr @ we
            ke = k[src] + e
            score = jnp.sum(q[dst] * ke, axis=-1) / jnp.sqrt(jnp.asarray(ke.shape[-1], x.dtype))
            smax = jax.ops.segment_max(score, dst, num_segments=n_nodes)
            a = jnp.exp(score - smax[dst])
            denom = jax.ops.segment_sum(a, dst, num_segments=n_nodes)
            alpha = a / denom[dst]
            msg = alpha[:, None] * (v[src] + e)
            out = jax.ops.segment_sum(msg, dst, num_segments=n_nodes)
            out = out + x @ ws + bs
            return out
        key = jax.random.key(seed)
        ks = jax.random.split(key, 24)

        def g(i, shape, scale):
            return jax.random.normal(ks[i], shape, dtype=jnp.float32) * scale
        inp = {'x': g(0, (N, D), 1.0), 'edge_index': jax.random.randint(ks[1], (2, E), 0, N, dtype=jnp.int64), 'edge_attr': g(2, (E, DE), 1.0), 'q1_w': g(3, (D, H), D ** (-0.5)), 'q1_b': jnp.zeros((H,), jnp.float32), 'k1_w': g(4, (D, H), D ** (-0.5)), 'k1_b': jnp.zeros((H,), jnp.float32), 'v1_w': g(5, (D, H), D ** (-0.5)), 'v1_b': jnp.zeros((H,), jnp.float32), 'e1_w': g(6, (DE, H), DE ** (-0.5)), 's1_w': g(7, (D, H), D ** (-0.5)), 's1_b': jnp.zeros((H,), jnp.float32), 'q2_w': g(8, (H, H), H ** (-0.5)), 'q2_b': jnp.zeros((H,), jnp.float32), 'k2_w': g(9, (H, H), H ** (-0.5)), 'k2_b': jnp.zeros((H,), jnp.float32), 'v2_w': g(10, (H, H), H ** (-0.5)), 'v2_b': jnp.zeros((H,), jnp.float32), 'e2_w': g(11, (DE, H), DE ** (-0.5)), 's2_w': g(12, (H, H), H ** (-0.5)), 's2_b': jnp.zeros((H,), jnp.float32), 'skip_w': g(13, (2 * H, D), (2 * H) ** (-0.5)), 'skip_b': jnp.zeros((D,), jnp.float32)}
        return inp
    _L0_gnn_all = _L0_gnn_setup()
    _L0_gnn_in = {k: v for k, v in _L0_gnn_all.items() if k in ('q1_w', 'q1_b', 'k1_w', 'k1_b', 'v1_w', 'v1_b', 'e1_w', 's1_w', 's1_b', 'q2_w', 'q2_b', 'k2_w', 'k2_b', 'v2_w', 'v2_b', 'e2_w', 's2_w', 's2_b', 'skip_w', 'skip_b')}
    del _L0_gnn_all

    def _L1_gnn_setup():
        import jax, jax.numpy as jnp
        import numpy as np
        N_NODES, N_EDGES, C_IN, C_HID, N_REL, N_BASES, N_LAYERS = (6250, 100000, 64, 64, 8, 4, 3)

        def _rgcn_layer(h, src, dst, edge_type, basis_l, comp_l, root_l, bias_l, num_relations):
            n = h.shape[0]
            W = jnp.einsum('rb,bch->rch', comp_l, basis_l)
            seg = edge_type * n + dst
            msg = h[src]
            agg = jax.ops.segment_sum(msg, seg, num_segments=num_relations * n)
            agg = agg.reshape(num_relations, n, -1)
            cnt = jax.ops.segment_sum(jnp.ones(seg.shape, h.dtype), seg, num_segments=num_relations * n)
            cnt = cnt.reshape(num_relations, n, 1)
            agg = agg / jnp.maximum(cnt, 1.0)
            return jnp.einsum('rnc,rch->nh', agg, W) + h @ root_l + bias_l
        key = jax.random.key(seed)
        ks = jax.random.split(key, 6)
        x = jax.random.normal(ks[0], (N_NODES, C_IN), dtype=jnp.float32)
        edge_index = jax.random.randint(ks[1], (2, N_EDGES), 0, N_NODES)
        edge_type = jax.random.randint(ks[2], (N_EDGES,), 0, N_REL)
        basis = jax.random.normal(ks[3], (N_LAYERS, N_BASES, C_IN, C_HID), dtype=jnp.float32) * 0.1
        comp = jax.random.normal(ks[4], (N_LAYERS, N_REL, N_BASES), dtype=jnp.float32) * 0.5
        root = jax.random.normal(ks[5], (N_LAYERS, C_IN, C_HID), dtype=jnp.float32) * 0.1
        bias = jnp.zeros((N_LAYERS, C_HID), dtype=jnp.float32)
        return {'x': x, 'edge_index': edge_index, 'edge_type': edge_type, 'basis': basis, 'comp': comp, 'root': root, 'bias': bias}
    _L1_gnn_all = _L1_gnn_setup()
    _L1_gnn_in = {k: v for k, v in _L1_gnn_all.items() if k in ('basis', 'comp', 'root', 'bias')}
    del _L1_gnn_all

    def _L2_gnn_setup():
        import jax, jax.numpy as jnp
        import numpy as np
        LN_EPS = 1e-05
        key = jax.random.key(seed)
        ks = jax.random.split(key, 8)
        N, E, D = (12500, 125000, 64)
        node_feats = jax.random.normal(ks[0], (N, D), dtype=jnp.float32)
        edge_feats = jax.random.normal(ks[1], (E, D), dtype=jnp.float32)
        edge_index = jax.random.randint(ks[2], (2, E), 0, N, dtype=jnp.int64)
        W1 = jax.random.normal(ks[3], (D, 2 * D), dtype=jnp.float32) / np.sqrt(D)
        b1 = jnp.zeros((2 * D,), dtype=jnp.float32)
        ln_g = jnp.ones((2 * D,), dtype=jnp.float32)
        ln_b = jnp.zeros((2 * D,), dtype=jnp.float32)
        W2 = jax.random.normal(ks[4], (2 * D, D), dtype=jnp.float32) / np.sqrt(2 * D)
        b2 = jnp.zeros((D,), dtype=jnp.float32)
        eps = jnp.zeros((1,), dtype=jnp.float32)
        return {'node_feats': node_feats, 'edge_feats': edge_feats, 'W1': W1, 'b1': b1, 'ln_g': ln_g, 'ln_b': ln_b, 'W2': W2, 'b2': b2, 'eps': eps, 'edge_index': edge_index, 'num_nodes': 12500}
    _L2_gnn_all = _L2_gnn_setup()
    _L2_gnn_in = {k: v for k, v in _L2_gnn_all.items() if k in ('W1', 'b1', 'ln_g', 'ln_b', 'W2', 'b2', 'eps')}
    del _L2_gnn_all

    def _L3_gnn_setup():
        import jax, jax.numpy as jnp
        import numpy as np
        N_NODES = 12500
        N_EDGES = 200000
        IN_CH = 64
        OUT_CH = 64
        EDGE_DIM = 16
        key = jax.random.key(seed)
        ks = jax.random.split(key, 8)
        x = jax.random.normal(ks[0], (N_NODES, IN_CH), dtype=jnp.float32)
        edge_index = jax.random.randint(ks[1], (2, N_EDGES), 0, N_NODES, dtype=jnp.int64)
        edge_attr = jax.random.normal(ks[2], (N_EDGES, EDGE_DIM), dtype=jnp.float32)
        W_l = jax.random.normal(ks[3], (IN_CH, OUT_CH), dtype=jnp.float32) / np.sqrt(IN_CH)
        b_l = jnp.zeros((OUT_CH,), dtype=jnp.float32)
        W_r = jax.random.normal(ks[4], (IN_CH, OUT_CH), dtype=jnp.float32) / np.sqrt(IN_CH)
        W_e = jax.random.normal(ks[5], (EDGE_DIM, OUT_CH), dtype=jnp.float32) / np.sqrt(EDGE_DIM)
        b_e = jax.random.normal(ks[6], (OUT_CH,), dtype=jnp.float32) * 0.01
        return {'x': x, 'edge_index': edge_index, 'edge_attr': edge_attr, 'W_l': W_l, 'b_l': b_l, 'W_r': W_r, 'W_e': W_e, 'b_e': b_e}
    _L3_gnn_all = _L3_gnn_setup()
    _L3_gnn_in = {k: v for k, v in _L3_gnn_all.items() if k in ('W_l', 'b_l', 'W_r', 'W_e', 'b_e')}
    del _L3_gnn_all
    return {'x': x, 'src': src, 'dst': dst, 'edge_attr_16': edge_attr_16, 'edge_attr_32': edge_attr_32, 'edge_attr_64': edge_attr_64, 'edge_type_8': edge_type_8, 'L0_gnn_q1_w': _L0_gnn_in['q1_w'], 'L0_gnn_q1_b': _L0_gnn_in['q1_b'], 'L0_gnn_k1_w': _L0_gnn_in['k1_w'], 'L0_gnn_k1_b': _L0_gnn_in['k1_b'], 'L0_gnn_v1_w': _L0_gnn_in['v1_w'], 'L0_gnn_v1_b': _L0_gnn_in['v1_b'], 'L0_gnn_e1_w': _L0_gnn_in['e1_w'], 'L0_gnn_s1_w': _L0_gnn_in['s1_w'], 'L0_gnn_s1_b': _L0_gnn_in['s1_b'], 'L0_gnn_q2_w': _L0_gnn_in['q2_w'], 'L0_gnn_q2_b': _L0_gnn_in['q2_b'], 'L0_gnn_k2_w': _L0_gnn_in['k2_w'], 'L0_gnn_k2_b': _L0_gnn_in['k2_b'], 'L0_gnn_v2_w': _L0_gnn_in['v2_w'], 'L0_gnn_v2_b': _L0_gnn_in['v2_b'], 'L0_gnn_e2_w': _L0_gnn_in['e2_w'], 'L0_gnn_s2_w': _L0_gnn_in['s2_w'], 'L0_gnn_s2_b': _L0_gnn_in['s2_b'], 'L0_gnn_skip_w': _L0_gnn_in['skip_w'], 'L0_gnn_skip_b': _L0_gnn_in['skip_b'], 'L1_gnn_basis': _L1_gnn_in['basis'], 'L1_gnn_comp': _L1_gnn_in['comp'], 'L1_gnn_root': _L1_gnn_in['root'], 'L1_gnn_bias': _L1_gnn_in['bias'], 'L2_gnn_W1': _L2_gnn_in['W1'], 'L2_gnn_b1': _L2_gnn_in['b1'], 'L2_gnn_ln_g': _L2_gnn_in['ln_g'], 'L2_gnn_ln_b': _L2_gnn_in['ln_b'], 'L2_gnn_W2': _L2_gnn_in['W2'], 'L2_gnn_b2': _L2_gnn_in['b2'], 'L2_gnn_eps': _L2_gnn_in['eps'], 'L3_gnn_W_l': _L3_gnn_in['W_l'], 'L3_gnn_b_l': _L3_gnn_in['b_l'], 'L3_gnn_W_r': _L3_gnn_in['W_r'], 'L3_gnn_W_e': _L3_gnn_in['W_e'], 'L3_gnn_b_e': _L3_gnn_in['b_e']}

def reference(x, src, dst, edge_attr_16, edge_attr_32, edge_attr_64, edge_type_8, L0_gnn_q1_w, L0_gnn_q1_b, L0_gnn_k1_w, L0_gnn_k1_b, L0_gnn_v1_w, L0_gnn_v1_b, L0_gnn_e1_w, L0_gnn_s1_w, L0_gnn_s1_b, L0_gnn_q2_w, L0_gnn_q2_b, L0_gnn_k2_w, L0_gnn_k2_b, L0_gnn_v2_w, L0_gnn_v2_b, L0_gnn_e2_w, L0_gnn_s2_w, L0_gnn_s2_b, L0_gnn_skip_w, L0_gnn_skip_b, L1_gnn_basis, L1_gnn_comp, L1_gnn_root, L1_gnn_bias, L2_gnn_W1, L2_gnn_b1, L2_gnn_ln_g, L2_gnn_ln_b, L2_gnn_W2, L2_gnn_b2, L2_gnn_eps, L3_gnn_W_l, L3_gnn_b_l, L3_gnn_W_r, L3_gnn_W_e, L3_gnn_b_e):
    import jax
    import jax.numpy as jnp

    def _L0_gnn_ref(x, edge_index, edge_attr, q1_w, q1_b, k1_w, k1_b, v1_w, v1_b, e1_w, s1_w, s1_b, q2_w, q2_b, k2_w, k2_b, v2_w, v2_b, e2_w, s2_w, s2_b, skip_w, skip_b):
        import jax, jax.numpy as jnp
        import numpy as np
        N = 6250
        E = 100000
        D = 64
        H = 64
        DE = 32

        def _transformer_conv(x, src, dst, edge_attr, wq, bq, wk, bk, wv, bv, we, ws, bs, n_nodes):
            q = x @ wq + bq
            k = x @ wk + bk
            v = x @ wv + bv
            e = edge_attr @ we
            ke = k[src] + e
            score = jnp.sum(q[dst] * ke, axis=-1) / jnp.sqrt(jnp.asarray(ke.shape[-1], x.dtype))
            smax = jax.ops.segment_max(score, dst, num_segments=n_nodes)
            a = jnp.exp(score - smax[dst])
            denom = jax.ops.segment_sum(a, dst, num_segments=n_nodes)
            alpha = a / denom[dst]
            msg = alpha[:, None] * (v[src] + e)
            out = jax.ops.segment_sum(msg, dst, num_segments=n_nodes)
            out = out + x @ ws + bs
            return out
        src, dst = (edge_index[0], edge_index[1])
        n = x.shape[0]
        h1 = jax.nn.relu(_transformer_conv(x, src, dst, edge_attr, q1_w, q1_b, k1_w, k1_b, v1_w, v1_b, e1_w, s1_w, s1_b, n))
        h2 = jax.nn.relu(_transformer_conv(h1, src, dst, edge_attr, q2_w, q2_b, k2_w, k2_b, v2_w, v2_b, e2_w, s2_w, s2_b, n))
        skip_xs = jnp.concatenate([h1, h2], axis=-1)
        return jax.nn.relu(skip_xs @ skip_w + skip_b)

    def _L1_gnn_ref(x, edge_index, edge_type, basis, comp, root, bias):
        import jax, jax.numpy as jnp
        import numpy as np
        N_NODES, N_EDGES, C_IN, C_HID, N_REL, N_BASES, N_LAYERS = (6250, 100000, 64, 64, 8, 4, 3)

        def _rgcn_layer(h, src, dst, edge_type, basis_l, comp_l, root_l, bias_l, num_relations):
            n = h.shape[0]
            W = jnp.einsum('rb,bch->rch', comp_l, basis_l)
            seg = edge_type * n + dst
            msg = h[src]
            agg = jax.ops.segment_sum(msg, seg, num_segments=num_relations * n)
            agg = agg.reshape(num_relations, n, -1)
            cnt = jax.ops.segment_sum(jnp.ones(seg.shape, h.dtype), seg, num_segments=num_relations * n)
            cnt = cnt.reshape(num_relations, n, 1)
            agg = agg / jnp.maximum(cnt, 1.0)
            return jnp.einsum('rnc,rch->nh', agg, W) + h @ root_l + bias_l
        num_relations = comp.shape[1]
        num_layers = basis.shape[0]
        src, dst = (edge_index[0], edge_index[1])
        h = x
        for l in range(num_layers):
            h = _rgcn_layer(h, src, dst, edge_type, basis[l], comp[l], root[l], bias[l], num_relations)
            if l < num_layers - 1:
                h = jax.nn.relu(h)
        return h

    def _L2_gnn_ref(node_feats, edge_feats, W1, b1, ln_g, ln_b, W2, b2, eps, edge_index, num_nodes):
        import jax, jax.numpy as jnp
        import numpy as np
        LN_EPS = 1e-05
        message = jax.nn.relu(node_feats[edge_index[1]] + edge_feats)
        message_reduce = jax.ops.segment_sum(message, edge_index[0], num_segments=num_nodes)
        h = (1.0 + eps) * node_feats + message_reduce
        x = h @ W1 + b1
        mu = jnp.mean(x, axis=-1, keepdims=True)
        var = jnp.mean(jnp.square(x - mu), axis=-1, keepdims=True)
        x = (x - mu) * jax.lax.rsqrt(var + LN_EPS) * ln_g + ln_b
        x = jax.nn.relu(x)
        return x @ W2 + b2

    def _L3_gnn_ref(x, edge_index, edge_attr, W_l, b_l, W_r, W_e, b_e):
        import jax, jax.numpy as jnp
        import numpy as np
        N_NODES = 12500
        N_EDGES = 200000
        IN_CH = 64
        OUT_CH = 64
        EDGE_DIM = 16
        N = x.shape[0]
        row, col = (edge_index[0], edge_index[1])
        x_j = x[row]
        agg = jax.ops.segment_sum(x_j, col, num_segments=N)
        cnt = jax.ops.segment_sum(jnp.ones((row.shape[0],), x.dtype), col, num_segments=N)
        mean = agg / jnp.maximum(cnt, 1.0)[:, None]
        out = mean @ W_l + b_l + x @ W_r
        e = edge_attr @ W_e + b_e
        out = out + jnp.zeros_like(out).at[col].set(e)
        return out
    edge_index = jnp.stack([src, dst])
    x = _layernorm(x + _L0_gnn_ref(x, edge_index, edge_attr_32, L0_gnn_q1_w, L0_gnn_q1_b, L0_gnn_k1_w, L0_gnn_k1_b, L0_gnn_v1_w, L0_gnn_v1_b, L0_gnn_e1_w, L0_gnn_s1_w, L0_gnn_s1_b, L0_gnn_q2_w, L0_gnn_q2_b, L0_gnn_k2_w, L0_gnn_k2_b, L0_gnn_v2_w, L0_gnn_v2_b, L0_gnn_e2_w, L0_gnn_s2_w, L0_gnn_s2_b, L0_gnn_skip_w, L0_gnn_skip_b), axis=-1)
    x = _layernorm(x + _L1_gnn_ref(x, edge_index, edge_type_8, L1_gnn_basis, L1_gnn_comp, L1_gnn_root, L1_gnn_bias), axis=-1)
    x = _layernorm(x + _L2_gnn_ref(x, edge_attr_64, L2_gnn_W1, L2_gnn_b1, L2_gnn_ln_g, L2_gnn_ln_b, L2_gnn_W2, L2_gnn_b2, L2_gnn_eps, edge_index, 6250), axis=-1)
    x = _layernorm(x + _L3_gnn_ref(x, edge_index, edge_attr_16, L3_gnn_W_l, L3_gnn_b_l, L3_gnn_W_r, L3_gnn_W_e, L3_gnn_b_e), axis=-1)
    return x

_drawn_inputs = setup_inputs


def setup_inputs(seed=0):
    import zlib

    import numpy as np

    out = dict(_drawn_inputs(seed))
    spreads = {'L0_gnn_q1_b': (0.0, 0.661),
     'L0_gnn_k1_b': (0.0, 2.0),
     'L0_gnn_v1_b': (0.0, 0.1),
     'L0_gnn_s1_b': (0.0, 0.27),
     'L0_gnn_q2_b': (0.0, 0.8),
     'L0_gnn_k2_b': (0.0, 2.0),
     'L0_gnn_v2_b': (0.0, 0.1),
     'L0_gnn_s2_b': (0.0, 0.1),
     'L0_gnn_skip_b': (0.0, 0.1),
     'L1_gnn_bias': (0.0, 0.1),
     'L2_gnn_b1': (0.0, 2.0),
     'L2_gnn_ln_g': (1.0, 0.2),
     'L2_gnn_ln_b': (0.0, 0.1),
     'L2_gnn_b2': (0.0, 0.1),
     'L3_gnn_b_l': (0.0, 0.1)}
    factors = {'L0_gnn_k2_w': 3.049, 'L3_gnn_b_e': 8.0}
    for name, (base, spread) in spreads.items():
        noise = np.random.default_rng([zlib.crc32(name.encode()), seed]).standard_normal(out[name].shape)
        drawn = base * np.exp(spread * noise) if base else spread * noise
        out[name] = jnp.asarray(drawn.astype(out[name].dtype))
    for name, factor in factors.items():
        out[name] = (out[name] * factor).astype(out[name].dtype)
    return out
```

```python
from contextlib import ExitStack, contextmanager

import concourse.bass as bass
from concourse import mybir

F32 = mybir.dt.float32
BF16 = mybir.dt.bfloat16
I32 = mybir.dt.int32
ALU = mybir.AluOpType
ACT = mybir.ActivationFunctionType
AX = mybir.AxisListType

P = 128
D = 64
N = 6250
E = 206250
SLOTS = 16
HALF = SLOTS // 2
TURNS = -(-E // (P * SLOTS))
T = TURNS * SLOTS
ROW = SLOTS * P
NT = 50
NROWS = NT * P
CHUNKS = 16
CW = 404
NCOLS = CHUNKS * CW
RELS = 8
BASES = 4
LAYERS = 3
COPIES = 4
BIG = 3.0e38
EPS = 1e-5
NODE_SLOTS = 5

assert NROWS >= N + 1 + P and NCOLS >= N + P

WIDTHS = [
    ("kv1", 128), ("qq1", 96), ("comb1", 64), ("self1", 64),
    ("kv2", 128), ("qq2", 96), ("comb2", 64), ("self2", 64),
    ("skip_h1", 64), ("skip_h2", 64),
    ("root0", 64), ("root1", 64), ("root2", 64),
    ("w1", 128), ("w2", 64), ("b2", 64), ("ln_g", 128), ("ln_b", 128), ("eps", 1),
    ("w_l", 64), ("w_e", 64), ("w_r", 64),
    ("pick96", 64), ("pick64", 64),
    ("ident", 128), ("iota", 128), ("below", 128), ("lane", 1), ("trash", 1),
    ("q1_t", 65), ("e1_t", 32), ("q2_t", 65), ("e2_t", 32),
]
WCOL = {}
_at = 0
for _name, _w in WIDTHS:
    WCOL[_name] = (_at, _w)
    _at += _w
WTOTAL = _at


class Buffers:

    def __init__(self, nc, ctx):
        def sb(name, shape, dt):
            return ctx.enter_context(nc.sbuf_tensor(name, shape, dt))

        self.node_a = sb("node_a", [P, NCOLS], F32)
        self.node_b = sb("node_b", [P, NCOLS], F32)
        self.query = sb("query", [P, NCOLS], F32)
        self.acc = sb("acc", [P, NCOLS], F32)
        self.x = sb("x", [P, NT * D], F32)
        self.weights = sb("weights", [P, WTOTAL], F32)
        self.rel_w = sb("rel_w", [D, LAYERS * RELS * D], F32)
        self.src_ids = sb("src_ids", [P, T + SLOTS], I32)
        self.rel_ids = sb("rel_ids", [P, T + SLOTS], I32)
        self.dst_off = sb("dst_off", [P, T], F32)
        self.rel_wt = sb("rel_wt", [P, T], F32)
        self.is_last = sb("is_last", [P, T], F32)
        self.score = sb("score", [P, T], F32)
        self.window = sb("window", [1, T], I32)
        self.ring = sb("ring", [P, SLOTS, P], F32)
        self.ids = sb("ids", [P, SLOTS], I32)
        self.edge_t = sb("edge_t", [P, ROW], F32)
        self.hot = sb("hot", [P, 4, P], F32)
        self.bcast_w = sb("bcast_w", [2, P], BF16)
        self.psum = ctx.enter_context(nc.psum_tensor("psum", [P, 8, 512], F32))

    def w(self, name, rows=P):
        a, n = WCOL[name]
        return self.weights[0:rows, a:a + n]

    def ident(self, n=P):
        a = WCOL["ident"][0]
        return self.weights[0:n, a:a + n]


@contextmanager
def stage(nc):
    before = nc.snapshot_sems()
    with ExitStack() as ctx:
        yield ctx
    nc.clear_and_free_semaphores(nc.allocated_since(before))
    nc.all_engine_barrier()


def sems(nc, ctx, *names):
    return [nc.alloc_semaphore(name=f"{n}_{nc.next_id()}") for n in names]


def by_slot(columns):
    return columns.rearrange("p (i u) -> p u i", u=SLOTS)


def load_inputs(nc, b, io):
    with stage(nc) as ctx:
        loaded, chain, folded, kept = sems(nc, ctx, "in_loaded", "in_chain", "in_folded", "in_kept")
        basis = b.acc[0:D, 0:LAYERS * BASES * D].rearrange("c (l b h) -> c l b h", l=LAYERS, b=BASES)
        comp = b.acc[0:D, LAYERS * BASES * D:LAYERS * BASES * D + LAYERS * RELS * BASES]
        block = ctx.enter_context(nc.Block())

        @block.sync
        def _(sp):
            sp.dma_start(b.weights[:, :], io["weights"]).then_inc(loaded, 16)
            sp.dma_start(b.acc[0:D, 0:LAYERS * BASES * D], io["basis"]).then_inc(loaded, 16)
            sp.dma_start(comp, io["comp"]).then_inc(loaded, 16)
            sp.dma_start(b.node_a[0:D + 1, :], io["x_t"]).then_inc(loaded, 16)
            sp.dma_start(b.x[:, :], io["x_rows"]).then_inc(loaded, 16)
            sp.dma_start(b.src_ids[:, :], io["src_lane"]).then_inc(loaded, 16)
            sp.dma_start(b.rel_ids[:, :], io["type_lane"]).then_inc(loaded, 16)
            sp.dma_start(b.window[:, :], io["window"]).then_inc(loaded, 16)
            sp.wait_ge(loaded, 128)

        @block.tensor
        def _(pe):
            pe.wait_ge(loaded, 128)
            for n in (1, 2):
                pe.matmul(b.psum[0:65, n, 0:32], lhsT=b.w(f"q{n}_t", D), rhs=b.w(f"e{n}_t", D),
                          start=True, stop=True).then_inc(folded, 1)

        @block.vector
        def _(dve):
            done = [0]

            def link(ins):
                done[0] += 1
                ins.then_inc(chain, 1)
                dve.wait_ge(chain, done[0])

            dve.wait_ge(loaded, 128)
            for l in range(LAYERS):
                for r in range(RELS):
                    out = b.rel_w[:, (l * RELS + r) * D:(l * RELS + r + 1) * D]
                    for k in range(BASES):
                        at = (l * RELS + r) * BASES + k
                        if k == 0:
                            link(dve.tensor_scalar(out, basis[:, l, k, :], comp[:, at:at + 1], None, ALU.mult))
                        else:
                            link(dve.scalar_tensor_tensor(out=out, in0=basis[:, l, k, :], scalar=comp[:, at:at + 1],
                                                          in1=out, op0=ALU.mult, op1=ALU.add))
            link(dve.scalar_tensor_tensor(out=b.rel_ids[:, :], in0=b.src_ids[:, :], scalar=float(RELS),
                                          in1=b.rel_ids[:, :], op0=ALU.mult, op1=ALU.add))
            dve.memset(b.node_b[64:65, :], 1.0).then_inc(kept, 1)
            dve.memset(b.bcast_w[0:2, :], 1.0).then_inc(kept, 1)
            dve.wait_ge(kept, 2)
            dve.memset(b.bcast_w[0:1, :], float(P)).then_inc(kept, 1)
            dve.wait_ge(folded, 2)
            for n in (1, 2):
                a = WCOL[f"qq{n}"][0] + D
                dve.tensor_copy(b.weights[0:65, a:a + 32], b.psum[0:65, n, 0:32]).then_inc(kept, 1)
            dve.wait_ge(kept, 5)


def turn_view(buffer, n):
    return buffer[0:TURNS, n * ROW:(n + 1) * ROW]


def carry_rows(pe, b, cols, n, carry_ready, carry_turned, k):
    pe.wait_ge(carry_ready, 2 * k + 1)
    for j in range(2):
        ins = pe.transpose(b.psum[0:n, 4 + j, 0:TURNS], cols[0:TURNS, j, 0:n], b.ident(TURNS))
    ins.then_inc(carry_turned, 1)
    pe.wait_ge(carry_ready, 2 * k + 2)
    pe.transpose(b.psum[0:TURNS, 7, 0:n], b.hot[0:n, 2, 0:TURNS], b.ident(n)).then_inc(carry_turned, 1)


def carry_scan(dve, link, b, n, ops, start, backward, into, carry_ready, carry_turned, k):
    lasts, flags, out = b.hot[0:n, 0, 0:TURNS], b.hot[0:n, 1, 0:TURNS], b.hot[0:n, 3, 0:TURNS]
    shifted = b.hot[0:n, 2, 0:TURNS]
    dve.wait_ge(carry_turned, 2 * k + 1)
    link(dve.tensor_copy(lasts, b.psum[0:n, 4, 0:TURNS]))
    link(dve.tensor_copy(flags, b.psum[0:n, 5, 0:TURNS]))
    link(dve.memset(shifted, start))
    if backward:
        link(dve.tensor_tensor_scan(out[:, ::-1], flags[:, ::-1], lasts[:, ::-1], start, *ops))
        link(dve.tensor_copy(shifted[:, 0:TURNS - 1], out[:, 1:TURNS]))
    else:
        link(dve.tensor_tensor_scan(out, flags, lasts, start, *ops))
        link(dve.tensor_copy(shifted[:, 1:TURNS], out[:, 0:TURNS - 1]))
    dve.sem_inc(carry_ready, 1)
    dve.wait_ge(carry_turned, 2 * k + 2)
    link(dve.tensor_copy(into, b.psum[0:TURNS, 7, 0:n]))


def lanes_from_turns(pe, b, source, ready, count, turned):
    pe.wait_ge(ready, count)
    for u in range(SLOTS):
        ins = pe.transpose(b.psum[:, u // 4, (u % 4) * P:(u % 4) * P + TURNS],
                           source[:, u * P:(u + 1) * P], b.ident(TURNS))
    ins.then_inc(turned, 1)


def copy_lanes(dve, link, b, columns):
    for q in range(4):
        link(dve.tensor_copy(by_slot(columns)[:, 4 * q:4 * q + 4, :],
                             b.psum[:, q, :].rearrange("p (u e) -> p u e", e=P)[:, :, 0:TURNS]))


def edge_tables(nc, b, io, rows_dram):
    with stage(nc) as ctx:
        loaded, chain, ready, turned, carry_ready, carry_turned, stored = sems(
            nc, ctx, "et_loaded", "et_chain", "et_ready", "et_turned", "et_carry_ready", "et_carry_turned",
            "et_stored")
        dst_i = b.query[0:TURNS, 0:ROW + 2].bitcast(I32)
        dst = b.query[0:TURNS, ROW + 2:2 * ROW + 4]
        dst_mid = dst[:, 1:ROW + 1]
        onward = turn_view(b.acc, 0)
        back = turn_view(b.acc, 1)
        kind_i = turn_view(b.acc, 2).bitcast(I32)
        kind = b.node_b[0:TURNS, 0:ROW]
        this = b.node_b[0:TURNS, ROW:2 * ROW]
        ahead = b.node_b[0:TURNS, 2 * ROW:3 * ROW]
        behind = b.query[0:TURNS, 2 * ROW + 4:3 * ROW + 4]
        total = b.edge_t[0:TURNS, :]
        src_i = turn_view(b.acc, 2).bitcast(I32)
        part_i = b.node_b[0:TURNS, 0:ROW].bitcast(I32)
        halves = b.ring[0:TURNS, :, :].rearrange("p u e -> p (u e)").bitcast(BF16)
        rows_hi, rows_lo = halves[:, 0:2 * ROW], b.node_b[0:TURNS, ROW:2 * ROW].bitcast(BF16)
        cols = b.score[0:TURNS, 0:2 * RELS * 2].rearrange("p (w j n) -> p w j n", w=2, j=2)
        carried = b.score[0:TURNS, 64:64 + 2 * RELS].rearrange("p (w n) -> p w n", w=2)
        block = ctx.enter_context(nc.Block())

        @block.sync
        def _(sp):
            sp.dma_start(dst_i, io["dst_turn"]).then_inc(loaded, 16)
            sp.dma_start(kind_i, io["type_turn"]).then_inc(loaded, 16)
            sp.wait_ge(ready, 1)
            sp.dma_start(src_i, io["src_turn"]).then_inc(loaded, 16)
            sp.wait_ge(ready, 5)
            sp.dma_start(rows_dram[0].rearrange("(i e) -> i e", i=TURNS), rows_hi).then_inc(stored, 16)
            sp.dma_start(rows_dram[1].rearrange("(i e) -> i e", i=TURNS), rows_lo).then_inc(stored, 16)
            sp.wait_ge(stored, 32)

        @block.tensor
        def _(pe):
            lanes_from_turns(pe, b, this, ready, 1, turned)
            lanes_from_turns(pe, b, ahead, ready, 2, turned)
            carry_rows(pe, b, cols[:, 0], RELS, carry_ready, carry_turned, 0)
            carry_rows(pe, b, cols[:, 1], RELS, carry_ready, carry_turned, 1)
            lanes_from_turns(pe, b, total, ready, 4, turned)

        @block.vector
        def _(dve):
            done = [0]

            def link(ins):
                done[0] += 1
                ins.then_inc(chain, 1)
                dve.wait_ge(chain, done[0])

            dve.wait_ge(loaded, 32)
            link(dve.tensor_copy(dst, dst_i))
            link(dve.tensor_copy(kind, kind_i))
            link(dve.tensor_tensor(onward, dst_mid, dst[:, 0:ROW], ALU.is_equal))
            link(dve.tensor_tensor(back, dst_mid, dst[:, 2:ROW + 2], ALU.is_equal))
            d3 = dst_mid.rearrange("p (u e) -> p u e", e=P)
            link(dve.tensor_tensor(this.rearrange("p (u e) -> p u e", e=P), d3,
                                   d3[:, :, 0:1].broadcast_to([TURNS, SLOTS, P]), ALU.subtract))
            dve.sem_inc(ready, 1)
            link(dve.tensor_scalar(ahead, back, -1.0, 1.0, ALU.mult, ALU.add))
            dve.wait_ge(turned, 1)
            copy_lanes(dve, link, b, b.dst_off)
            dve.sem_inc(ready, 1)
            hi3 = rows_hi.rearrange("p (u w e) -> p u w e", u=SLOTS, w=2)
            dve.wait_ge(turned, 2)
            copy_lanes(dve, link, b, b.is_last)

            scan = (ALU.mult, ALU.add)
            link(dve.tensor_reduce(cols[:, 0, 1, 0:1], onward, AX.X, ALU.min))
            link(dve.tensor_reduce(cols[:, 1, 1, 0:1], back, AX.X, ALU.min))
            for w in range(2):
                link(dve.tensor_copy(cols[:, w, 1, 1:RELS], cols[:, w, 1, 0:1].broadcast_to([TURNS, RELS - 1])))
            for r in range(RELS):
                link(dve.tensor_scalar(this, kind, float(r), None, ALU.is_equal))
                link(dve.tensor_tensor_scan(ahead, onward, this, 0.0, *scan))
                link(dve.tensor_tensor_scan(behind[:, ::-1], back[:, ::-1], this[:, ::-1], 0.0, *scan))
                link(dve.tensor_copy(cols[:, 0, 0, r:r + 1], ahead[:, ROW - 1:ROW]))
                link(dve.tensor_copy(cols[:, 1, 0, r:r + 1], behind[:, 0:1]))
            dve.sem_inc(carry_ready, 1)
            carry_scan(dve, link, b, RELS, scan, 0.0, False, carried[:, 0, :], carry_ready, carry_turned, 0)
            dve.sem_inc(carry_ready, 1)
            carry_scan(dve, link, b, RELS, scan, 0.0, True, carried[:, 1, :], carry_ready, carry_turned, 1)
            link(dve.memset(total, 0.0))
            for r in range(RELS):
                link(dve.tensor_scalar(this, kind, float(r), None, ALU.is_equal))
                link(dve.tensor_tensor_scan(ahead, onward, this, carried[:, 0, r:r + 1], *scan))
                link(dve.tensor_tensor_scan(behind[:, ::-1], back[:, ::-1], this[:, ::-1],
                                            carried[:, 1, r:r + 1], *scan))
                link(dve.tensor_tensor(ahead, ahead, behind, ALU.add))
                link(dve.scalar_tensor_tensor(out=ahead, in0=ahead, scalar=-1.0, in1=this,
                                              op0=ALU.add, op1=ALU.mult))
                link(dve.tensor_tensor(total, total, ahead, ALU.add))
            link(dve.reciprocal(total, total))
            dve.sem_inc(ready, 2)
            dve.wait_ge(turned, 3)
            copy_lanes(dve, link, b, b.rel_wt)

            dve.wait_ge(loaded, 48)
            link(dve.memset(rows_hi, 0.0))
            link(dve.tensor_scalar(part_i, src_i, 7, None, ALU.logical_shift_right))
            link(dve.tensor_copy(hi3[:, :, 0, :], part_i.rearrange("p (u e) -> p u e", e=P)))
            link(dve.tensor_scalar(part_i, src_i, P - 1, None, ALU.bitwise_and))
            lo3 = rows_lo.rearrange("p (u w e) -> p u w e", u=SLOTS, w=2)
            link(dve.tensor_copy(lo3[:, :, 0, :], part_i.rearrange("p (u e) -> p u e", e=P)))
            link(dve.tensor_tensor(lo3[:, :, 1, :], d3,
                                   d3[:, :, 0:1].broadcast_to([TURNS, SLOTS, P]), ALU.subtract))
            dve.sem_inc(ready, 1)
            dve.wait_ge(stored, 32)
            link(dve.memset(b.node_b[64:65, :], 1.0))


def node_rows(nc, b, source, weights, ncols, rows, table):
    with stage(nc) as ctx:
        staged, made, copied, gate = sems(nc, ctx, "nr_staged", "nr_made", "nr_copied", "nr_gate")
        stored = sems(nc, ctx, *[f"nr_stored{u}" for u in range(NODE_SLOTS)])
        out = b.query[:, 0:NODE_SLOTS * ncols].rearrange("p (u n) -> p u n", u=NODE_SLOTS)
        table_rows = table.rearrange("(t p) n -> t p n", p=P)
        turns = NT // NODE_SLOTS
        block = ctx.enter_context(nc.Block())

        @block.scalar
        def _(act):
            with act.Fori(0, turns) as i:
                for u in range(NODE_SLOTS):
                    n = i * NODE_SLOTS + u
                    act.wait_ge(made, n + 1)
                    act.sem_inc(gate, 1)
                    act.copy(b.edge_t[0:rows, u * P:(u + 1) * P],
                             source[0:rows, bass.ds(n * P, P)]).then_inc(staged, 1)

        @block.tensor
        def _(pe):
            pe.sem_inc(made, NODE_SLOTS)
            with pe.Fori(0, turns) as i:
                for u in range(NODE_SLOTS):
                    n = i * NODE_SLOTS + u
                    pe.wait_ge(staged, n + 1)
                    pe.wait_ge(copied, n + 1)
                    pe.matmul(b.psum[:, u, 0:ncols], lhsT=b.edge_t[0:rows, u * P:(u + 1) * P],
                              rhs=weights, start=True, stop=True).then_inc(made, 1)

        @block.vector
        def _(dve):
            dve.sem_inc(copied, NODE_SLOTS)
            with dve.Fori(0, turns) as i:
                for u in range(NODE_SLOTS):
                    n = i * NODE_SLOTS + u
                    dve.wait_ge(made, NODE_SLOTS + n + 1)
                    dve.wait_ge(stored[u], 16 * i + 16)
                    dve.tensor_copy(out[:, u, :], b.psum[:, u, 0:ncols]).then_inc(copied, 1)

        @block.sync
        def _(sp):
            for u in range(NODE_SLOTS):
                sp.sem_inc(stored[u], 16)
            with sp.Fori(0, turns) as i:
                for u in range(NODE_SLOTS):
                    n = i * NODE_SLOTS + u
                    sp.wait_ge(copied, NODE_SLOTS + n + 1)
                    sp.dma_start(table_rows[bass.ds(n, 1), :, :].rearrange("o p n -> (o p) n"),
                                 out[:, u, :]).then_inc(stored[u], 16)
            for u in range(NODE_SLOTS):
                sp.wait_ge(stored[u], 16 * turns + 16)


def node_query(nc, b, source, weights):
    with stage(nc) as ctx:
        made, copied, gate = sems(nc, ctx, "nq_made", "nq_copied", "nq_gate")
        block = ctx.enter_context(nc.Block())

        @block.tensor
        def _(pe):
            with pe.Fori(0, CHUNKS // 2) as i:
                for u in range(2):
                    pe.wait_ge(copied, 2 * i + u + 1)
                    pe.sem_inc(gate, 1)
                    pe.matmul(b.psum[0:96, u, 0:CW], lhsT=weights,
                              rhs=source[0:D + 1, bass.ds((2 * i + u) * CW, CW)],
                              start=True, stop=True).then_inc(made, 1)

        @block.scalar
        def _(act):
            act.sem_inc(copied, 2)
            with act.Fori(0, CHUNKS // 2) as i:
                for u in range(2):
                    act.wait_ge(made, 2 * i + u + 1)
                    act.sem_inc(gate, 1)
                    act.copy(b.query[0:96, bass.ds((2 * i + u) * CW, CW)],
                             b.psum[0:96, u, 0:CW]).then_inc(copied, 1)


def edge_scores(nc, b, io, table, values):
    with stage(nc) as ctx:
        ids, turned, keyed, scored, picked, gate, offs, cleared = sems(
            nc, ctx, "sc_ids", "sc_turned", "sc_keyed", "sc_scored", "sc_picked", "sc_gate", "sc_offs",
            "sc_cleared")
        got = sems(nc, ctx, *[f"sc_got{u}" for u in range(SLOTS)])
        spilled = sems(nc, ctx, "sc_spilled0", "sc_spilled1")
        feats = sems(nc, ctx, "sc_feats0", "sc_feats1")
        off16 = b.hot[:, 0, 0:2 * SLOTS].rearrange("p (a u) -> p a u", a=2)
        junk = b.hot[:, 1:3, :]
        score16 = b.hot[:, 3, 0:SLOTS]
        block = ctx.enter_context(nc.Block())

        @block.gpsimd
        def _(pool):
            with pool.Fori(0, TURNS) as i:
                for u in range(SLOTS):
                    h = u // HALF
                    if u % HALF == 0:
                        pool.wait_ge(ids, 2 * i + h + 1)
                        pool.wait_ge(spilled[h], 16 * i + 16)
                    pool.wait_ge(turned, i * SLOTS + u + 1)
                    pool.sem_inc(gate, 1)
                    pool.indirect_dma_start(
                        out=b.ring[:, u, :], out_offset=None, in_=table,
                        in_offset=bass.IndirectOffsetOnAxis(ap=b.ids[:, u:u + 1], axis=0)).then_inc(got[u], 16)

        @block.sync
        def _(sp):
            for h in range(2):
                sp.sem_inc(spilled[h], 16)
            with sp.Fori(0, TURNS) as i:
                for h in range(2):
                    sp.wait_ge(scored, i * SLOTS + (h + 1) * HALF)
                    sp.dma_start(b.edge_t[D:D + 32, h * HALF * P:(h + 1) * HALF * P],
                                 io["ea32_t"][:, bass.ds(i * ROW + h * HALF * P, HALF * P)]).then_inc(feats[h], 16)
                for h in range(2):
                    for u in range(h * HALF, (h + 1) * HALF):
                        sp.wait_ge(got[u], 16 * i + 16)
                    sp.dma_start(values[:, bass.ds(i * SLOTS + h * HALF, HALF), :],
                                 b.ring[:, h * HALF:(h + 1) * HALF, D:2 * D]).then_inc(spilled[h], 16)
            for h in range(2):
                sp.wait_ge(spilled[h], 16 * TURNS + 16)

        def turn_key(pe, i, u):
            pe.wait_ge(got[u], 16 * i + 16)
            pe.wait_ge(keyed, i * SLOTS + u + 1)
            pe.sem_inc(gate, 1)
            pe.transpose(b.psum[0:D, u % 2, 0:P], b.ring[:, u, 0:D], b.ident()).then_inc(turned, 1)

        def score(pe, i, u, start):
            pe.wait_ge(keyed, 2 + i * SLOTS + u + 1)
            if u % HALF == 0:
                pe.wait_ge(feats[u // HALF], 16 * i + 16)
            pe.wait_ge(picked, i * SLOTS + u + 1)
            pe.sem_inc(gate, 1)
            pe.matmul(b.psum[:, 2 + u % 2, 0:P], lhsT=b.edge_t[0:96, u * P:(u + 1) * P],
                      rhs=b.query[0:96, bass.ds(start, P)], start=True, stop=True).then_inc(scored, 1)

        def pe_turn(pe, i, last):
            for h in range(2):
                starts = [pe.value_load(b.window[0:1, bass.ds(i * SLOTS + h * HALF + v, 1)],
                                        min_val=0, max_val=N) for v in range(HALF)]
                for v in range(HALF):
                    u = h * HALF + v
                    score(pe, i, u, starts[v])
                    if u + 2 < SLOTS:
                        turn_key(pe, i, u + 2)
                    elif not last:
                        turn_key(pe, i + 1, u + 2 - SLOTS)

        @block.tensor
        def _(pe):
            pe.sem_inc(turned, SLOTS)
            pe.sem_inc(scored, SLOTS)
            turn_key(pe, 0, 0)
            turn_key(pe, 0, 1)
            with pe.Fori(0, TURNS - 1) as i:
                pe_turn(pe, i, False)
            pe_turn(pe, TURNS - 1, True)

        @block.scalar
        def _(act):
            act.sem_inc(keyed, 2)
            with act.Fori(0, TURNS) as i:
                for u in range(SLOTS):
                    act.wait_ge(turned, SLOTS + i * SLOTS + u + 1)
                    act.wait_ge(scored, i * SLOTS + u + 1)
                    act.copy(b.edge_t[0:D, u * P:(u + 1) * P], b.psum[0:D, u % 2, 0:P]).then_inc(keyed, 1)

        @block.vector
        def _(dve):
            dve.sem_inc(picked, 2)
            for h in range(2):
                dve.tensor_copy(b.ids[:, h * HALF:(h + 1) * HALF],
                                b.src_ids[:, h * HALF:(h + 1) * HALF]).then_inc(ids, 1)
            with dve.Fori(0, TURNS) as i:
                dve.tensor_copy(off16[:, 0, :], b.dst_off[:, bass.ds(i * SLOTS, SLOTS)]).then_inc(offs, 1)
                dve.wait_ge(offs, i + 1)
                for u in range(SLOTS):
                    dve.wait_ge(scored, SLOTS + i * SLOTS + u + 1)
                    dve.scalar_tensor_tensor(
                        out=junk[:, u % 2, :], in0=b.w("iota"), scalar=off16[:, 0, u:u + 1],
                        in1=b.psum[:, 2 + u % 2, 0:P], op0=ALU.is_equal, op1=ALU.mult,
                        accum_out=score16[:, u:u + 1]).then_inc(picked, 1)
                    if u % HALF == HALF - 1:
                        h = u // HALF
                        dve.tensor_copy(b.ids[:, h * HALF:(h + 1) * HALF],
                                        b.src_ids[:, bass.ds((i + 1) * SLOTS + h * HALF, HALF)]).then_inc(ids, 1)
                dve.wait_ge(picked, 2 + (i + 1) * SLOTS)
                dve.tensor_copy(b.score[:, bass.ds(i * SLOTS, SLOTS)], score16).then_inc(cleared, 1)
                dve.wait_ge(cleared, i + 1)


def softmax_parts(nc, b, io):
    with stage(nc) as ctx:
        loaded, chain, turned, ready, carry_ready, carry_turned, shifted, raised = sems(
            nc, ctx, "sm_loaded", "sm_chain", "sm_turned", "sm_ready", "sm_carry_ready", "sm_carry_turned",
            "sm_shifted", "sm_raised")
        dst = b.query[0:TURNS, 0:ROW + 2].bitcast(I32)
        by_turn = b.query[0:TURNS, ROW + 2:2 * ROW + 2]
        ahead = b.query[0:TURNS, 2 * ROW + 2:3 * ROW + 2]
        onward, back, behind = (turn_view(b.acc, k) for k in range(3))
        cols = b.ring[0:TURNS, 0, 0:4].rearrange("p (w j n) -> p w j n", w=2, j=2)
        carried = b.ring[0:TURNS, 1, 0:2]
        block = ctx.enter_context(nc.Block())

        @block.sync
        def _(sp):
            sp.dma_start(dst, io["dst_turn"]).then_inc(loaded, 16)

        @block.tensor
        def _(pe):
            for u in range(SLOTS):
                ins = pe.transpose(b.psum[0:TURNS, u // 4, (u % 4) * P:(u % 4 + 1) * P],
                                   by_slot(b.score)[:, u, :], b.ident())
            ins.then_inc(turned, 1)
            carry_rows(pe, b, cols[:, 0], 1, carry_ready, carry_turned, 0)
            carry_rows(pe, b, cols[:, 1], 1, carry_ready, carry_turned, 1)
            lanes_from_turns(pe, b, by_turn, raised, 1, turned)

        @block.scalar
        def _(act):
            act.wait_ge(shifted, 1)
            act.activation(by_turn, by_turn, ACT.Exp, scale=float(D) ** -0.5).then_inc(raised, 1)

        @block.vector
        def _(dve):
            done = [0]

            def link(ins):
                done[0] += 1
                ins.then_inc(chain, 1)
                dve.wait_ge(chain, done[0])

            dve.wait_ge(loaded, 16)
            for flag, lo in ((onward, 0), (back, 2)):
                link(dve.tensor_tensor(flag, dst[:, 1:ROW + 1], dst[:, lo:lo + ROW], ALU.is_equal))
                link(dve.tensor_scalar(flag, flag, 2 * BIG / 2, None, ALU.mult))
                link(dve.tensor_scalar(flag, flag, -BIG / 2, 2.0, ALU.add, ALU.mult))
            dve.wait_ge(turned, 1)
            for q in range(4):
                link(dve.tensor_copy(by_turn[:, q * 512:(q + 1) * 512], b.psum[0:TURNS, q, :]))
            scan = (ALU.min, ALU.max)
            link(dve.tensor_reduce(cols[:, 0, 1, :], onward, AX.X, ALU.min))
            link(dve.tensor_reduce(cols[:, 1, 1, :], back, AX.X, ALU.min))
            link(dve.tensor_tensor_scan(ahead, onward, by_turn, -BIG, *scan))
            link(dve.tensor_tensor_scan(behind[:, ::-1], back[:, ::-1], by_turn[:, ::-1], -BIG, *scan))
            link(dve.tensor_copy(cols[:, 0, 0, :], ahead[:, ROW - 1:ROW]))
            link(dve.tensor_copy(cols[:, 1, 0, :], behind[:, 0:1]))
            dve.sem_inc(carry_ready, 1)
            carry_scan(dve, link, b, 1, scan, -BIG, False, carried[:, 0:1], carry_ready, carry_turned, 0)
            dve.sem_inc(carry_ready, 1)
            carry_scan(dve, link, b, 1, scan, -BIG, True, carried[:, 1:2], carry_ready, carry_turned, 1)
            link(dve.tensor_tensor_scan(ahead, onward, by_turn, carried[:, 0:1], *scan))
            link(dve.tensor_tensor_scan(behind[:, ::-1], back[:, ::-1], by_turn[:, ::-1], carried[:, 1:2], *scan))
            link(dve.tensor_tensor(ahead, ahead, behind, ALU.max))
            dve.tensor_tensor(by_turn, by_turn, ahead, ALU.subtract).then_inc(shifted, 1)
            dve.wait_ge(turned, 2)
            copy_lanes(dve, link, b, b.score)


ATTEND, RELATE, AVERAGE = range(3)
SUM_ROWS = {ATTEND: 97, RELATE: 64, AVERAGE: 82}


def sum_edges(nc, b, io, what, source):
    rows = SUM_ROWS[what]
    weight = {ATTEND: b.score, RELATE: b.rel_wt, AVERAGE: None}[what]
    index = {ATTEND: None, RELATE: b.rel_ids, AVERAGE: b.src_ids}[what]
    with stage(nc) as ctx:
        ids, hot, summed, added, gate, offs, cleared, extra = sems(
            nc, ctx, "su_ids", "su_hot", "su_summed", "su_added", "su_gate", "su_offs", "su_cleared", "su_extra")
        got = sems(nc, ctx, *[f"su_got{u}" for u in range(SLOTS)]) if index is not None else None
        rows_in = sems(nc, ctx, "su_rows0", "su_rows1")
        off16 = b.edge_t[:, 0:2 * SLOTS].rearrange("p (a u) -> p a u", a=2)
        wt16 = b.edge_t[:, 2 * SLOTS:4 * SLOTS].rearrange("p (a u) -> p a u", a=2)
        feats16 = b.edge_t[:, 4 * SLOTS:20 * SLOTS].rearrange("p (u f) -> p u f", u=SLOTS)
        block = ctx.enter_context(nc.Block())

        if index is not None:
            @block.gpsimd
            def _(pool):
                with pool.Fori(0, TURNS) as i:
                    for u in range(SLOTS):
                        if u % HALF == 0:
                            pool.wait_ge(ids, 2 * i + u // HALF + 1)
                        pool.wait_ge(summed, i * SLOTS + u + 1)
                        pool.sem_inc(gate, 1)
                        pool.indirect_dma_start(
                            out=b.ring[:, u, 0:D], out_offset=None, in_=source,
                            in_offset=bass.IndirectOffsetOnAxis(ap=b.ids[:, u:u + 1], axis=0)).then_inc(got[u], 16)

        if what != RELATE:
            @block.sync
            def _(sp):
                with sp.Fori(0, TURNS) as i:
                    for h in range(2):
                        half = slice(h * HALF, (h + 1) * HALF)
                        if what == ATTEND:
                            sp.wait_ge(summed, i * SLOTS + (h + 1) * HALF)
                            sp.dma_start(b.ring[:, half, 0:D],
                                         source[:, bass.ds(i * SLOTS + h * HALF, HALF), :]).then_inc(rows_in[h], 16)
                            sp.dma_start(b.ring[:, half, D:D + 32],
                                         io["ea32"][:, bass.ds(i * SLOTS + h * HALF, HALF), :]).then_inc(
                                             rows_in[h], 16)
                        else:
                            sp.wait_ge(extra, 2 * (2 * i + h) + 2)
                            sp.dma_start(feats16[:, half, :],
                                         io["ea16"][:, bass.ds(i * SLOTS + h * HALF, HALF), :]).then_inc(
                                             rows_in[h], 16)

        @block.tensor
        def _(pe):
            pe.sem_inc(summed, SLOTS)
            with pe.Fori(0, TURNS) as i:
                for u in range(SLOTS):
                    if index is not None:
                        pe.wait_ge(got[u], 16 * i + 16)
                    if what == ATTEND and u % HALF == 0:
                        pe.wait_ge(rows_in[u // HALF], 32 * i + 32)
                    if what == AVERAGE and u % HALF == 0:
                        pe.wait_ge(extra, 4 + 2 * (2 * i + u // HALF) + 2)
                    pe.wait_ge(hot, i * SLOTS + u + 1)
                    pe.wait_ge(added, i * SLOTS + u + 1)
                    pe.matmul(b.psum[0:rows, u % 4, 0:P], lhsT=b.ring[:, u, 0:rows], rhs=b.hot[:, u % 4, :],
                              start=True, stop=True).then_inc(summed, 1)

        def make_hot(dve, i, u, a):
            dve.wait_ge(summed, SLOTS - 4 + i * SLOTS + u + 1)
            if weight is None:
                ins = dve.tensor_scalar(b.hot[:, u % 4, :], b.w("iota"), off16[:, a, u:u + 1], None, ALU.is_equal)
            else:
                ins = dve.tensor_scalar(b.hot[:, u % 4, :], b.w("iota"), off16[:, a, u:u + 1],
                                        wt16[:, a, u:u + 1], ALU.is_equal, ALU.mult)
            ins.then_inc(hot, 1)

        def fetch(dve, i, count):
            dve.tensor_copy(off16[:, 0, :], b.dst_off[:, bass.ds(i * SLOTS, SLOTS)]).then_inc(offs, 1)
            if weight is not None:
                dve.tensor_copy(wt16[:, 0, :], weight[:, bass.ds(i * SLOTS, SLOTS)]).then_inc(offs, 1)
            else:
                dve.sem_inc(offs, 1)
            dve.wait_ge(offs, 2 * i + 2)

        def mark_last(dve, i, h):
            half = slice(h * HALF, (h + 1) * HALF)
            dve.wait_ge(rows_in[h], 16 * i + 16)
            dve.wait_ge(summed, i * SLOTS + (h + 1) * HALF)
            flag = b.is_last[:, bass.ds(i * SLOTS + h * HALF, HALF)].rearrange("p (u o) -> p u o", o=1)
            dve.tensor_tensor(b.ring[:, half, 65:81], feats16[:, half, :],
                              flag.broadcast_to([P, HALF, 16]), ALU.mult).then_inc(extra, 1)
            dve.tensor_copy(b.ring[:, half, 81:82], flag).then_inc(extra, 1)

        @block.vector
        def _(dve):
            dve.sem_inc(added, 4)
            if what == AVERAGE:
                dve.sem_inc(extra, 4)
            dve.memset(b.acc[0:rows, :], 0.0).then_inc(cleared, 1)
            if what != RELATE:
                one = D if what == AVERAGE else 96
                dve.memset(b.ring[:, :, one:one + 1], 1.0).then_inc(cleared, 1)
                dve.wait_ge(cleared, 2)
            else:
                dve.wait_ge(cleared, 1)
            if index is not None:
                for h in range(2):
                    dve.tensor_copy(b.ids[:, h * HALF:(h + 1) * HALF],
                                    index[:, h * HALF:(h + 1) * HALF]).then_inc(ids, 1)
            with dve.Fori(0, TURNS) as i:
                fetch(dve, i, 0)
                for h in range(2):
                    if what == AVERAGE:
                        mark_last(dve, i, h)
                    starts = [dve.value_load(b.window[0:1, bass.ds(i * SLOTS + h * HALF + v, 1)],
                                             min_val=0, max_val=N) for v in range(HALF)]
                    if h == 0:
                        make_hot(dve, i, 0, 0)
                        make_hot(dve, i, 1, 0)
                    for v in range(HALF):
                        u = h * HALF + v
                        if u + 2 < SLOTS:
                            make_hot(dve, i, u + 2, 0)
                        dve.wait_ge(summed, SLOTS + i * SLOTS + u + 1)
                        dve.wait_ge(added, 4 + i * SLOTS + u)
                        place = b.acc[0:rows, bass.ds(starts[v], P)]
                        dve.tensor_tensor(place, place, b.psum[0:rows, u % 4, 0:P], ALU.add).then_inc(added, 1)
                    if index is not None:
                        dve.tensor_copy(b.ids[:, h * HALF:(h + 1) * HALF],
                                        index[:, bass.ds((i + 1) * SLOTS + h * HALF, HALF)]).then_inc(ids, 1)


def divide_sums(nc, b, top, under, least, beside, relu, source, target):
    rows = top.shape[0]
    with stage(nc) as ctx:
        made, read, gate, step = sems(nc, ctx, "ds_made", "ds_read", "ds_gate", "ds_step")
        t = b.edge_t[0:D, 0:2 * CW].rearrange("p (u n) -> p u n", u=2)
        block = ctx.enter_context(nc.Block())

        @block.tensor
        def _(pe):
            with pe.Fori(0, CHUNKS // 2) as i:
                for u in range(2):
                    at = bass.ds((2 * i + u) * CW, CW)
                    pe.wait_ge(read, 2 * i + u + 1)
                    pe.sem_inc(gate, 1)
                    pe.matmul(b.psum[0:D, 4 * u, 0:CW], lhsT=top, rhs=b.acc[0:rows, at], start=True, stop=True)
                    pe.matmul(b.psum[0:D, 4 * u + 1, 0:CW], lhsT=under, rhs=b.acc[0:rows, at],
                              start=True, stop=True)
                    for k, (w, array, r) in enumerate(beside):
                        ins = pe.matmul(b.psum[0:D, 4 * u + 2, 0:CW], lhsT=w, rhs=array[0:r, at],
                                        start=(k == 0), stop=(k == len(beside) - 1))
                    ins.then_inc(made, 1)

        @block.vector
        def _(dve):
            dve.sem_inc(read, 2)
            with dve.Fori(0, CHUNKS // 2) as i:
                for u in range(2):
                    n = 2 * i + u
                    dve.wait_ge(made, n + 1)
                    dve.tensor_scalar(t[:, u, :], b.psum[0:D, 4 * u + 1, 0:CW], least, None,
                                      ALU.max).then_inc(step, 1)
                    dve.wait_ge(step, 4 * n + 1)
                    dve.reciprocal(t[:, u, :], t[:, u, :]).then_inc(step, 1)
                    dve.wait_ge(step, 4 * n + 2)
                    dve.tensor_tensor(t[:, u, :], b.psum[0:D, 4 * u, 0:CW], t[:, u, :], ALU.mult).then_inc(step, 1)
                    dve.wait_ge(step, 4 * n + 3)
                    dve.tensor_tensor(t[:, u, :], t[:, u, :], b.psum[0:D, 4 * u + 2, 0:CW],
                                      ALU.add).then_inc(step, 1)
                    dve.wait_ge(step, 4 * n + 4)
                    dve.tensor_scalar(target[0:D, bass.ds(n * CW, CW)], t[:, u, :], 0.0 if relu else -BIG, None,
                                      ALU.max).then_inc(read, 1)


def add_root(nc, b, root, features):
    with stage(nc) as ctx:
        made, read, gate, step = sems(nc, ctx, "ar_made", "ar_read", "ar_gate", "ar_step")
        t = b.edge_t[0:D, 0:2 * CW].rearrange("p (u n) -> p u n", u=2)
        block = ctx.enter_context(nc.Block())

        @block.tensor
        def _(pe):
            with pe.Fori(0, CHUNKS // 2) as i:
                for u in range(2):
                    pe.wait_ge(read, 2 * i + u + 1)
                    pe.sem_inc(gate, 1)
                    pe.matmul(b.psum[0:D, u, 0:CW], lhsT=root, rhs=features[0:D + 1, bass.ds((2 * i + u) * CW, CW)],
                              start=True, stop=True).then_inc(made, 1)

        @block.vector
        def _(dve):
            dve.sem_inc(read, 2)
            with dve.Fori(0, CHUNKS // 2) as i:
                for u in range(2):
                    n = 2 * i + u
                    dve.wait_ge(made, n + 1)
                    dve.tensor_tensor(t[:, u, :], b.acc[0:D, bass.ds(n * CW, CW)], b.psum[0:D, u, 0:CW],
                                      ALU.add).then_inc(step, 1)
                    dve.wait_ge(step, n + 1)
                    dve.tensor_scalar(features[0:D, bass.ds(n * CW, CW)], t[:, u, :], 0.0, None,
                                      ALU.max).then_inc(read, 1)


def add_rows(nc, b, parts, relu):
    with stage(nc) as ctx:
        staged, made, added, gate = sems(nc, ctx, "ad_staged", "ad_made", "ad_added", "ad_gate")
        held = b.edge_t[:, 0:2 * NODE_SLOTS * P].rearrange("p (k u n) -> p k u n", k=2, u=NODE_SLOTS)
        turns = NT // NODE_SLOTS
        m = len(parts)
        block = ctx.enter_context(nc.Block())

        @block.scalar
        def _(act):
            with act.Fori(0, turns) as i:
                for u in range(NODE_SLOTS):
                    n = i * NODE_SLOTS + u
                    act.wait_ge(made, n + 1)
                    act.sem_inc(gate, 1)
                    for k, (array, rows, _) in enumerate(parts):
                        act.copy(held[0:rows, k, u, :], array[0:rows, bass.ds(n * P, P)]).then_inc(staged, 1)

        @block.tensor
        def _(pe):
            pe.sem_inc(made, NODE_SLOTS)
            with pe.Fori(0, turns) as i:
                for u in range(NODE_SLOTS):
                    n = i * NODE_SLOTS + u
                    pe.wait_ge(staged, m * n + m)
                    pe.wait_ge(added, n + 1)
                    for k, (_, rows, w) in enumerate(parts):
                        ins = pe.matmul(b.psum[:, u, 0:D], lhsT=held[0:rows, k, u, :], rhs=w,
                                        start=(k == 0), stop=(k == m - 1))
                    ins.then_inc(made, 1)

        @block.vector
        def _(dve):
            dve.sem_inc(added, NODE_SLOTS)
            with dve.Fori(0, turns) as i:
                for u in range(NODE_SLOTS):
                    n = i * NODE_SLOTS + u
                    dve.wait_ge(made, NODE_SLOTS + n + 1)
                    xt = b.x[:, bass.ds(n * D, D)]
                    dve.scalar_tensor_tensor(out=xt, in0=b.psum[:, u, 0:D], scalar=0.0 if relu else -BIG,
                                             in1=xt, op0=ALU.max, op1=ALU.add).then_inc(added, 1)


def normalize(dve, link, b, rows, width, spare, stats, act_wait):
    mean, var = stats[:, 0:NT], stats[:, NT:2 * NT]

    def wide(column):
        return column.rearrange("p (t o) -> p t o", o=1).broadcast_to([P, NT, width])

    link(dve.tensor_reduce(mean, rows, AX.X, ALU.add))
    link(dve.tensor_scalar(mean, mean, 1.0 / width, None, ALU.mult))
    link(dve.tensor_tensor(rows, rows, wide(mean), ALU.subtract))
    link(dve.tensor_tensor(spare, rows, rows, ALU.mult))
    link(dve.tensor_reduce(var, spare, AX.X, ALU.add))
    link(dve.tensor_scalar(var, var, 1.0 / width, EPS, ALU.mult, ALU.add))
    act_wait(var)
    link(dve.reciprocal(var, var))
    link(dve.tensor_tensor(rows, rows, wide(var), ALU.mult))


def turn_nodes(nc, b, rows, width, turned_to, ones):
    with stage(nc) as ctx:
        staged, made, copied, gate = sems(nc, ctx, "tn_staged", "tn_made", "tn_copied", "tn_gate")
        held = b.edge_t[:, 0:NODE_SLOTS * P].rearrange("p (u n) -> p u n", u=NODE_SLOTS)
        turns = NT // NODE_SLOTS
        block = ctx.enter_context(nc.Block())

        @block.scalar
        def _(act):
            with act.Fori(0, turns) as i:
                for u in range(NODE_SLOTS):
                    n = i * NODE_SLOTS + u
                    act.wait_ge(made, n + 1)
                    act.sem_inc(gate, 1)
                    act.copy(held[:, u, 0:width], rows[:, bass.ds(n * width, width)]).then_inc(staged, 1)

        @block.tensor
        def _(pe):
            pe.sem_inc(made, NODE_SLOTS)
            with pe.Fori(0, turns) as i:
                for u in range(NODE_SLOTS):
                    n = i * NODE_SLOTS + u
                    pe.wait_ge(staged, n + 1)
                    pe.wait_ge(copied, n + 1)
                    pe.sem_inc(gate, 1)
                    pe.transpose(b.psum[0:width, u, 0:P], held[:, u, 0:width], b.ident()).then_inc(made, 1)

        @block.vector
        def _(dve):
            dve.sem_inc(copied, NODE_SLOTS)
            with dve.Fori(0, turns) as i:
                for u in range(NODE_SLOTS):
                    n = i * NODE_SLOTS + u
                    dve.wait_ge(made, NODE_SLOTS + n + 1)
                    dve.sem_inc(gate, 1)
                    dve.tensor_copy(turned_to[0:width, bass.ds(n * P, P)],
                                    b.psum[0:width, u, 0:P]).then_inc(copied, 1)


def norm_x(nc, b, out):
    with stage(nc) as ctx:
        chain, asked, rooted, stored = sems(nc, ctx, "nx_chain", "nx_asked", "nx_rooted", "nx_stored")
        x = b.x[:, :].rearrange("p (t d) -> p t d", d=D)
        spare = b.acc[:, 0:NT * D].rearrange("p (t d) -> p t d", d=D)
        stats = b.hot[:, 0, :]
        var = stats[:, NT:2 * NT]
        full = out.shape[0] // P
        block = ctx.enter_context(nc.Block())

        @block.vector
        def _(dve):
            done = [0]

            def link(ins):
                done[0] += 1
                ins.then_inc(chain, 1)
                dve.wait_ge(chain, done[0])

            def act_wait(_):
                dve.sem_inc(asked, 1)
                dve.wait_ge(rooted, 1)

            normalize(dve, link, b, x, D, spare, stats, act_wait)
            dve.sem_inc(asked, 1)

        @block.scalar
        def _(act):
            act.wait_ge(asked, 1)
            act.sqrt(var, var).then_inc(rooted, 1)

        @block.sync
        def _(sp):
            sp.wait_ge(asked, 2)
            sp.dma_start(out[0:full * P, :].rearrange("(t p) d -> p t d", p=P), x[:, 0:full, :]).then_inc(stored, 16)
            rest = out.shape[0] - full * P
            if rest:
                sp.dma_start(out[full * P:, :], x[0:rest, full, :]).then_inc(stored, 16)
            sp.wait_ge(stored, 32 if rest else 16)


def scatter_messages(nc, b, io, table, rows_dram, partial):
    with stage(nc) as ctx:
        broadcast, spread, equal, moved, joined, ordered, offs, chain = sems(
            nc, ctx, "me_broadcast", "me_spread", "me_equal", "me_moved", "me_joined", "me_ordered",
            "me_offs", "me_chain")
        message, relued, copied, zeroed, cleared, freed = sems(
            nc, ctx, "me_message", "me_relued", "me_copied", "me_zeroed", "me_cleared", "me_freed")
        key_rows = sems(nc, ctx, "me_key_rows0", "me_key_rows1")
        feats = sems(nc, ctx, "me_feats0", "me_feats1")
        windows = sems(nc, ctx, "me_windows0", "me_windows1")
        sent = sems(nc, ctx, *[f"me_sent{k}" for k in range(COPIES)])
        big = b.query
        o = [0]

        def take(n):
            o[0] += n
            return big[:, o[0] - n:o[0]]

        win = take(SLOTS * D).rearrange("p (u d) -> p u d", u=SLOTS)
        feat = take(SLOTS * D).rearrange("p (u d) -> p u d", u=SLOTS)
        keys = take(ROW)[0:2, :].bitcast(BF16).rearrange("p (u w) -> p u w", u=SLOTS)
        out_hot = take(2 * P).rearrange("p (u n) -> p u n", u=2)
        same = take(4 * P).rearrange("p (u n) -> p u n", u=4)
        msg = take(4 * D).rearrange("p (u d) -> p u d", u=4)
        total = take(HALF * D).rearrange("p (u d) -> p u d", u=HALF)
        junk = take(P)
        src_f = take(SLOTS)
        earlier = take(SLOTS)
        pick = take(SLOTS)
        trash = take(SLOTS)
        ids = b.ids
        key_dram = rows_dram
        block = ctx.enter_context(nc.Block())

        @block.sync
        def _(sp):
            with sp.Fori(0, TURNS) as i:
                for h in range(2):
                    half = slice(h * HALF, (h + 1) * HALF)
                    sp.wait_ge(message, i * SLOTS + (h + 1) * HALF)
                    for r in range(2):
                        sp.dma_start(keys[r:r + 1, half, :].rearrange("o u w -> o (u w)"),
                                     key_dram[r:r + 1, bass.ds((i * SLOTS + h * HALF) * 2 * P, HALF * 2 * P)]
                                     ).then_inc(key_rows[h], 16)
                    sp.dma_start(feat[:, half, :],
                                 io["ea64"][:, bass.ds(i * SLOTS + h * HALF, HALF), :]).then_inc(feats[h], 16)
                    starts = [sp.value_load(b.window[0:1, bass.ds(i * SLOTS + h * HALF + v, 1)],
                                            min_val=0, max_val=N) for v in range(HALF)]
                    for v in range(HALF):
                        sp.dma_start(win[:, h * HALF + v, :], table[bass.ds(starts[v], P), :]).then_inc(windows[h], 16)
            
        def bcast(pe, i, u):
            if u % HALF == 0:
                pe.wait_ge(key_rows[u // HALF], 32 * i + 32)
            pe.wait_ge(spread, i * SLOTS + u + 1)
            pe.matmul(b.psum[:, u % 2, 0:2 * P], lhsT=b.bcast_w[0:2, :], rhs=keys[0:2, u, :],
                      start=True, stop=True).then_inc(broadcast, 1)

        def pick_rows(pe, i, u):
            if u % HALF == 0:
                pe.wait_ge(windows[u // HALF], (16 * HALF) * (i + 1))
            pe.wait_ge(spread, 2 + i * SLOTS + u + 1)
            pe.wait_ge(message, SLOTS - 2 + i * SLOTS + u + 1)
            pe.matmul(b.psum[:, 2 + u % 2, 0:D], lhsT=out_hot[:, u % 2, :], rhs=win[:, u, :],
                      start=True, stop=True).then_inc(moved, 1)

        def join(pe, i, u):
            pe.wait_ge(relued, i * SLOTS + u + 1)
            pe.wait_ge(copied, i * SLOTS + u + 1)
            pe.matmul(b.psum[:, 4 + u % 2, 0:D], lhsT=same[:, u % 4, :], rhs=msg[:, u % 4, :],
                      start=True, stop=True).then_inc(joined, 1)

        def pe_turn(pe, i, last, first=False):
            for u in range(SLOTS):
                if u + 1 < SLOTS:
                    bcast(pe, i, u + 1)
                elif not last:
                    bcast(pe, i + 1, 0)
                pick_rows(pe, i, u)
                if u >= 2:
                    join(pe, i, u - 2)
                elif not first:
                    join(pe, i - 1, u - 2 + SLOTS)

        @block.tensor
        def _(pe):
            pe.sem_inc(joined, 4)
            bcast(pe, 0, 0)
            pe_turn(pe, 0, False, True)
            with pe.Fori(1, TURNS - 1) as i:
                pe_turn(pe, i, False)
            pe_turn(pe, TURNS - 1, True)
            join(pe, TURNS - 1, SLOTS - 2)
            join(pe, TURNS - 1, SLOTS - 1)

        @block.scalar
        def _(act):
            act.sem_inc(copied, 2)

            def relu(i, u):
                act.wait_ge(message, SLOTS + i * SLOTS + u + 1)
                act.activation(msg[:, u % 4, :], msg[:, u % 4, :], ACT.Relu).then_inc(relued, 1)

            def copy(i, u):
                act.wait_ge(joined, 4 + i * SLOTS + u + 1)
                act.wait_ge(freed, HALF + i * SLOTS + u + 1)
                act.copy(total[:, u % HALF, :], b.psum[:, 4 + u % 2, 0:D]).then_inc(copied, 1)

            def act_turn(i, first):
                for u in range(SLOTS):
                    relu(i, u)
                    if u >= 2:
                        copy(i, u - 2)
                    elif not first:
                        copy(i - 1, u - 2 + SLOTS)

            act_turn(0, True)
            with act.Fori(1, TURNS) as i:
                act_turn(i, False)
            copy(TURNS - 1, SLOTS - 2)
            copy(TURNS - 1, SLOTS - 1)

        @block.vector
        def _(dve):
            dve.memset(b.acc[:, 0:NT * D], 0.0).then_inc(zeroed, 1)
            dve.sem_inc(spread, 2)
            dve.sem_inc(message, SLOTS)
            with dve.Fori(0, TURNS) as i:
                dve.tensor_copy(src_f, b.src_ids[:, bass.ds(i * SLOTS, SLOTS)]).then_inc(offs, 1)
                dve.wait_ge(offs, i + 1)
                for h in range(2):
                    for v in range(HALF):
                        u = h * HALF + v
                        n = i * SLOTS + u
                        dve.wait_ge(broadcast, n + 1)
                        dve.wait_ge(joined, n + 1)
                        dve.tensor_scalar(same[:, u % 4, :], b.psum[:, u % 2, 0:P], src_f[:, u:u + 1], None,
                                          ALU.is_equal).then_inc(equal, 1)
                        dve.tensor_scalar(out_hot[:, u % 2, :], b.psum[:, u % 2, P:2 * P], b.w("lane"), None,
                                          ALU.is_equal).then_inc(spread, 1)
                        dve.wait_ge(equal, n + 1)
                        dve.tensor_tensor_reduce(junk, same[:, u % 4, :], b.w("below"), 1.0, 0.0, ALU.mult,
                                                 ALU.add, earlier[:, u:u + 1]).then_inc(chain, 1)
                        dve.wait_ge(moved, n + 1)
                        if u % HALF == 0:
                            dve.wait_ge(feats[h], 16 * i + 16)
                        dve.tensor_tensor(msg[:, u % 4, :], b.psum[:, 2 + u % 2, 0:D], feat[:, u, :],
                                          ALU.add).then_inc(message, 1)
                    half = slice(h * HALF, (h + 1) * HALF)
                    k = 2 * i + h
                    dve.wait_ge(chain, i * SLOTS + (h + 1) * HALF)
                    dve.tensor_scalar(pick[:, half], earlier[:, half], 0.0, None, ALU.is_gt).then_inc(ordered, 1)
                    dve.tensor_scalar(trash[:, half], src_f[:, half], -1.0, b.w("trash"),
                                      ALU.mult, ALU.add).then_inc(ordered, 1)
                    dve.wait_ge(ordered, 4 * k + 2)
                    dve.tensor_tensor(trash[:, half], trash[:, half], pick[:, half], ALU.mult).then_inc(ordered, 1)
                    dve.wait_ge(ordered, 4 * k + 3)
                    dve.wait_ge(freed, HALF + i * SLOTS + h * HALF)
                    dve.tensor_tensor(ids[:, half], trash[:, half], src_f[:, half], ALU.add).then_inc(ordered, 1)
                dve.wait_ge(ordered, 8 * i + 8)

        @block.gpsimd
        def _(pool):
            pool.wait_ge(zeroed, 1)
            for c in range(COPIES):
                pool.dma_start(partial[c].rearrange("(p t) d -> p (t d)", p=P),
                               b.acc[:, 0:NT * D]).then_inc(cleared, 16)
            pool.wait_ge(cleared, 16 * COPIES)
            pool.sem_inc(freed, COPIES + HALF)

            def pool_turn(i, first):
                for u in range(SLOTS):
                    h = u // HALF
                    pool.wait_ge(copied, 2 + i * SLOTS + u + 1)
                    if u % HALF == 0:
                        pool.wait_ge(ordered, 4 * (2 * i + h) + 4)
                    if not first or u >= COPIES:
                        pool.wait_ge(sent[u % COPIES], 16 * (i * (SLOTS // COPIES) + u // COPIES))
                    pool.sem_inc(freed, 1)
                    pool.indirect_dma_start(
                        out=partial[u % COPIES],
                        out_offset=bass.IndirectOffsetOnAxis(ap=ids[:, u:u + 1], axis=0),
                        in_=total[:, u % HALF, :], in_offset=None,
                        compute_op=ALU.add).then_inc(sent[u % COPIES], 16)

            pool_turn(0, True)
            with pool.Fori(1, TURNS) as i:
                pool_turn(i, False)
            for c in range(COPIES):
                pool.wait_ge(sent[c], 16 * (SLOTS // COPIES) * TURNS)


def gather_partials(nc, b, partial):
    with stage(nc) as ctx:
        loaded, chain = sems(nc, ctx, "gp_loaded", "gp_chain")
        total = b.acc[:, 0:NT * D]
        parts = [b.query[:, 0:NT * D], b.query[:, NT * D:2 * NT * D],
                 b.node_b[:, 0:NT * D], b.node_b[:, NT * D:2 * NT * D]]
        block = ctx.enter_context(nc.Block())

        @block.sync
        def _(sp):
            with sp.Fori(0, NT) as t:
                for k in range(COPIES):
                    sp.dma_start(parts[k][:, bass.ds(t * D, D)],
                                 partial[k][bass.ds(t * P, P), :]).then_inc(loaded, 16)
            sp.wait_ge(loaded, 16 * COPIES * NT)

        @block.vector
        def _(dve):
            done = [0]

            def link(ins):
                done[0] += 1
                ins.then_inc(chain, 1)
                dve.wait_ge(chain, done[0])

            dve.wait_ge(loaded, 16 * COPIES * NT)
            link(dve.tensor_tensor(parts[0], parts[0], parts[1], ALU.add))
            link(dve.tensor_tensor(parts[2], parts[2], parts[3], ALU.add))
            link(dve.tensor_tensor(parts[0], parts[0], parts[2], ALU.add))
            link(dve.scalar_tensor_tensor(out=total, in0=b.x[:, :], scalar=b.w("eps"), in1=b.x[:, :],
                                          op0=ALU.mult, op1=ALU.add))
            link(dve.tensor_tensor(total, total, parts[0], ALU.add))


def widen(nc, b):
    with stage(nc) as ctx:
        staged, made, copied, gate = sems(nc, ctx, "wi_staged", "wi_made", "wi_copied", "wi_gate")
        held = b.edge_t[:, 0:NODE_SLOTS * P].rearrange("p (u n) -> p u n", u=NODE_SLOTS)
        turns = NT // NODE_SLOTS
        block = ctx.enter_context(nc.Block())

        @block.scalar
        def _(act):
            with act.Fori(0, turns) as i:
                for u in range(NODE_SLOTS):
                    n = i * NODE_SLOTS + u
                    act.wait_ge(made, n + 1)
                    act.sem_inc(gate, 1)
                    act.copy(held[0:D + 1, u, :], b.node_b[0:D + 1, bass.ds(n * P, P)]).then_inc(staged, 1)

        @block.tensor
        def _(pe):
            pe.sem_inc(made, NODE_SLOTS)
            with pe.Fori(0, turns) as i:
                for u in range(NODE_SLOTS):
                    n = i * NODE_SLOTS + u
                    pe.wait_ge(staged, n + 1)
                    pe.wait_ge(copied, n + 1)
                    pe.matmul(b.psum[:, u, 0:P], lhsT=held[0:D + 1, u, :], rhs=b.w("w1", D + 1),
                              start=True, stop=True).then_inc(made, 1)

        @block.vector
        def _(dve):
            dve.sem_inc(copied, NODE_SLOTS)
            with dve.Fori(0, turns) as i:
                for u in range(NODE_SLOTS):
                    n = i * NODE_SLOTS + u
                    dve.wait_ge(made, NODE_SLOTS + n + 1)
                    dve.sem_inc(gate, 1)
                    dve.tensor_copy(b.query[:, bass.ds(n * P, P)], b.psum[:, u, 0:P]).then_inc(copied, 1)


def norm_wide(nc, b):
    with stage(nc) as ctx:
        chain, asked, rooted = sems(nc, ctx, "nw_chain", "nw_asked", "nw_rooted")
        z = b.query[:, 0:NT * P].rearrange("p (t d) -> p t d", d=P)
        spare = b.acc[:, 0:NT * P].rearrange("p (t d) -> p t d", d=P)
        stats = b.hot[:, 0, :]
        var = stats[:, NT:2 * NT]
        block = ctx.enter_context(nc.Block())

        def each_node(w):
            return w.rearrange("p (o d) -> p o d", o=1).broadcast_to([P, NT, P])

        @block.vector
        def _(dve):
            done = [0]

            def link(ins):
                done[0] += 1
                ins.then_inc(chain, 1)
                dve.wait_ge(chain, done[0])

            def act_wait(_):
                dve.sem_inc(asked, 1)
                dve.wait_ge(rooted, 1)

            normalize(dve, link, b, z, P, spare, stats, act_wait)
            link(dve.tensor_tensor(z, z, each_node(b.w("ln_g")), ALU.mult))
            link(dve.tensor_tensor(z, z, each_node(b.w("ln_b")), ALU.add))
            link(dve.tensor_scalar(z, z, 0.0, None, ALU.max))

        @block.scalar
        def _(act):
            act.wait_ge(asked, 1)
            act.sqrt(var, var).then_inc(rooted, 1)


def program(nc, io, out):
    def dram(name, shape, dt=F32):
        return nc.dram_tensor(name, shape, dt, kind="Internal").ap()

    kv_table = dram("kv_table", (NROWS, 2 * D))
    values = dram("values", (P, T, D))
    rel_table = dram("rel_table", (NROWS, RELS * D))
    x_table = dram("x_table", (NROWS, D))
    rows_dram = dram("rows_dram", (2, T * 2 * P), BF16)
    partial = [dram(f"partial{k}", (NROWS, D)) for k in range(COPIES)]

    with ExitStack() as ctx:
        b = Buffers(nc, ctx)
        load_inputs(nc, b, io)
        edge_tables(nc, b, io, rows_dram)

        for n, source, target in ((1, b.node_a, b.node_b), (2, b.node_b, b.node_a)):
            node_rows(nc, b, source, b.w(f"kv{n}", 65), 2 * D, 65, kv_table)
            node_query(nc, b, source, b.w(f"qq{n}", 65))
            edge_scores(nc, b, io, kv_table, values)
            softmax_parts(nc, b, io)
            sum_edges(nc, b, io, ATTEND, values)
            divide_sums(nc, b, b.w(f"comb{n}", 97), b.w("pick96", 97), 1e-30,
                        [(b.w(f"self{n}", 65), source, 65)], True, source, target)
        add_rows(nc, b, [(b.node_b, 64, b.w("skip_h1", 64)), (b.node_a, 65, b.w("skip_h2", 65))], True)
        norm_x(nc, b, x_table)
        turn_nodes(nc, b, b.x, D, b.node_a, True)

        for l in range(LAYERS):
            node_rows(nc, b, b.node_a, b.rel_w[:, l * RELS * D:(l + 1) * RELS * D], RELS * D, 64, rel_table)
            sum_edges(nc, b, io, RELATE, rel_table.rearrange("n (r d) -> (n r) d", d=D))
            if l < LAYERS - 1:
                add_root(nc, b, b.w(f"root{l}", 65), b.node_a)
        add_rows(nc, b, [(b.acc, 64, b.ident(64)), (b.node_a, 65, b.w("root2", 65))], False)
        norm_x(nc, b, x_table)

        scatter_messages(nc, b, io, x_table, rows_dram, partial)
        gather_partials(nc, b, partial)
        restore_one(nc, b)
        turn_nodes(nc, b, b.acc, D, b.node_b, False)
        widen(nc, b)
        norm_wide(nc, b)
        turn_nodes(nc, b, b.query, P, b.acc, False)
        add_rows(nc, b, [(b.acc, P, b.w("w2", P)), (b.node_b, 65, b.w("b2", 65))], False)
        norm_x(nc, b, x_table)
        turn_nodes(nc, b, b.x, D, b.node_a, True)

        sum_edges(nc, b, io, AVERAGE, x_table)
        divide_sums(nc, b, b.w("w_l", 82), b.w("pick64", 82), 1.0,
                    [(b.w("w_r", 65), b.node_a, 65), (b.w("w_e", 82), b.acc, 82)], False, b.node_a, b.node_b)
        add_rows(nc, b, [(b.node_b, 64, b.ident(64))], False)
        norm_x(nc, b, out)


def restore_one(nc, b):
    with stage(nc) as ctx:
        (set_,) = sems(nc, ctx, "ro_set")
        block = ctx.enter_context(nc.Block())

        @block.vector
        def _(dve):
            dve.memset(b.node_b[64:65, :], 1.0).then_inc(set_, 1)


def kernel(**inputs):
    import numpy as np
    import concourse.bacc as _bacc
    from concourse import mybir as _mybir
    from concourse.bass_utils import run_bass_kernel_spmd as _run

    a = {k: np.asarray(v) for k, v in inputs.items()}
    f4, i4 = np.float32, np.int32

    def lane(values, fill, extra=0):
        out = np.full(((T + extra) * P,) + values.shape[1:], fill, values.dtype)
        out[:E] = values
        out = out.reshape((T + extra, P) + values.shape[1:])
        return np.ascontiguousarray(np.swapaxes(out, 0, 1))

    def turn(values, fill):
        out = np.full(T * P, fill, values.dtype)
        out[:E] = values
        return out

    weights = np.zeros((P, WTOTAL), f4)

    def put(name, block, row=0, col=0):
        at = WCOL[name][0] + col
        block = np.atleast_2d(block)
        weights[row:row + block.shape[0], at:at + block.shape[1]] = block

    for n in (1, 2):
        w = {k: a[f"L0_gnn_{k[0]}{n}{k[1:]}"] for k in ("q_w", "q_b", "k_w", "k_b", "v_w", "v_b", "e_w", "s_w", "s_b")}
        put(f"kv{n}", w["k_w"])
        put(f"kv{n}", w["v_w"], 0, D)
        put(f"kv{n}", w["k_b"], 64)
        put(f"kv{n}", w["v_b"], 64, D)
        put(f"qq{n}", w["q_w"])
        put(f"qq{n}", w["q_b"], 64)
        put(f"q{n}_t", w["q_w"].T)
        put(f"q{n}_t", w["q_b"][:, None], 0, 64)
        put(f"e{n}_t", w["e_w"].T)
        put(f"comb{n}", np.eye(D, dtype=f4))
        put(f"comb{n}", w["e_w"], 64)
        put(f"self{n}", w["s_w"])
        put(f"self{n}", w["s_b"], 64)
    put("skip_h1", a["L0_gnn_skip_w"][:D])
    put("skip_h2", a["L0_gnn_skip_w"][D:])
    put("skip_h2", a["L0_gnn_skip_b"], 64)
    for l in range(LAYERS):
        put(f"root{l}", a["L1_gnn_root"][l])
        put(f"root{l}", a["L1_gnn_bias"][l], 64)
    put("w1", a["L2_gnn_W1"])
    put("w1", a["L2_gnn_b1"], 64)
    put("w2", a["L2_gnn_W2"])
    put("b2", a["L2_gnn_b2"], 64)
    put("ln_g", np.broadcast_to(a["L2_gnn_ln_g"], (P, P)))
    put("ln_b", np.broadcast_to(a["L2_gnn_ln_b"], (P, P)))
    put("eps", np.broadcast_to(a["L2_gnn_eps"], (P, 1)))
    put("w_l", a["L3_gnn_W_l"])
    put("w_r", a["L3_gnn_W_r"])
    put("w_r", a["L3_gnn_b_l"], 64)
    put("w_e", a["L3_gnn_W_e"], 65)
    put("w_e", a["L3_gnn_b_e"], 81)
    lanes = np.arange(P, dtype=f4)
    put("pick96", np.ones((1, D), f4), 96)
    put("pick64", np.ones((1, D), f4), 64)
    put("ident", np.eye(P, dtype=f4))
    put("iota", np.broadcast_to(lanes, (P, P)))
    put("below", np.tril(np.ones((P, P), f4), -1))
    put("lane", lanes[:, None])
    put("trash", np.arange(N + 1, N + 1 + P, dtype=f4)[:, None])

    x = a["x"]
    x_pad = np.zeros((NROWS, D), f4)
    x_pad[:N] = x
    x_t = np.zeros((D + 1, NCOLS), f4)
    x_t[:D, :N] = x.T
    x_t[D] = 1.0
    dst = turn(a["dst"], N)
    ext = np.concatenate([np.full(1, -1, i4), dst, np.full(1, -1, i4)])
    dst_turn = np.stack([ext[i * ROW:i * ROW + ROW + 2] for i in range(TURNS)])
    ea32_t = np.zeros((32, T * P), f4)
    ea32_t[:, :E] = a["edge_attr_32"].T

    arrays = {
        "weights": weights,
        "basis": np.ascontiguousarray(a["L1_gnn_basis"].transpose(2, 0, 1, 3).reshape(D, -1)),
        "comp": np.ascontiguousarray(np.broadcast_to(a["L1_gnn_comp"].reshape(1, -1), (D, LAYERS * RELS * BASES))),
        "x_t": x_t,
        "x_rows": np.ascontiguousarray(x_pad.reshape(NT, P, D).transpose(1, 0, 2).reshape(P, NT * D)),
        "src_lane": lane(a["src"], N, SLOTS),
        "type_lane": lane(a["edge_type_8"], 0, SLOTS),
        "window": np.ascontiguousarray(dst.reshape(T, P)[:, 0].reshape(1, T)),
        "dst_turn": dst_turn,
        "type_turn": turn(a["edge_type_8"], 0).reshape(TURNS, ROW),
        "src_turn": turn(a["src"], N).reshape(TURNS, ROW),
        "ea32_t": ea32_t,
        "ea32": lane(a["edge_attr_32"], 0),
        "ea16": lane(a["edge_attr_16"], 0),
        "ea64": lane(a["edge_attr_64"], 0),
    }
    nc = _bacc.Bacc("TRN2", target_bir_lowering=False, num_devices=1)
    io = {k: nc.dram_tensor(f"in_{k}", v.shape, _mybir.dt.from_np(v.dtype), kind="ExternalInput").ap()
          for k, v in arrays.items()}
    out = nc.dram_tensor("out", (N, D), _mybir.dt.float32, kind="ExternalOutput").ap()
    program(nc, io, out)
    r = _run(nc, [{f"in_{k}": v for k, v in arrays.items()}], core_ids=[0])
    return r.results[0]["out"]
```

```python
from contextlib import ExitStack, contextmanager

import concourse.bass as bass
from concourse import mybir

F32 = mybir.dt.float32
BF16 = mybir.dt.bfloat16
I32 = mybir.dt.int32
ALU = mybir.AluOpType
ACT = mybir.ActivationFunctionType
AX = mybir.AxisListType

P = 128
D = 64
N = 6250
E = 206250
SLOTS = 16
HALF = SLOTS // 2
GROUP = 4
GROUPS = SLOTS // GROUP
TURNS = -(-E // (P * SLOTS))
T = TURNS * SLOTS
ROW = SLOTS * P
NT = 50
NROWS = NT * P
CHUNKS = 16
CW = 404
NCOLS = CHUNKS * CW
RELS = 8
BASES = 4
LAYERS = 3
COPIES = 4
PARTS = 3
BIG = 3.0e38
EPS = 1e-5
NODE_SLOTS = 5

GAP_BITS = ((GROUP - 1) * P).bit_length()
assert (GROUP - 1) * GAP_BITS < 31 and GAP_BITS == 9
assert NROWS >= N + 1 + P and NCOLS >= N + P

WIDTHS = [
    ("kv1", 128), ("qq1", 96), ("comb1", 64), ("self1", 64),
    ("kv2", 128), ("qq2", 96), ("comb2", 64), ("self2", 64),
    ("skip_h1", 64), ("skip_h2", 64),
    ("root0", 64), ("root1", 64), ("root2", 64),
    ("w1", 128), ("w2", 64), ("b2", 64), ("ln_g", 128), ("ln_b", 128), ("eps", 1),
    ("w_l", 64), ("w_e", 64), ("w_r", 64),
    ("pick96", 64), ("pick64", 64),
    ("ident", 128), ("iota", 128), ("below", 128), ("minus_lane", 1), ("one", 1), ("trash", 1),
    ("q1_t", 65), ("e1_t", 32), ("q2_t", 65), ("e2_t", 32),
]
WCOL = {}
_at = 0
for _name, _w in WIDTHS:
    WCOL[_name] = (_at, _w)
    _at += _w
WTOTAL = _at


class Buffers:

    def __init__(self, nc, ctx):
        def sb(name, shape, dt):
            return ctx.enter_context(nc.sbuf_tensor(name, shape, dt))

        self.node_a = sb("node_a", [P, NCOLS], F32)
        self.node_b = sb("node_b", [P, NCOLS], F32)
        self.query = sb("query", [P, NCOLS], F32)
        self.acc = sb("acc", [P, N + GROUP * P + 2], F32)
        self.x = sb("x", [P, NT * D], F32)
        self.weights = sb("weights", [P, WTOTAL], F32)
        self.rel_w = sb("rel_w", [D, LAYERS * RELS * D], F32)
        self.src_ids = sb("src_ids", [P, T + SLOTS], I32)
        self.rel_ids = sb("rel_ids", [P, T + SLOTS], I32)
        self.dst_off = sb("dst_off", [P, T + SLOTS], F32)
        self.rel_wt = sb("rel_wt", [P, T + SLOTS], F32)
        self.is_last = sb("is_last", [P, T], F32)
        self.score = sb("score", [P, T + SLOTS], F32)
        self.window = sb("window", [1, T], I32)
        self.window_gap = sb("window_gap", [1, T // GROUP], I32)
        self.ring_hot = sb("ring_hot", [P, 18 * SLOTS], F32)
        self.ring = sb("ring", [P, SLOTS, P], F32)
        self.ids = sb("ids", [P, SLOTS], I32)
        self.edge_t = sb("edge_t", [P, ROW], F32)
        self.hot = sb("hot", [P, 4, P], F32)
        self.bcast_w = sb("bcast_w", [2, P], BF16)
        self.psum = ctx.enter_context(nc.psum_tensor("psum", [P, 8, 512], F32))

    def w(self, name, rows=P):
        a, n = WCOL[name]
        return self.weights[0:rows, a:a + n]

    def ident(self, n=P):
        a = WCOL["ident"][0]
        return self.weights[0:n, a:a + n]


@contextmanager
def stage(nc):
    before = nc.snapshot_sems()
    with ExitStack() as ctx:
        yield ctx
    nc.clear_and_free_semaphores(nc.allocated_since(before))
    nc.all_engine_barrier()


def tiles_of(g):
    return range(g * GROUP, (g + 1) * GROUP)


def window_gaps(eng, b, n):
    packed = eng.value_load(b.window_gap[0:1, bass.ds(n, 1)], min_val=0, max_val=(1 << (GROUP - 1) * GAP_BITS) - 1)
    return [0] + [((packed >> (u * GAP_BITS)) & ((1 << GAP_BITS) - 1)).with_bounds(min_val=0, max_val=(GROUP - 1) * P)
                  for u in range(GROUP - 1)]


def window_starts(eng, b, n):
    first = eng.value_load(b.window[0:1, bass.ds(n * GROUP, 1)], min_val=0, max_val=N)
    return [(first + gap).with_bounds(min_val=0, max_val=N) if v else first for v, gap in enumerate(window_gaps(eng, b, n))]


def sems(nc, ctx, *names):
    return [nc.alloc_semaphore(name=f"{n}_{nc.next_id()}") for n in names]


def by_slot(columns):
    return columns[:, 0:T].rearrange("p (i u) -> p u i", u=SLOTS)


def load_inputs(nc, b, io):
    with stage(nc) as ctx:
        loaded, chain, folded, kept = sems(nc, ctx, "in_loaded", "in_chain", "in_folded", "in_kept")
        basis = b.acc[0:D, 0:LAYERS * BASES * D].rearrange("c (l b h) -> c l b h", l=LAYERS, b=BASES)
        comp = b.acc[0:D, LAYERS * BASES * D:LAYERS * BASES * D + LAYERS * RELS * BASES]
        block = ctx.enter_context(nc.Block())

        @block.sync
        def _(sp):
            sp.dma_start(b.weights[:, :], io["weights"]).then_inc(loaded, 16)
            sp.dma_start(b.acc[0:D, 0:LAYERS * BASES * D], io["basis"]).then_inc(loaded, 16)
            sp.dma_start(comp, io["comp"]).then_inc(loaded, 16)
            sp.dma_start(b.node_a[0:D + 1, :], io["x_t"]).then_inc(loaded, 16)
            sp.dma_start(b.x[:, :], io["x_rows"]).then_inc(loaded, 16)
            sp.dma_start(b.src_ids[:, :], io["src_lane"]).then_inc(loaded, 16)
            sp.dma_start(b.rel_ids[:, :], io["type_lane"]).then_inc(loaded, 16)
            sp.dma_start(b.window[:, :], io["window"]).then_inc(loaded, 16)
            sp.wait_ge(loaded, 128)

        @block.tensor
        def _(pe):
            pe.wait_ge(loaded, 128)
            for n in (1, 2):
                pe.matmul(b.psum[0:65, n, 0:32], lhsT=b.w(f"q{n}_t", D), rhs=b.w(f"e{n}_t", D),
                          start=True, stop=True).then_inc(folded, 1)

        @block.vector
        def _(dve):
            done = [0]

            def link(ins):
                done[0] += 1
                ins.then_inc(chain, 1)
                dve.wait_ge(chain, done[0])

            dve.wait_ge(loaded, 128)
            for l in range(LAYERS):
                for r in range(RELS):
                    out = b.rel_w[:, (l * RELS + r) * D:(l * RELS + r + 1) * D]
                    for k in range(BASES):
                        at = (l * RELS + r) * BASES + k
                        if k == 0:
                            link(dve.tensor_scalar(out, basis[:, l, k, :], comp[:, at:at + 1], None, ALU.mult))
                        else:
                            link(dve.scalar_tensor_tensor(out=out, in0=basis[:, l, k, :], scalar=comp[:, at:at + 1],
                                                          in1=out, op0=ALU.mult, op1=ALU.add))
            starts = b.window[:, :].rearrange("o (n u) -> o n u", u=GROUP)
            spare = b.acc[0:1, LAYERS * BASES * D + LAYERS * RELS * BASES:][:, 0:T].bitcast(I32)
            gaps = spare.rearrange("o (n u) -> o n u", u=GROUP)
            packed = b.window_gap[:, :].rearrange("o (n u) -> o n u", u=1)
            link(dve.tensor_tensor(gaps, starts, starts[:, :, 0:1].broadcast_to([1, T // GROUP, GROUP]),
                                   ALU.subtract))
            link(dve.tensor_copy(packed, gaps[:, :, 1:2]))
            for u in range(2, GROUP):
                link(dve.tensor_scalar(gaps[:, :, u:u + 1], gaps[:, :, u:u + 1], (u - 1) * GAP_BITS, None,
                                       ALU.logical_shift_left))
                link(dve.tensor_tensor(packed, packed, gaps[:, :, u:u + 1], ALU.bitwise_or))
            link(dve.scalar_tensor_tensor(out=b.rel_ids[:, :], in0=b.src_ids[:, :], scalar=float(RELS),
                                          in1=b.rel_ids[:, :], op0=ALU.mult, op1=ALU.add))
            for columns in (b.dst_off, b.rel_wt, b.score):
                link(dve.memset(columns[:, T:T + SLOTS], 0.0))
            dve.memset(b.node_b[64:65, :], 1.0).then_inc(kept, 1)
            dve.memset(b.bcast_w[0:2, :], 1.0).then_inc(kept, 1)
            dve.wait_ge(kept, 2)
            dve.memset(b.bcast_w[0:1, :], float(P)).then_inc(kept, 1)
            dve.wait_ge(folded, 2)
            for n in (1, 2):
                a = WCOL[f"qq{n}"][0] + D
                dve.tensor_copy(b.weights[0:65, a:a + 32], b.psum[0:65, n, 0:32]).then_inc(kept, 1)
            dve.wait_ge(kept, 5)


def turn_view(buffer, n):
    return buffer[0:TURNS, n * ROW:(n + 1) * ROW]


def carry_rows(pe, b, cols, n, carry_ready, carry_turned, k):
    pe.wait_ge(carry_ready, 2 * k + 1)
    for j in range(2):
        ins = pe.transpose(b.psum[0:n, 4 + j, 0:TURNS], cols[0:TURNS, j, 0:n], b.ident(TURNS))
    ins.then_inc(carry_turned, 1)
    pe.wait_ge(carry_ready, 2 * k + 2)
    pe.transpose(b.psum[0:TURNS, 7, 0:n], b.hot[0:n, 2, 0:TURNS], b.ident(n)).then_inc(carry_turned, 1)


def carry_scan(dve, link, b, n, ops, start, backward, into, carry_ready, carry_turned, k):
    lasts, flags, out = b.hot[0:n, 0, 0:TURNS], b.hot[0:n, 1, 0:TURNS], b.hot[0:n, 3, 0:TURNS]
    shifted = b.hot[0:n, 2, 0:TURNS]
    dve.wait_ge(carry_turned, 2 * k + 1)
    link(dve.tensor_copy(lasts, b.psum[0:n, 4, 0:TURNS]))
    link(dve.tensor_copy(flags, b.psum[0:n, 5, 0:TURNS]))
    link(dve.memset(shifted, start))
    if backward:
        link(dve.tensor_tensor_scan(out[:, ::-1], flags[:, ::-1], lasts[:, ::-1], start, *ops))
        link(dve.tensor_copy(shifted[:, 0:TURNS - 1], out[:, 1:TURNS]))
    else:
        link(dve.tensor_tensor_scan(out, flags, lasts, start, *ops))
        link(dve.tensor_copy(shifted[:, 1:TURNS], out[:, 0:TURNS - 1]))
    dve.sem_inc(carry_ready, 1)
    dve.wait_ge(carry_turned, 2 * k + 2)
    link(dve.tensor_copy(into, b.psum[0:TURNS, 7, 0:n]))


def lanes_from_turns(pe, b, source, ready, count, turned):
    pe.wait_ge(ready, count)
    for u in range(SLOTS):
        ins = pe.transpose(b.psum[:, u // 4, (u % 4) * P:(u % 4) * P + TURNS],
                           source[:, u * P:(u + 1) * P], b.ident(TURNS))
    ins.then_inc(turned, 1)


def copy_lanes(dve, link, b, columns):
    for q in range(4):
        link(dve.tensor_copy(by_slot(columns)[:, 4 * q:4 * q + 4, :],
                             b.psum[:, q, :].rearrange("p (u e) -> p u e", e=P)[:, :, 0:TURNS]))


def edge_tables(nc, b, io, rows_dram):
    with stage(nc) as ctx:
        loaded, chain, ready, turned, carry_ready, carry_turned, stored = sems(
            nc, ctx, "et_loaded", "et_chain", "et_ready", "et_turned", "et_carry_ready", "et_carry_turned",
            "et_stored")
        dst_i = b.query[0:TURNS, 0:ROW + 2].bitcast(I32)
        dst = b.query[0:TURNS, ROW + 2:2 * ROW + 4]
        dst_mid = dst[:, 1:ROW + 1]
        onward = turn_view(b.acc, 0)
        back = turn_view(b.acc, 1)
        kind_i = turn_view(b.acc, 2).bitcast(I32)
        kind = b.node_b[0:TURNS, 0:ROW]
        this = b.node_b[0:TURNS, ROW:2 * ROW]
        ahead = b.node_b[0:TURNS, 2 * ROW:3 * ROW]
        behind = b.query[0:TURNS, 2 * ROW + 4:3 * ROW + 4]
        total = b.edge_t[0:TURNS, :]
        src_i = turn_view(b.acc, 2).bitcast(I32)
        part_i = b.node_b[0:TURNS, 0:ROW].bitcast(I32)
        halves = b.ring[0:TURNS, :, :].rearrange("p u e -> p (u e)").bitcast(BF16)
        rows_hi, rows_lo = halves[:, 0:2 * ROW], b.node_b[0:TURNS, ROW:2 * ROW].bitcast(BF16)
        cols = b.score[0:TURNS, 0:2 * RELS * 2].rearrange("p (w j n) -> p w j n", w=2, j=2)
        carried = b.score[0:TURNS, 64:64 + 2 * RELS].rearrange("p (w n) -> p w n", w=2)
        block = ctx.enter_context(nc.Block())

        @block.sync
        def _(sp):
            sp.dma_start(dst_i, io["dst_turn"]).then_inc(loaded, 16)
            sp.dma_start(kind_i, io["type_turn"]).then_inc(loaded, 16)
            sp.wait_ge(ready, 1)
            sp.dma_start(src_i, io["src_turn"]).then_inc(loaded, 16)
            sp.wait_ge(ready, 5)
            sp.dma_start(rows_dram[0].rearrange("(i e) -> i e", i=TURNS), rows_hi).then_inc(stored, 16)
            sp.dma_start(rows_dram[1].rearrange("(i e) -> i e", i=TURNS), rows_lo).then_inc(stored, 16)
            sp.wait_ge(stored, 32)

        @block.tensor
        def _(pe):
            lanes_from_turns(pe, b, this, ready, 1, turned)
            lanes_from_turns(pe, b, ahead, ready, 2, turned)
            carry_rows(pe, b, cols[:, 0], RELS, carry_ready, carry_turned, 0)
            carry_rows(pe, b, cols[:, 1], RELS, carry_ready, carry_turned, 1)
            lanes_from_turns(pe, b, total, ready, 4, turned)

        @block.vector
        def _(dve):
            done = [0]

            def link(ins):
                done[0] += 1
                ins.then_inc(chain, 1)
                dve.wait_ge(chain, done[0])

            dve.wait_ge(loaded, 32)
            link(dve.tensor_copy(dst, dst_i))
            link(dve.tensor_copy(kind, kind_i))
            link(dve.tensor_tensor(onward, dst_mid, dst[:, 0:ROW], ALU.is_equal))
            link(dve.tensor_tensor(back, dst_mid, dst[:, 2:ROW + 2], ALU.is_equal))
            d3 = dst_mid.rearrange("p (u e) -> p u e", e=P)
            link(dve.tensor_tensor(this.rearrange("p (u e) -> p u e", e=P), d3,
                                   d3[:, :, 0:1].broadcast_to([TURNS, SLOTS, P]), ALU.subtract))
            dve.sem_inc(ready, 1)
            link(dve.tensor_scalar(ahead, back, -1.0, 1.0, ALU.mult, ALU.add))
            dve.wait_ge(turned, 1)
            copy_lanes(dve, link, b, b.dst_off)
            dve.sem_inc(ready, 1)
            hi3 = rows_hi.rearrange("p (u w e) -> p u w e", u=SLOTS, w=2)
            dve.wait_ge(turned, 2)
            copy_lanes(dve, link, b, b.is_last)

            scan = (ALU.mult, ALU.add)
            link(dve.tensor_reduce(cols[:, 0, 1, 0:1], onward, AX.X, ALU.min))
            link(dve.tensor_reduce(cols[:, 1, 1, 0:1], back, AX.X, ALU.min))
            for w in range(2):
                link(dve.tensor_copy(cols[:, w, 1, 1:RELS], cols[:, w, 1, 0:1].broadcast_to([TURNS, RELS - 1])))
            for r in range(RELS):
                link(dve.tensor_scalar(this, kind, float(r), None, ALU.is_equal))
                link(dve.tensor_tensor_scan(ahead, onward, this, 0.0, *scan))
                link(dve.tensor_tensor_scan(behind[:, ::-1], back[:, ::-1], this[:, ::-1], 0.0, *scan))
                link(dve.tensor_copy(cols[:, 0, 0, r:r + 1], ahead[:, ROW - 1:ROW]))
                link(dve.tensor_copy(cols[:, 1, 0, r:r + 1], behind[:, 0:1]))
            dve.sem_inc(carry_ready, 1)
            carry_scan(dve, link, b, RELS, scan, 0.0, False, carried[:, 0, :], carry_ready, carry_turned, 0)
            dve.sem_inc(carry_ready, 1)
            carry_scan(dve, link, b, RELS, scan, 0.0, True, carried[:, 1, :], carry_ready, carry_turned, 1)
            link(dve.memset(total, 0.0))
            for r in range(RELS):
                link(dve.tensor_scalar(this, kind, float(r), None, ALU.is_equal))
                link(dve.tensor_tensor_scan(ahead, onward, this, carried[:, 0, r:r + 1], *scan))
                link(dve.tensor_tensor_scan(behind[:, ::-1], back[:, ::-1], this[:, ::-1],
                                            carried[:, 1, r:r + 1], *scan))
                link(dve.tensor_tensor(ahead, ahead, behind, ALU.add))
                link(dve.scalar_tensor_tensor(out=ahead, in0=ahead, scalar=-1.0, in1=this,
                                              op0=ALU.add, op1=ALU.mult))
                link(dve.tensor_tensor(total, total, ahead, ALU.add))
            link(dve.reciprocal(total, total))
            dve.sem_inc(ready, 2)
            dve.wait_ge(turned, 3)
            copy_lanes(dve, link, b, b.rel_wt)

            dve.wait_ge(loaded, 48)
            link(dve.memset(rows_hi, 0.0))
            link(dve.tensor_scalar(part_i, src_i, 7, None, ALU.logical_shift_right))
            link(dve.tensor_copy(hi3[:, :, 0, :], part_i.rearrange("p (u e) -> p u e", e=P)))
            link(dve.tensor_scalar(part_i, src_i, P - 1, None, ALU.bitwise_and))
            lo3 = rows_lo.rearrange("p (u w e) -> p u w e", u=SLOTS, w=2)
            link(dve.tensor_copy(lo3[:, :, 0, :], part_i.rearrange("p (u e) -> p u e", e=P)))
            link(dve.tensor_tensor(lo3[:, :, 1, :], d3,
                                   d3[:, :, 0:1].broadcast_to([TURNS, SLOTS, P]), ALU.subtract))
            dve.sem_inc(ready, 1)
            dve.wait_ge(stored, 32)
            link(dve.memset(b.node_b[64:65, :], 1.0))


def node_rows(nc, b, source, weights, ncols, rows, table):
    with stage(nc) as ctx:
        staged, made, copied, gate = sems(nc, ctx, "nr_staged", "nr_made", "nr_copied", "nr_gate")
        stored = sems(nc, ctx, *[f"nr_stored{u}" for u in range(NODE_SLOTS)])
        out = b.query[:, 0:NODE_SLOTS * ncols].rearrange("p (u n) -> p u n", u=NODE_SLOTS)
        table_rows = table.rearrange("(t p) n -> t p n", p=P)
        turns = NT // NODE_SLOTS
        block = ctx.enter_context(nc.Block())

        @block.scalar
        def _(act):
            with act.Fori(0, turns) as i:
                for u in range(NODE_SLOTS):
                    n = i * NODE_SLOTS + u
                    act.wait_ge(made, n + 1)
                    act.sem_inc(gate, 1)
                    act.copy(b.edge_t[0:rows, u * P:(u + 1) * P],
                             source[0:rows, bass.ds(n * P, P)]).then_inc(staged, 1)

        @block.tensor
        def _(pe):
            pe.sem_inc(made, NODE_SLOTS)
            with pe.Fori(0, turns) as i:
                for u in range(NODE_SLOTS):
                    n = i * NODE_SLOTS + u
                    pe.wait_ge(staged, n + 1)
                    pe.wait_ge(copied, n + 1)
                    pe.matmul(b.psum[:, u, 0:ncols], lhsT=b.edge_t[0:rows, u * P:(u + 1) * P],
                              rhs=weights, start=True, stop=True).then_inc(made, 1)

        @block.vector
        def _(dve):
            dve.sem_inc(copied, NODE_SLOTS)
            with dve.Fori(0, turns) as i:
                for u in range(NODE_SLOTS):
                    n = i * NODE_SLOTS + u
                    dve.wait_ge(made, NODE_SLOTS + n + 1)
                    dve.wait_ge(stored[u], 16 * i + 16)
                    dve.tensor_copy(out[:, u, :], b.psum[:, u, 0:ncols]).then_inc(copied, 1)

        @block.sync
        def _(sp):
            for u in range(NODE_SLOTS):
                sp.sem_inc(stored[u], 16)
            with sp.Fori(0, turns) as i:
                for u in range(NODE_SLOTS):
                    n = i * NODE_SLOTS + u
                    sp.wait_ge(copied, NODE_SLOTS + n + 1)
                    sp.dma_start(table_rows[bass.ds(n, 1), :, :].rearrange("o p n -> (o p) n"),
                                 out[:, u, :]).then_inc(stored[u], 16)
            for u in range(NODE_SLOTS):
                sp.wait_ge(stored[u], 16 * turns + 16)


def node_query(nc, b, source, weights):
    with stage(nc) as ctx:
        made, copied, gate = sems(nc, ctx, "nq_made", "nq_copied", "nq_gate")
        block = ctx.enter_context(nc.Block())

        @block.tensor
        def _(pe):
            with pe.Fori(0, CHUNKS // 2) as i:
                for u in range(2):
                    pe.wait_ge(copied, 2 * i + u + 1)
                    pe.sem_inc(gate, 1)
                    pe.matmul(b.psum[0:96, u, 0:CW], lhsT=weights,
                              rhs=source[0:D + 1, bass.ds((2 * i + u) * CW, CW)],
                              start=True, stop=True).then_inc(made, 1)

        @block.scalar
        def _(act):
            act.sem_inc(copied, 2)
            with act.Fori(0, CHUNKS // 2) as i:
                for u in range(2):
                    act.wait_ge(made, 2 * i + u + 1)
                    act.sem_inc(gate, 1)
                    act.copy(b.query[0:96, bass.ds((2 * i + u) * CW, CW)],
                             b.psum[0:96, u, 0:CW]).then_inc(copied, 1)


def first_ids(act, b, index, ids):
    for g in range(GROUPS):
        mine = slice(g * GROUP, (g + 1) * GROUP)
        act.copy(b.ids[:, mine], index[:, mine]).then_inc(ids, 1)


def next_ids(act, b, index, ids, i, g):
    act.copy(b.ids[:, g * GROUP:(g + 1) * GROUP],
             index[:, bass.ds((i + 1) * SLOTS + g * GROUP, GROUP)]).then_inc(ids, 1)


def edge_scores(nc, b, io, table, values):
    with stage(nc) as ctx:
        ids, turned, keyed, scored, picked, gate, offs, kept = sems(
            nc, ctx, "sc_ids", "sc_turned", "sc_keyed", "sc_scored", "sc_picked", "sc_gate", "sc_offs", "sc_kept")
        got = sems(nc, ctx, *[f"sc_got{g}" for g in range(GROUPS)])
        spilled = sems(nc, ctx, "sc_spilled0", "sc_spilled1")
        feats = sems(nc, ctx, "sc_feats0", "sc_feats1")
        off16 = b.hot[:, 0, 0:SLOTS]
        score16 = b.hot[:, 0, SLOTS:2 * SLOTS]
        block = ctx.enter_context(nc.Block())

        @block.gpsimd
        def _(pool):
            with pool.Fori(0, TURNS) as i:
                for g in range(GROUPS):
                    h = g // 2
                    pool.wait_ge(ids, i * GROUPS + g + 1)
                    if g % 2 == 0:
                        pool.wait_ge(spilled[h], 16 * i + 16)
                    pool.wait_ge(turned, i * GROUPS + g + 1)
                    pool.sem_inc(gate, 1)
                    for u in tiles_of(g):
                        pool.indirect_dma_start(
                            out=b.ring[:, u, :], out_offset=None, in_=table,
                            in_offset=bass.IndirectOffsetOnAxis(ap=b.ids[:, u:u + 1], axis=0)).then_inc(got[g], 16)

        @block.sync
        def _(sp):
            for h in range(2):
                sp.sem_inc(spilled[h], 16)
            with sp.Fori(0, TURNS) as i:
                for h in range(2):
                    sp.wait_ge(scored, i * GROUPS + 2 * h + 2)
                    sp.dma_start(b.edge_t[D:D + 32, h * HALF * P:(h + 1) * HALF * P],
                                 io["ea32_t"][:, bass.ds(i * ROW + h * HALF * P, HALF * P)]).then_inc(feats[h], 16)
                    for g in (2 * h, 2 * h + 1):
                        sp.wait_ge(got[g], 16 * GROUP * (i + 1))
                    sp.dma_start(values[:, bass.ds(i * SLOTS + h * HALF, HALF), :],
                                 b.ring[:, h * HALF:(h + 1) * HALF, D:2 * D]).then_inc(spilled[h], 16)
            for h in range(2):
                sp.wait_ge(spilled[h], 16 * TURNS + 16)

        def turn_keys(pe, i, g):
            pe.wait_ge(got[g], 16 * GROUP * (i + 1))
            pe.wait_ge(keyed, i * GROUPS + g + 1)
            pe.sem_inc(gate, 1)
            for u in tiles_of(g):
                ins = pe.transpose(b.psum[0:D, g % 2, (u % GROUP) * P:(u % GROUP + 1) * P], b.ring[:, u, 0:D],
                                   b.ident())
            ins.then_inc(turned, 1)

        def score(pe, i, g, starts):
            pe.wait_ge(keyed, 2 + i * GROUPS + g + 1)
            if g % 2 == 0:
                pe.wait_ge(feats[g // 2], 16 * i + 16)
            pe.wait_ge(picked, i * GROUPS + g + 1)
            pe.sem_inc(gate, 1)
            for u in tiles_of(g):
                ins = pe.matmul(b.psum[:, 2 + g % 2, (u % GROUP) * P:(u % GROUP + 1) * P],
                                lhsT=b.edge_t[0:96, u * P:(u + 1) * P],
                                rhs=b.query[0:96, bass.ds(starts[u % GROUP], P)], start=True, stop=True)
            ins.then_inc(scored, 1)

        def pe_turn(pe, i, last):
            for g in range(GROUPS):
                starts = window_starts(pe, b, i * GROUPS + g)
                if g + 1 < GROUPS:
                    turn_keys(pe, i, g + 1)
                elif not last:
                    turn_keys(pe, i + 1, 0)
                score(pe, i, g, starts)

        @block.tensor
        def _(pe):
            pe.sem_inc(turned, GROUPS)
            pe.sem_inc(scored, GROUPS)
            turn_keys(pe, 0, 0)
            with pe.Fori(0, TURNS - 1) as i:
                pe_turn(pe, i, False)
            pe_turn(pe, TURNS - 1, True)

        @block.scalar
        def _(act):
            act.sem_inc(keyed, 2)
            first_ids(act, b, b.src_ids, ids)
            with act.Fori(0, TURNS) as i:
                for g in range(GROUPS):
                    act.wait_ge(turned, GROUPS + i * GROUPS + g + 1)
                    act.sem_inc(gate, 1)
                    next_ids(act, b, b.src_ids, ids, i, g)
                    act.wait_ge(scored, i * GROUPS + g + 1)
                    act.copy(b.edge_t[0:D, g * GROUP * P:(g + 1) * GROUP * P], b.psum[0:D, g % 2, :]).then_inc(keyed, 1)

        @block.vector
        def _(dve):
            dve.sem_inc(picked, 2)
            with dve.Fori(0, TURNS) as i:
                dve.tensor_copy(off16, b.dst_off[:, bass.ds(i * SLOTS, SLOTS)]).then_inc(offs, 1)
                dve.wait_ge(offs, i + 1)
                for g in range(GROUPS):
                    dve.wait_ge(scored, GROUPS + i * GROUPS + g + 1)
                    for u in tiles_of(g):
                        found = b.psum[:, 2 + g % 2, (u % GROUP) * P:(u % GROUP + 1) * P]
                        ins = dve.scalar_tensor_tensor(
                            out=found, in0=b.w("iota"), scalar=off16[:, u:u + 1], in1=found,
                            op0=ALU.is_equal, op1=ALU.mult, accum_out=score16[:, u:u + 1])
                    ins.then_inc(picked, 1)
                dve.wait_ge(picked, 2 + (i + 1) * GROUPS)
                dve.tensor_copy(b.score[:, bass.ds(i * SLOTS, SLOTS)], score16).then_inc(kept, 1)
                dve.wait_ge(kept, i + 1)


def softmax_parts(nc, b, io):
    with stage(nc) as ctx:
        loaded, chain, turned, ready, carry_ready, carry_turned, shifted, raised = sems(
            nc, ctx, "sm_loaded", "sm_chain", "sm_turned", "sm_ready", "sm_carry_ready", "sm_carry_turned",
            "sm_shifted", "sm_raised")
        dst = b.query[0:TURNS, 0:ROW + 2].bitcast(I32)
        by_turn = b.query[0:TURNS, ROW + 2:2 * ROW + 2]
        ahead = b.query[0:TURNS, 2 * ROW + 2:3 * ROW + 2]
        onward, back, behind = (turn_view(b.acc, k) for k in range(3))
        cols = b.ring[0:TURNS, 0, 0:4].rearrange("p (w j n) -> p w j n", w=2, j=2)
        carried = b.ring[0:TURNS, 1, 0:2]
        block = ctx.enter_context(nc.Block())

        @block.sync
        def _(sp):
            sp.dma_start(dst, io["dst_turn"]).then_inc(loaded, 16)

        @block.tensor
        def _(pe):
            for u in range(SLOTS):
                ins = pe.transpose(b.psum[0:TURNS, u // 4, (u % 4) * P:(u % 4 + 1) * P],
                                   by_slot(b.score)[:, u, :], b.ident())
            ins.then_inc(turned, 1)
            carry_rows(pe, b, cols[:, 0], 1, carry_ready, carry_turned, 0)
            carry_rows(pe, b, cols[:, 1], 1, carry_ready, carry_turned, 1)
            lanes_from_turns(pe, b, by_turn, raised, 1, turned)

        @block.scalar
        def _(act):
            act.wait_ge(shifted, 1)
            act.activation(by_turn, by_turn, ACT.Exp, scale=float(D) ** -0.5).then_inc(raised, 1)

        @block.vector
        def _(dve):
            done = [0]

            def link(ins):
                done[0] += 1
                ins.then_inc(chain, 1)
                dve.wait_ge(chain, done[0])

            dve.wait_ge(loaded, 16)
            for flag, lo in ((onward, 0), (back, 2)):
                link(dve.tensor_tensor(flag, dst[:, 1:ROW + 1], dst[:, lo:lo + ROW], ALU.is_equal))
                link(dve.tensor_scalar(flag, flag, 2 * BIG / 2, None, ALU.mult))
                link(dve.tensor_scalar(flag, flag, -BIG / 2, 2.0, ALU.add, ALU.mult))
            dve.wait_ge(turned, 1)
            for q in range(4):
                link(dve.tensor_copy(by_turn[:, q * 512:(q + 1) * 512], b.psum[0:TURNS, q, :]))
            scan = (ALU.min, ALU.max)
            link(dve.tensor_reduce(cols[:, 0, 1, :], onward, AX.X, ALU.min))
            link(dve.tensor_reduce(cols[:, 1, 1, :], back, AX.X, ALU.min))
            link(dve.tensor_tensor_scan(ahead, onward, by_turn, -BIG, *scan))
            link(dve.tensor_tensor_scan(behind[:, ::-1], back[:, ::-1], by_turn[:, ::-1], -BIG, *scan))
            link(dve.tensor_copy(cols[:, 0, 0, :], ahead[:, ROW - 1:ROW]))
            link(dve.tensor_copy(cols[:, 1, 0, :], behind[:, 0:1]))
            dve.sem_inc(carry_ready, 1)
            carry_scan(dve, link, b, 1, scan, -BIG, False, carried[:, 0:1], carry_ready, carry_turned, 0)
            dve.sem_inc(carry_ready, 1)
            carry_scan(dve, link, b, 1, scan, -BIG, True, carried[:, 1:2], carry_ready, carry_turned, 1)
            link(dve.tensor_tensor_scan(ahead, onward, by_turn, carried[:, 0:1], *scan))
            link(dve.tensor_tensor_scan(behind[:, ::-1], back[:, ::-1], by_turn[:, ::-1], carried[:, 1:2], *scan))
            link(dve.tensor_tensor(ahead, ahead, behind, ALU.max))
            dve.tensor_tensor(by_turn, by_turn, ahead, ALU.subtract).then_inc(shifted, 1)
            dve.wait_ge(turned, 2)
            copy_lanes(dve, link, b, b.score)


ATTEND, RELATE, AVERAGE = range(3)
SUM_ROWS = {ATTEND: 97, RELATE: 64, AVERAGE: 82}


def sum_edges(nc, b, io, what, source):
    rows = SUM_ROWS[what]
    weight = {ATTEND: b.score, RELATE: b.rel_wt, AVERAGE: None}[what]
    index = {ATTEND: None, RELATE: b.rel_ids, AVERAGE: b.src_ids}[what]
    with stage(nc) as ctx:
        ids, hot, summed, added, gate, offs, cleared, extra, zeroed = sems(
            nc, ctx, "su_ids", "su_hot", "su_summed", "su_added", "su_gate", "su_offs", "su_cleared", "su_extra",
            "su_zeroed")
        got = sems(nc, ctx, *[f"su_got{g}" for g in range(GROUPS)]) if index is not None else None
        rows_in = sems(nc, ctx, "su_rows0", "su_rows1")
        off16, wt16 = b.ring_hot[:, 0:SLOTS], b.ring_hot[:, SLOTS:2 * SLOTS]
        feats16 = b.ring_hot[:, 2 * SLOTS:18 * SLOTS].rearrange("p (u f) -> p u f", u=SLOTS)
        hots = b.edge_t[:, 0:2 * GROUP * P].rearrange("p (g u n) -> p g u n", g=2, u=GROUP)
        zeros = b.edge_t[0:1, 2 * GROUP * P:2 * GROUP * P + 320].bitcast(BF16)
        block = ctx.enter_context(nc.Block())

        if index is not None:
            @block.gpsimd
            def _(pool):
                with pool.Fori(0, TURNS) as i:
                    for g in range(GROUPS):
                        pool.wait_ge(ids, i * GROUPS + g + 1)
                        pool.wait_ge(summed, i * GROUPS + g + 1)
                        pool.sem_inc(gate, 1)
                        for u in tiles_of(g):
                            pool.indirect_dma_start(
                                out=b.ring[:, u, 0:D], out_offset=None, in_=source,
                                in_offset=bass.IndirectOffsetOnAxis(ap=b.ids[:, u:u + 1], axis=0)
                            ).then_inc(got[g], 16)

            @block.scalar
            def _(act):
                first_ids(act, b, index, ids)
                with act.Fori(0, TURNS) as i:
                    for g in range(GROUPS):
                        act.wait_ge(summed, GROUPS + i * GROUPS + g + 1)
                        act.sem_inc(gate, 1)
                        next_ids(act, b, index, ids, i, g)

        if what != RELATE:
            @block.sync
            def _(sp):
                with sp.Fori(0, TURNS) as i:
                    for h in range(2):
                        half = slice(h * HALF, (h + 1) * HALF)
                        if what == ATTEND:
                            sp.wait_ge(summed, i * GROUPS + 2 * h + 2)
                            sp.dma_start(b.ring[:, half, 0:D],
                                         source[:, bass.ds(i * SLOTS + h * HALF, HALF), :]).then_inc(rows_in[h], 16)
                            sp.dma_start(b.ring[:, half, D:D + 32],
                                         io["ea32"][:, bass.ds(i * SLOTS + h * HALF, HALF), :]).then_inc(
                                             rows_in[h], 16)
                        else:
                            sp.wait_ge(extra, 2 * (2 * i + h) + 2)
                            sp.dma_start(feats16[:, half, :],
                                         io["ea16"][:, bass.ds(i * SLOTS + h * HALF, HALF), :]).then_inc(
                                             rows_in[h], 16)

        @block.tensor
        def _(pe):
            pe.sem_inc(summed, GROUPS)
            pe.wait_ge(zeroed, 1)
            with pe.Fori(0, TURNS) as i:
                for g in range(GROUPS):
                    away = window_gaps(pe, b, i * GROUPS + g)
                    pe.wait_ge(added, i * GROUPS + g + 1)
                    bank = b.psum[0:rows, g % 2, :]
                    pe.matmul(bank, lhsT=zeros[:, 0:rows], rhs=zeros[:, P:P + 512], start=True, stop=False,
                              skip_group_check=True)
                    if index is not None:
                        pe.wait_ge(got[g], 16 * GROUP * (i + 1))
                    if what == ATTEND and g % 2 == 0:
                        pe.wait_ge(rows_in[g // 2], 32 * i + 32)
                    if what == AVERAGE and g % 2 == 0:
                        pe.wait_ge(extra, 4 + 2 * (2 * i + g // 2) + 2)
                    pe.wait_ge(hot, i * GROUPS + g + 1)
                    pe.sem_inc(gate, 1)
                    for v, u in enumerate(tiles_of(g)):
                        place = bank[:, 0:P] if v == 0 else b.psum[0:rows, g % 2, bass.ds(away[v], P)]
                        ins = pe.matmul(place, lhsT=b.ring[:, u, 0:rows], rhs=hots[:, g % 2, v, :],
                                        start=False, stop=(v == GROUP - 1), skip_group_check=True)
                    ins.then_inc(summed, 1)

        def make_hots(dve, i, g):
            dve.wait_ge(summed, GROUPS - 2 + i * GROUPS + g + 1)
            for v, u in enumerate(tiles_of(g)):
                if weight is None:
                    ins = dve.tensor_scalar(hots[:, g % 2, v, :], b.w("iota"), off16[:, u:u + 1], None, ALU.is_equal)
                else:
                    ins = dve.tensor_scalar(hots[:, g % 2, v, :], b.w("iota"), off16[:, u:u + 1],
                                            wt16[:, u:u + 1], ALU.is_equal, ALU.mult)
            ins.then_inc(hot, 1)

        def fetch(dve, i):
            dve.tensor_copy(off16, b.dst_off[:, bass.ds(i * SLOTS, SLOTS)]).then_inc(offs, 1)
            if weight is not None:
                dve.tensor_copy(wt16, weight[:, bass.ds(i * SLOTS, SLOTS)]).then_inc(offs, 1)
            else:
                dve.sem_inc(offs, 1)
            dve.wait_ge(offs, 2 * i + 2)

        def mark_last(dve, i, h):
            half = slice(h * HALF, (h + 1) * HALF)
            dve.wait_ge(rows_in[h], 16 * i + 16)
            dve.wait_ge(summed, i * GROUPS + 2 * h + 2)
            flag = b.is_last[:, bass.ds(i * SLOTS + h * HALF, HALF)].rearrange("p (u o) -> p u o", o=1)
            dve.tensor_tensor(b.ring[:, half, 65:81], feats16[:, half, :],
                              flag.broadcast_to([P, HALF, 16]), ALU.mult).then_inc(extra, 1)
            dve.tensor_copy(b.ring[:, half, 81:82], flag).then_inc(extra, 1)

        @block.vector
        def _(dve):
            dve.memset(zeros, 0.0).then_inc(zeroed, 1)
            dve.sem_inc(added, 2)
            if what == AVERAGE:
                dve.sem_inc(extra, 4)
            dve.memset(b.acc[0:rows, :], 0.0).then_inc(cleared, 1)
            if what != RELATE:
                one = D if what == AVERAGE else 96
                dve.memset(b.ring[:, :, one:one + 1], 1.0).then_inc(cleared, 1)
                dve.wait_ge(cleared, 2)
            else:
                dve.wait_ge(cleared, 1)
            fetch(dve, 0)
            make_hots(dve, 0, 0)
            with dve.Fori(0, TURNS) as i:
                for g in range(GROUPS):
                    if what == AVERAGE and g % 2 == 0:
                        mark_last(dve, i, g // 2)
                    start = dve.value_load(b.window[0:1, bass.ds(i * SLOTS + g * GROUP, 1)], min_val=0, max_val=N)
                    if g + 1 < GROUPS:
                        make_hots(dve, i, g + 1)
                    else:
                        dve.wait_ge(hot, (i + 1) * GROUPS)
                        fetch(dve, i + 1)
                        make_hots(dve, i + 1, 0)
                    dve.wait_ge(summed, GROUPS + i * GROUPS + g + 1)
                    dve.wait_ge(added, 2 + i * GROUPS + g)
                    place = b.acc[0:rows, bass.ds(start, GROUP * P)]
                    dve.tensor_tensor(place, place, b.psum[0:rows, g % 2, :], ALU.add).then_inc(added, 1)


def divide_sums(nc, b, top, under, least, beside, relu, source, target):
    rows = top.shape[0]
    with stage(nc) as ctx:
        made, read, gate, step = sems(nc, ctx, "ds_made", "ds_read", "ds_gate", "ds_step")
        t = b.edge_t[0:D, 0:2 * CW].rearrange("p (u n) -> p u n", u=2)
        block = ctx.enter_context(nc.Block())

        @block.tensor
        def _(pe):
            with pe.Fori(0, CHUNKS // 2) as i:
                for u in range(2):
                    at = bass.ds((2 * i + u) * CW, CW)
                    pe.wait_ge(read, 2 * i + u + 1)
                    pe.sem_inc(gate, 1)
                    pe.matmul(b.psum[0:D, 4 * u, 0:CW], lhsT=top, rhs=b.acc[0:rows, at], start=True, stop=True)
                    pe.matmul(b.psum[0:D, 4 * u + 1, 0:CW], lhsT=under, rhs=b.acc[0:rows, at],
                              start=True, stop=True)
                    for k, (w, array, r) in enumerate(beside):
                        ins = pe.matmul(b.psum[0:D, 4 * u + 2, 0:CW], lhsT=w, rhs=array[0:r, at],
                                        start=(k == 0), stop=(k == len(beside) - 1))
                    ins.then_inc(made, 1)

        @block.vector
        def _(dve):
            dve.sem_inc(read, 2)
            with dve.Fori(0, CHUNKS // 2) as i:
                for u in range(2):
                    n = 2 * i + u
                    dve.wait_ge(made, n + 1)
                    dve.tensor_scalar(t[:, u, :], b.psum[0:D, 4 * u + 1, 0:CW], least, None,
                                      ALU.max).then_inc(step, 1)
                    dve.wait_ge(step, 4 * n + 1)
                    dve.reciprocal(t[:, u, :], t[:, u, :]).then_inc(step, 1)
                    dve.wait_ge(step, 4 * n + 2)
                    dve.tensor_tensor(t[:, u, :], b.psum[0:D, 4 * u, 0:CW], t[:, u, :], ALU.mult).then_inc(step, 1)
                    dve.wait_ge(step, 4 * n + 3)
                    dve.tensor_tensor(t[:, u, :], t[:, u, :], b.psum[0:D, 4 * u + 2, 0:CW],
                                      ALU.add).then_inc(step, 1)
                    dve.wait_ge(step, 4 * n + 4)
                    dve.tensor_scalar(target[0:D, bass.ds(n * CW, CW)], t[:, u, :], 0.0 if relu else -BIG, None,
                                      ALU.max).then_inc(read, 1)


def add_root(nc, b, root, features):
    with stage(nc) as ctx:
        made, read, gate, step = sems(nc, ctx, "ar_made", "ar_read", "ar_gate", "ar_step")
        t = b.edge_t[0:D, 0:2 * CW].rearrange("p (u n) -> p u n", u=2)
        block = ctx.enter_context(nc.Block())

        @block.tensor
        def _(pe):
            with pe.Fori(0, CHUNKS // 2) as i:
                for u in range(2):
                    pe.wait_ge(read, 2 * i + u + 1)
                    pe.sem_inc(gate, 1)
                    pe.matmul(b.psum[0:D, u, 0:CW], lhsT=root, rhs=features[0:D + 1, bass.ds((2 * i + u) * CW, CW)],
                              start=True, stop=True).then_inc(made, 1)

        @block.vector
        def _(dve):
            dve.sem_inc(read, 2)
            with dve.Fori(0, CHUNKS // 2) as i:
                for u in range(2):
                    n = 2 * i + u
                    dve.wait_ge(made, n + 1)
                    dve.tensor_tensor(t[:, u, :], b.acc[0:D, bass.ds(n * CW, CW)], b.psum[0:D, u, 0:CW],
                                      ALU.add).then_inc(step, 1)
                    dve.wait_ge(step, n + 1)
                    dve.tensor_scalar(features[0:D, bass.ds(n * CW, CW)], t[:, u, :], 0.0, None,
                                      ALU.max).then_inc(read, 1)


def add_rows(nc, b, parts, relu):
    with stage(nc) as ctx:
        staged, made, added, gate = sems(nc, ctx, "ad_staged", "ad_made", "ad_added", "ad_gate")
        held = b.edge_t[:, 0:2 * NODE_SLOTS * P].rearrange("p (k u n) -> p k u n", k=2, u=NODE_SLOTS)
        turns = NT // NODE_SLOTS
        m = len(parts)
        block = ctx.enter_context(nc.Block())

        @block.scalar
        def _(act):
            with act.Fori(0, turns) as i:
                for u in range(NODE_SLOTS):
                    n = i * NODE_SLOTS + u
                    act.wait_ge(made, n + 1)
                    act.sem_inc(gate, 1)
                    for k, (array, rows, _) in enumerate(parts):
                        act.copy(held[0:rows, k, u, :], array[0:rows, bass.ds(n * P, P)]).then_inc(staged, 1)

        @block.tensor
        def _(pe):
            pe.sem_inc(made, NODE_SLOTS)
            with pe.Fori(0, turns) as i:
                for u in range(NODE_SLOTS):
                    n = i * NODE_SLOTS + u
                    pe.wait_ge(staged, m * n + m)
                    pe.wait_ge(added, n + 1)
                    for k, (_, rows, w) in enumerate(parts):
                        ins = pe.matmul(b.psum[:, u, 0:D], lhsT=held[0:rows, k, u, :], rhs=w,
                                        start=(k == 0), stop=(k == m - 1))
                    ins.then_inc(made, 1)

        @block.vector
        def _(dve):
            dve.sem_inc(added, NODE_SLOTS)
            with dve.Fori(0, turns) as i:
                for u in range(NODE_SLOTS):
                    n = i * NODE_SLOTS + u
                    dve.wait_ge(made, NODE_SLOTS + n + 1)
                    xt = b.x[:, bass.ds(n * D, D)]
                    dve.scalar_tensor_tensor(out=xt, in0=b.psum[:, u, 0:D], scalar=0.0 if relu else -BIG,
                                             in1=xt, op0=ALU.max, op1=ALU.add).then_inc(added, 1)


def normalize(dve, link, b, rows, width, spare, stats, act_wait):
    mean, var = stats[:, 0:NT], stats[:, NT:2 * NT]

    def wide(column):
        return column.rearrange("p (t o) -> p t o", o=1).broadcast_to([P, NT, width])

    link(dve.tensor_reduce(mean, rows, AX.X, ALU.add))
    link(dve.tensor_scalar(mean, mean, 1.0 / width, None, ALU.mult))
    link(dve.tensor_tensor(rows, rows, wide(mean), ALU.subtract))
    link(dve.tensor_tensor(spare, rows, rows, ALU.mult))
    link(dve.tensor_reduce(var, spare, AX.X, ALU.add))
    link(dve.tensor_scalar(var, var, 1.0 / width, EPS, ALU.mult, ALU.add))
    act_wait(var)
    link(dve.reciprocal(var, var))
    link(dve.tensor_tensor(rows, rows, wide(var), ALU.mult))


def turn_nodes(nc, b, rows, width, turned_to, ones):
    with stage(nc) as ctx:
        staged, made, copied, gate = sems(nc, ctx, "tn_staged", "tn_made", "tn_copied", "tn_gate")
        held = b.edge_t[:, 0:NODE_SLOTS * P].rearrange("p (u n) -> p u n", u=NODE_SLOTS)
        turns = NT // NODE_SLOTS
        block = ctx.enter_context(nc.Block())

        @block.scalar
        def _(act):
            with act.Fori(0, turns) as i:
                for u in range(NODE_SLOTS):
                    n = i * NODE_SLOTS + u
                    act.wait_ge(made, n + 1)
                    act.sem_inc(gate, 1)
                    act.copy(held[:, u, 0:width], rows[:, bass.ds(n * width, width)]).then_inc(staged, 1)

        @block.tensor
        def _(pe):
            pe.sem_inc(made, NODE_SLOTS)
            with pe.Fori(0, turns) as i:
                for u in range(NODE_SLOTS):
                    n = i * NODE_SLOTS + u
                    pe.wait_ge(staged, n + 1)
                    pe.wait_ge(copied, n + 1)
                    pe.sem_inc(gate, 1)
                    pe.transpose(b.psum[0:width, u, 0:P], held[:, u, 0:width], b.ident()).then_inc(made, 1)

        @block.vector
        def _(dve):
            dve.sem_inc(copied, NODE_SLOTS)
            with dve.Fori(0, turns) as i:
                for u in range(NODE_SLOTS):
                    n = i * NODE_SLOTS + u
                    dve.wait_ge(made, NODE_SLOTS + n + 1)
                    dve.sem_inc(gate, 1)
                    dve.tensor_copy(turned_to[0:width, bass.ds(n * P, P)],
                                    b.psum[0:width, u, 0:P]).then_inc(copied, 1)


def norm_x(nc, b, out):
    with stage(nc) as ctx:
        chain, asked, rooted, stored = sems(nc, ctx, "nx_chain", "nx_asked", "nx_rooted", "nx_stored")
        x = b.x[:, :].rearrange("p (t d) -> p t d", d=D)
        spare = b.acc[:, 0:NT * D].rearrange("p (t d) -> p t d", d=D)
        stats = b.hot[:, 0, :]
        var = stats[:, NT:2 * NT]
        full = out.shape[0] // P
        block = ctx.enter_context(nc.Block())

        @block.vector
        def _(dve):
            done = [0]

            def link(ins):
                done[0] += 1
                ins.then_inc(chain, 1)
                dve.wait_ge(chain, done[0])

            def act_wait(_):
                dve.sem_inc(asked, 1)
                dve.wait_ge(rooted, 1)

            normalize(dve, link, b, x, D, spare, stats, act_wait)
            dve.sem_inc(asked, 1)

        @block.scalar
        def _(act):
            act.wait_ge(asked, 1)
            act.sqrt(var, var).then_inc(rooted, 1)

        @block.sync
        def _(sp):
            sp.wait_ge(asked, 2)
            sp.dma_start(out[0:full * P, :].rearrange("(t p) d -> p t d", p=P), x[:, 0:full, :]).then_inc(stored, 16)
            rest = out.shape[0] - full * P
            if rest:
                sp.dma_start(out[full * P:, :], x[0:rest, full, :]).then_inc(stored, 16)
            sp.wait_ge(stored, 32 if rest else 16)


def split_x(nc, b, out):
    with stage(nc) as ctx:
        chain, split, stored = sems(nc, ctx, "sx_chain", "sx_split", "sx_stored")
        x = b.x[:, :].rearrange("p (t d) -> p t d", d=D)
        rest = b.acc[:, 0:NT * D].rearrange("p (t d) -> p t d", d=D)
        parts = b.query[:, 0:NT * PARTS * D // 2].bitcast(BF16).rearrange("p (t k d) -> p t k d", t=NT, k=PARTS)
        block = ctx.enter_context(nc.Block())

        @block.vector
        def _(dve):
            done = [0]

            def link(ins):
                done[0] += 1
                ins.then_inc(chain, 1)
                dve.wait_ge(chain, done[0])

            link(dve.tensor_copy(parts[:, :, 0, :], x))
            link(dve.tensor_tensor(rest, x, parts[:, :, 0, :], ALU.subtract))
            link(dve.tensor_copy(parts[:, :, 1, :], rest))
            link(dve.tensor_tensor(rest, rest, parts[:, :, 1, :], ALU.subtract))
            dve.tensor_copy(parts[:, :, 2, :], rest).then_inc(split, 1)

        @block.sync
        def _(sp):
            sp.wait_ge(split, 1)
            sp.dma_start(out.rearrange("(t p) w -> p t w", p=P), parts.rearrange("p t k d -> p t (k d)")
                         ).then_inc(stored, 16)
            sp.wait_ge(stored, 16)


def scatter_messages(nc, b, io, table, rows_dram, partial):
    with stage(nc) as ctx:
        broadcast, spread, apart, hot, moved, joined, ordered, offs = sems(
            nc, ctx, "me_broadcast", "me_spread", "me_apart", "me_hot", "me_moved", "me_joined", "me_ordered", "me_offs")
        message, relued, copied, zeroed, cleared, freed = sems(
            nc, ctx, "me_message", "me_relued", "me_copied", "me_zeroed", "me_cleared", "me_freed")
        key_rows = sems(nc, ctx, "me_key_rows0", "me_key_rows1")
        feats = sems(nc, ctx, "me_feats0", "me_feats1")
        windows = sems(nc, ctx, *[f"me_windows{g}" for g in range(GROUPS)])
        sent = sems(nc, ctx, *[f"me_sent{k}" for k in range(COPIES)])
        big = b.query
        o = [0]

        def take(n):
            o[0] += n
            return big[:, o[0] - n:o[0]]

        win = take(SLOTS * PARTS * D // 2).bitcast(BF16).rearrange("p (u k d) -> p u k d", u=SLOTS, k=PARTS)
        feat = take(SLOTS * D).rearrange("p (u d) -> p u d", u=SLOTS)
        keys = take(ROW)[0:2, :].bitcast(BF16).rearrange("p (u w) -> p u w", u=SLOTS)
        apart_hot = b.hot[:, 0:2, :].bitcast(BF16).rearrange("p a (v e) -> p (a v) e", e=P)
        out_hot = b.hot[:, 2:4, :].bitcast(BF16).rearrange("p a (v e) -> p (a v) e", e=P)
        same, before = (b.edge_t[:, k * 2 * GROUP * P:(k + 1) * 2 * GROUP * P].rearrange(
            "p (g u n) -> p g u n", g=2, u=GROUP) for k in range(2))
        msg = take(2 * GROUP * D).rearrange("p (g u d) -> p g u d", g=2, u=GROUP)
        total = take(GROUPS * GROUP * D).rearrange("p (g u d) -> p g u d", g=GROUPS, u=GROUP)
        src_all, row_all, spare_all = b.rel_wt, b.node_b[:, 0:T + SLOTS], b.score
        high_all = b.node_b[:, T + SLOTS:2 * (T + SLOTS)]
        src_f = take(SLOTS)
        row_f = take(SLOTS)
        spare = take(SLOTS)
        earlier = take(SLOTS)
        moves = take(SLOTS)
        ids = b.ids
        of_src, of_dst = (b.psum[:, 2 * w:2 * w + 2, :].rearrange("p g (v e) -> p g v e", v=GROUP) for w in range(2))
        block = ctx.enter_context(nc.Block())

        @block.sync
        def _(sp):
            with sp.Fori(0, TURNS) as i:
                for g in range(GROUPS):
                    starts = window_starts(sp, b, i * GROUPS + g)
                    sp.wait_ge(message, i * GROUPS + g + 1)
                    for v, u in enumerate(tiles_of(g)):
                        sp.dma_start(win[:, u, :, :].rearrange("p k d -> p (k d)"),
                                     table[bass.ds(starts[v], P), :]).then_inc(windows[g], 16)

        def load_keys(act, i, h):
            half = slice(h * HALF, (h + 1) * HALF)
            act.dma_start(keys[:, half, :].rearrange("o u w -> o (u w)"),
                          rows_dram[:, bass.ds((i * SLOTS + h * HALF) * 2 * P, HALF * 2 * P)]
                          ).then_inc(key_rows[h], 16)

        def load_feats(act, i, h):
            act.dma_start(feat[:, h * HALF:(h + 1) * HALF, :],
                          io["ea64"][:, bass.ds(i * SLOTS + h * HALF, HALF), :]).then_inc(feats[h], 16)

        def bcast(pe, i, g):
            if g % 2 == 0:
                pe.wait_ge(key_rows[g // 2], 16 * i + 16)
            pe.wait_ge(spread, i * GROUPS + g + 1)
            pe.wait_ge(hot, i * GROUPS + g + 1)
            for w, to in enumerate((of_src, of_dst)):
                ins = pe.matmul(to[:, g % 2, :, :], lhsT=b.bcast_w[0:2, :],
                                rhs=keys[0:2, g * GROUP:(g + 1) * GROUP, w * P:(w + 1) * P], start=True, stop=True)
            ins.then_inc(broadcast, 1)

        def pick_rows(pe, i, g):
            pe.wait_ge(windows[g], 16 * GROUP * (i + 1))
            pe.wait_ge(hot, 2 + i * GROUPS + g + 1)
            pe.wait_ge(message, GROUPS - 2 + i * GROUPS + g + 1)
            for v, u in enumerate(tiles_of(g)):
                for k in range(PARTS):
                    ins = pe.matmul(b.psum[:, 4 + g % 2, v * D:(v + 1) * D], lhsT=out_hot[:, v, :],
                                    rhs=win[:, u, k, :], start=(k == 0), stop=(k == PARTS - 1))
            ins.then_inc(moved, 1)

        def join(pe, i, g):
            pe.wait_ge(relued, i * GROUPS + g + 1)
            pe.wait_ge(copied, i * GROUPS + g + 1)
            for v in range(GROUP):
                ins = pe.matmul(b.psum[:, 6 + g % 2, v * D:(v + 1) * D], lhsT=same[:, g % 2, v, :],
                                rhs=msg[:, g % 2, v, :], start=True, stop=True)
            ins.then_inc(joined, 1)

        def pe_turn(pe, i, last, first=False):
            for g in range(GROUPS):
                if g + 1 < GROUPS:
                    bcast(pe, i, g + 1)
                elif not last:
                    bcast(pe, i + 1, 0)
                pick_rows(pe, i, g)
                if g >= 1:
                    join(pe, i, g - 1)
                elif not first:
                    join(pe, i - 1, GROUPS - 1)

        @block.tensor
        def _(pe):
            pe.sem_inc(moved, 1)
            pe.sem_inc(joined, 2)
            bcast(pe, 0, 0)
            pe_turn(pe, 0, False, True)
            with pe.Fori(1, TURNS - 1) as i:
                pe_turn(pe, i, False)
            pe_turn(pe, TURNS - 1, True)
            join(pe, TURNS - 1, GROUPS - 1)

        @block.scalar
        def _(act):
            act.sem_inc(copied, 2)
            act.sem_inc(hot, 2)

            def make_hots(i, g):
                act.wait_ge(broadcast, i * GROUPS + g + 1)
                act.wait_ge(moved, 1 + i * GROUPS + g)
                act.activation(apart_hot, of_dst[:, g % 2, :, :], ACT.Abs, bias=b.w("minus_lane")).then_inc(
                    apart, 1)
                act.wait_ge(apart, i * GROUPS + g + 1)
                act.activation(out_hot, apart_hot, ACT.Relu, bias=b.w("one"),
                               scale=-1.0).then_inc(hot, 1)

            def relu(i, g):
                act.wait_ge(message, GROUPS + i * GROUPS + g + 1)
                act.activation(msg[:, g % 2, :, :], msg[:, g % 2, :, :], ACT.Relu).then_inc(relued, 1)

            def copy(i, g):
                act.wait_ge(joined, 2 + i * GROUPS + g + 1)
                act.wait_ge(freed, i * SLOTS + g * GROUP + GROUP)
                act.copy(total[:, g, :, :], b.psum[:, 6 + g % 2, 0:GROUP * D].rearrange(
                    "p (u d) -> p u d", u=GROUP)).then_inc(copied, 1)

            def act_turn(i, first, last):
                for g in range(GROUPS):
                    relu(i, g)
                    if g % 2 == 1 and not last:
                        load_feats(act, i + 1, g // 2)
                    if g + 1 < GROUPS:
                        make_hots(i, g + 1)
                        if g % 2 == 0 and not last:
                            load_keys(act, i + 1, g // 2)
                    elif not last:
                        make_hots(i + 1, 0)
                    if g >= 1:
                        copy(i, g - 1)
                    elif not first:
                        copy(i - 1, GROUPS - 1)

            for h in range(2):
                load_keys(act, 0, h)
                load_feats(act, 0, h)
            make_hots(0, 0)
            act_turn(0, True, False)
            with act.Fori(1, TURNS - 1) as i:
                act_turn(i, False, False)
            act_turn(TURNS - 1, False, True)
            copy(TURNS - 1, GROUPS - 1)

        @block.vector
        def _(dve):
            dve.memset(b.acc[:, 0:NT * D], 0.0).then_inc(zeroed, 1)
            dve.sem_inc(spread, 2)
            dve.sem_inc(message, GROUPS)

            def add_feats(i, g):
                dve.wait_ge(moved, 1 + i * GROUPS + g + 1)
                if g % 2 == 0:
                    dve.wait_ge(feats[g // 2], 16 * i + 16)
                dve.tensor_tensor(msg[:, g % 2, :, :].rearrange("p u d -> p (u d)"),
                                  b.psum[:, 4 + g % 2, 0:GROUP * D],
                                  feat[:, g * GROUP:(g + 1) * GROUP, :].rearrange("p u d -> p (u d)"),
                                  ALU.add).then_inc(message, 1)

            def fetch(i):
                dve.tensor_copy(src_f, src_all[:, bass.ds(i * SLOTS, SLOTS)]).then_inc(offs, 1)
                dve.tensor_copy(row_f, row_all[:, bass.ds(i * SLOTS, SLOTS)]).then_inc(offs, 1)
                dve.tensor_copy(spare, spare_all[:, bass.ds(i * SLOTS, SLOTS)]).then_inc(offs, 1)

            high_i = high_all.bitcast(I32)
            dve.tensor_scalar(high_i, b.src_ids[:, :], 7, None, ALU.logical_shift_right).then_inc(offs, 1)
            dve.tensor_copy(src_all[:, :], b.src_ids[:, :]).then_inc(offs, 1)
            dve.wait_ge(offs, 2)
            dve.tensor_scalar(row_all, src_all[:, :], float(NT), None, ALU.mult).then_inc(offs, 1)
            dve.wait_ge(offs, 3)
            dve.scalar_tensor_tensor(out=row_all, in0=high_i, scalar=float(1 - P * NT), in1=row_all,
                                     op0=ALU.mult, op1=ALU.add).then_inc(offs, 1)
            dve.wait_ge(offs, 4)
            dve.tensor_scalar(spare_all[:, :], row_all, -1.0, b.w("trash"), ALU.mult, ALU.add).then_inc(offs, 1)
            dve.wait_ge(offs, 5)
            with dve.Fori(0, TURNS) as i:
                fetch(i)
                dve.wait_ge(offs, 5 + 3 * i + 3)
                for g in range(GROUPS):
                    n = i * GROUPS + g
                    dve.wait_ge(broadcast, n + 1)
                    dve.wait_ge(joined, n + 1)
                    dve.tensor_tensor(same[:, g % 2, :, :], of_src[:, g % 2, :, :],
                                      src_f[:, g * GROUP:(g + 1) * GROUP].rearrange("p (u o) -> p u o", o=1)
                                      .broadcast_to([P, GROUP, P]), ALU.is_equal)
                    for v, u in enumerate(tiles_of(g)):
                        ins = dve.scalar_tensor_tensor(
                            out=before[:, g % 2, v, :], in0=of_src[:, g % 2, v, :], scalar=src_f[:, u:u + 1],
                            in1=b.w("below"), op0=ALU.is_equal, op1=ALU.mult, accum_out=earlier[:, u:u + 1])
                    ins.then_inc(spread, 1)
                    add_feats(i, g)
                    mine = slice(g * GROUP, (g + 1) * GROUP)
                    dve.wait_ge(spread, 2 + n + 1)
                    dve.scalar_tensor_tensor(out=moves[:, mine], in0=earlier[:, mine], scalar=0.0, in1=spare[:, mine],
                                             op0=ALU.is_gt, op1=ALU.mult).then_inc(ordered, 1)
                    dve.wait_ge(ordered, 2 * n + 1)
                    dve.wait_ge(freed, i * SLOTS + g * GROUP + GROUP)
                    dve.tensor_tensor(ids[:, mine], moves[:, mine], row_f[:, mine], ALU.add).then_inc(ordered, 1)
                dve.wait_ge(ordered, 2 * GROUPS * (i + 1))

        @block.gpsimd
        def _(pool):
            pool.wait_ge(zeroed, 1)
            for c in range(COPIES):
                pool.dma_start(partial[c].rearrange("(p t) d -> p (t d)", p=P),
                               b.acc[:, 0:NT * D]).then_inc(cleared, 16)
            pool.wait_ge(cleared, 16 * COPIES)
            pool.sem_inc(freed, SLOTS - COPIES)

            def pool_turn(i, first):
                for g in range(GROUPS):
                    pool.wait_ge(copied, 2 + i * GROUPS + g + 1)
                    pool.wait_ge(ordered, 2 * (i * GROUPS + g) + 2)
                    for v, u in enumerate(tiles_of(g)):
                        if not first or u >= COPIES:
                            pool.wait_ge(sent[u % COPIES], 16 * (i * (SLOTS // COPIES) + u // COPIES))
                        pool.sem_inc(freed, 1)
                        pool.indirect_dma_start(
                            out=partial[u % COPIES],
                            out_offset=bass.IndirectOffsetOnAxis(ap=ids[:, u:u + 1], axis=0),
                            in_=total[:, g, v, :], in_offset=None,
                            compute_op=ALU.add).then_inc(sent[u % COPIES], 16)

            pool_turn(0, True)
            with pool.Fori(1, TURNS) as i:
                pool_turn(i, False)
            for c in range(COPIES):
                pool.wait_ge(sent[c], 16 * (SLOTS // COPIES) * TURNS)


def gather_partials(nc, b, partial):
    with stage(nc) as ctx:
        loaded, chain = sems(nc, ctx, "gp_loaded", "gp_chain")
        total = b.acc[:, 0:NT * D]
        parts = [b.query[:, 0:NT * D], b.query[:, NT * D:2 * NT * D],
                 b.node_b[:, 0:NT * D], b.node_b[:, NT * D:2 * NT * D]]
        block = ctx.enter_context(nc.Block())

        @block.sync
        def _(sp):
            for k in range(COPIES):
                sp.dma_start(parts[k], partial[k].rearrange("(p t) d -> p (t d)", p=P)).then_inc(loaded, 16)
            sp.wait_ge(loaded, 16 * COPIES)

        @block.vector
        def _(dve):
            done = [0]

            def link(ins):
                done[0] += 1
                ins.then_inc(chain, 1)
                dve.wait_ge(chain, done[0])

            dve.wait_ge(loaded, 16 * COPIES)
            link(dve.tensor_tensor(parts[0], parts[0], parts[1], ALU.add))
            link(dve.tensor_tensor(parts[2], parts[2], parts[3], ALU.add))
            link(dve.tensor_tensor(parts[0], parts[0], parts[2], ALU.add))
            link(dve.scalar_tensor_tensor(out=total, in0=b.x[:, :], scalar=b.w("eps"), in1=b.x[:, :],
                                          op0=ALU.mult, op1=ALU.add))
            link(dve.tensor_tensor(total, total, parts[0], ALU.add))


def widen(nc, b):
    with stage(nc) as ctx:
        staged, made, copied, gate = sems(nc, ctx, "wi_staged", "wi_made", "wi_copied", "wi_gate")
        held = b.edge_t[:, 0:NODE_SLOTS * P].rearrange("p (u n) -> p u n", u=NODE_SLOTS)
        turns = NT // NODE_SLOTS
        block = ctx.enter_context(nc.Block())

        @block.scalar
        def _(act):
            with act.Fori(0, turns) as i:
                for u in range(NODE_SLOTS):
                    n = i * NODE_SLOTS + u
                    act.wait_ge(made, n + 1)
                    act.sem_inc(gate, 1)
                    act.copy(held[0:D + 1, u, :], b.node_b[0:D + 1, bass.ds(n * P, P)]).then_inc(staged, 1)

        @block.tensor
        def _(pe):
            pe.sem_inc(made, NODE_SLOTS)
            with pe.Fori(0, turns) as i:
                for u in range(NODE_SLOTS):
                    n = i * NODE_SLOTS + u
                    pe.wait_ge(staged, n + 1)
                    pe.wait_ge(copied, n + 1)
                    pe.matmul(b.psum[:, u, 0:P], lhsT=held[0:D + 1, u, :], rhs=b.w("w1", D + 1),
                              start=True, stop=True).then_inc(made, 1)

        @block.vector
        def _(dve):
            dve.sem_inc(copied, NODE_SLOTS)
            with dve.Fori(0, turns) as i:
                for u in range(NODE_SLOTS):
                    n = i * NODE_SLOTS + u
                    dve.wait_ge(made, NODE_SLOTS + n + 1)
                    dve.sem_inc(gate, 1)
                    dve.tensor_copy(b.query[:, bass.ds(n * P, P)], b.psum[:, u, 0:P]).then_inc(copied, 1)


def norm_wide(nc, b):
    with stage(nc) as ctx:
        chain, asked, rooted = sems(nc, ctx, "nw_chain", "nw_asked", "nw_rooted")
        z = b.query[:, 0:NT * P].rearrange("p (t d) -> p t d", d=P)
        spare = b.acc[:, 0:NT * P].rearrange("p (t d) -> p t d", d=P)
        stats = b.hot[:, 0, :]
        var = stats[:, NT:2 * NT]
        block = ctx.enter_context(nc.Block())

        def each_node(w):
            return w.rearrange("p (o d) -> p o d", o=1).broadcast_to([P, NT, P])

        @block.vector
        def _(dve):
            done = [0]

            def link(ins):
                done[0] += 1
                ins.then_inc(chain, 1)
                dve.wait_ge(chain, done[0])

            def act_wait(_):
                dve.sem_inc(asked, 1)
                dve.wait_ge(rooted, 1)

            normalize(dve, link, b, z, P, spare, stats, act_wait)
            link(dve.tensor_tensor(z, z, each_node(b.w("ln_g")), ALU.mult))
            link(dve.tensor_tensor(z, z, each_node(b.w("ln_b")), ALU.add))
            link(dve.tensor_scalar(z, z, 0.0, None, ALU.max))

        @block.scalar
        def _(act):
            act.wait_ge(asked, 1)
            act.sqrt(var, var).then_inc(rooted, 1)


def program(nc, io, out):
    def dram(name, shape, dt=F32):
        return nc.dram_tensor(name, shape, dt, kind="Internal").ap()

    kv_table = dram("kv_table", (NROWS, 2 * D))
    values = dram("values", (P, T, D))
    rel_table = dram("rel_table", (NROWS, RELS * D))
    x_table = dram("x_table", (NROWS, D))
    x_parts = dram("x_parts", (NROWS, PARTS * D), BF16)
    rows_dram = dram("rows_dram", (2, T * 2 * P), BF16)
    partial = [dram(f"partial{k}", (NROWS, D)) for k in range(COPIES)]

    with ExitStack() as ctx:
        b = Buffers(nc, ctx)
        load_inputs(nc, b, io)
        edge_tables(nc, b, io, rows_dram)

        for n, source, target in ((1, b.node_a, b.node_b), (2, b.node_b, b.node_a)):
            node_rows(nc, b, source, b.w(f"kv{n}", 65), 2 * D, 65, kv_table)
            node_query(nc, b, source, b.w(f"qq{n}", 65))
            edge_scores(nc, b, io, kv_table, values)
            softmax_parts(nc, b, io)
            sum_edges(nc, b, io, ATTEND, values)
            divide_sums(nc, b, b.w(f"comb{n}", 97), b.w("pick96", 97), 1e-30,
                        [(b.w(f"self{n}", 65), source, 65)], True, source, target)
        add_rows(nc, b, [(b.node_b, 64, b.w("skip_h1", 64)), (b.node_a, 65, b.w("skip_h2", 65))], True)
        norm_x(nc, b, x_table)
        turn_nodes(nc, b, b.x, D, b.node_a, True)

        for l in range(LAYERS):
            node_rows(nc, b, b.node_a, b.rel_w[:, l * RELS * D:(l + 1) * RELS * D], RELS * D, 64, rel_table)
            sum_edges(nc, b, io, RELATE, rel_table.rearrange("n (r d) -> (n r) d", d=D))
            if l < LAYERS - 1:
                add_root(nc, b, b.w(f"root{l}", 65), b.node_a)
        add_rows(nc, b, [(b.acc, 64, b.ident(64)), (b.node_a, 65, b.w("root2", 65))], False)
        norm_x(nc, b, x_table)

        split_x(nc, b, x_parts)
        scatter_messages(nc, b, io, x_parts, rows_dram, partial)
        gather_partials(nc, b, partial)
        restore_one(nc, b)
        turn_nodes(nc, b, b.acc, D, b.node_b, False)
        widen(nc, b)
        norm_wide(nc, b)
        turn_nodes(nc, b, b.query, P, b.acc, False)
        add_rows(nc, b, [(b.acc, P, b.w("w2", P)), (b.node_b, 65, b.w("b2", 65))], False)
        norm_x(nc, b, x_table)
        turn_nodes(nc, b, b.x, D, b.node_a, True)

        sum_edges(nc, b, io, AVERAGE, x_table)
        divide_sums(nc, b, b.w("w_l", 82), b.w("pick64", 82), 1.0,
                    [(b.w("w_r", 65), b.node_a, 65), (b.w("w_e", 82), b.acc, 82)], False, b.node_a, b.node_b)
        add_rows(nc, b, [(b.node_b, 64, b.ident(64))], False)
        norm_x(nc, b, out)


def restore_one(nc, b):
    with stage(nc) as ctx:
        (set_,) = sems(nc, ctx, "ro_set")
        block = ctx.enter_context(nc.Block())

        @block.vector
        def _(dve):
            dve.memset(b.node_b[64:65, :], 1.0).then_inc(set_, 1)


def kernel(**inputs):
    import numpy as np
    import concourse.bacc as _bacc
    from concourse import mybir as _mybir
    from concourse.bass_utils import run_bass_kernel_spmd as _run

    a = {k: np.asarray(v) for k, v in inputs.items()}
    f4, i4 = np.float32, np.int32

    def lane(values, fill, extra=0):
        out = np.full(((T + extra) * P,) + values.shape[1:], fill, values.dtype)
        out[:E] = values
        out = out.reshape((T + extra, P) + values.shape[1:])
        return np.ascontiguousarray(np.swapaxes(out, 0, 1))

    def turn(values, fill):
        out = np.full(T * P, fill, values.dtype)
        out[:E] = values
        return out

    weights = np.zeros((P, WTOTAL), f4)

    def put(name, block, row=0, col=0):
        at = WCOL[name][0] + col
        block = np.atleast_2d(block)
        weights[row:row + block.shape[0], at:at + block.shape[1]] = block

    for n in (1, 2):
        w = {k: a[f"L0_gnn_{k[0]}{n}{k[1:]}"] for k in ("q_w", "q_b", "k_w", "k_b", "v_w", "v_b", "e_w", "s_w", "s_b")}
        put(f"kv{n}", w["k_w"])
        put(f"kv{n}", w["v_w"], 0, D)
        put(f"kv{n}", w["k_b"], 64)
        put(f"kv{n}", w["v_b"], 64, D)
        put(f"qq{n}", w["q_w"])
        put(f"qq{n}", w["q_b"], 64)
        put(f"q{n}_t", w["q_w"].T)
        put(f"q{n}_t", w["q_b"][:, None], 0, 64)
        put(f"e{n}_t", w["e_w"].T)
        put(f"comb{n}", np.eye(D, dtype=f4))
        put(f"comb{n}", w["e_w"], 64)
        put(f"self{n}", w["s_w"])
        put(f"self{n}", w["s_b"], 64)
    put("skip_h1", a["L0_gnn_skip_w"][:D])
    put("skip_h2", a["L0_gnn_skip_w"][D:])
    put("skip_h2", a["L0_gnn_skip_b"], 64)
    for l in range(LAYERS):
        put(f"root{l}", a["L1_gnn_root"][l])
        put(f"root{l}", a["L1_gnn_bias"][l], 64)
    put("w1", a["L2_gnn_W1"])
    put("w1", a["L2_gnn_b1"], 64)
    put("w2", a["L2_gnn_W2"])
    put("b2", a["L2_gnn_b2"], 64)
    put("ln_g", np.broadcast_to(a["L2_gnn_ln_g"], (P, P)))
    put("ln_b", np.broadcast_to(a["L2_gnn_ln_b"], (P, P)))
    put("eps", np.broadcast_to(a["L2_gnn_eps"], (P, 1)))
    put("w_l", a["L3_gnn_W_l"])
    put("w_r", a["L3_gnn_W_r"])
    put("w_r", a["L3_gnn_b_l"], 64)
    put("w_e", a["L3_gnn_W_e"], 65)
    put("w_e", a["L3_gnn_b_e"], 81)
    lanes = np.arange(P, dtype=f4)
    put("pick96", np.ones((1, D), f4), 96)
    put("pick64", np.ones((1, D), f4), 64)
    put("ident", np.eye(P, dtype=f4))
    put("iota", np.broadcast_to(lanes, (P, P)))
    put("below", np.tril(np.ones((P, P), f4), -1))
    put("minus_lane", -lanes[:, None])
    put("one", np.ones((P, 1), f4))
    spare = np.arange(N + 1, N + 1 + P)
    put("trash", (spare % P * NT + spare // P).astype(f4)[:, None])

    x = a["x"]
    x_pad = np.zeros((NROWS, D), f4)
    x_pad[:N] = x
    x_t = np.zeros((D + 1, NCOLS), f4)
    x_t[:D, :N] = x.T
    x_t[D] = 1.0
    dst = turn(a["dst"], N)
    ext = np.concatenate([np.full(1, -1, i4), dst, np.full(1, -1, i4)])
    dst_turn = np.stack([ext[i * ROW:i * ROW + ROW + 2] for i in range(TURNS)])
    ea32_t = np.zeros((32, T * P), f4)
    ea32_t[:, :E] = a["edge_attr_32"].T

    arrays = {
        "weights": weights,
        "basis": np.ascontiguousarray(a["L1_gnn_basis"].transpose(2, 0, 1, 3).reshape(D, -1)),
        "comp": np.ascontiguousarray(np.broadcast_to(a["L1_gnn_comp"].reshape(1, -1), (D, LAYERS * RELS * BASES))),
        "x_t": x_t,
        "x_rows": np.ascontiguousarray(x_pad.reshape(NT, P, D).transpose(1, 0, 2).reshape(P, NT * D)),
        "src_lane": lane(a["src"], N, SLOTS),
        "type_lane": lane(a["edge_type_8"], 0, SLOTS),
        "window": np.ascontiguousarray(dst.reshape(T, P)[:, 0].reshape(1, T)),
        "dst_turn": dst_turn,
        "type_turn": turn(a["edge_type_8"], 0).reshape(TURNS, ROW),
        "src_turn": turn(a["src"], N).reshape(TURNS, ROW),
        "ea32_t": ea32_t,
        "ea32": lane(a["edge_attr_32"], 0),
        "ea16": lane(a["edge_attr_16"], 0),
        "ea64": lane(a["edge_attr_64"], 0),
    }
    nc = _bacc.Bacc("TRN2", target_bir_lowering=False, num_devices=1)
    io = {k: nc.dram_tensor(f"in_{k}", v.shape, _mybir.dt.from_np(v.dtype), kind="ExternalInput").ap()
          for k, v in arrays.items()}
    out = nc.dram_tensor("out", (N, D), _mybir.dt.float32, kind="ExternalOutput").ap()
    program(nc, io, out)
    r = _run(nc, [{f"in_{k}": v for k, v in arrays.items()}], core_ids=[0])
    return r.results[0]["out"]
```

```python
from contextlib import ExitStack, contextmanager

import concourse.bass as bass
from concourse import mybir

F32 = mybir.dt.float32
BF16 = mybir.dt.bfloat16
I32 = mybir.dt.int32
ALU = mybir.AluOpType
ACT = mybir.ActivationFunctionType
AX = mybir.AxisListType

P = 128
D = 64
N = 6250
E = 206250
SLOTS = 16
HALF = SLOTS // 2
GROUP = 4
GROUPS = SLOTS // GROUP
TURNS = -(-E // (P * SLOTS))
T = TURNS * SLOTS
ROW = SLOTS * P
NT = 50
NROWS = NT * P
BANK = 512
CHUNKS = 16
CW = 404
NCOLS = CHUNKS * CW
RELS = 8
BASES = 4
LAYERS = 3
COPIES = 4
PARTS = 3
BIG = 3.0e38
EPS = 1e-5
NODE_SLOTS = 5

GAP_BITS = ((GROUP - 1) * P).bit_length()
assert (GROUP - 1) * GAP_BITS < 31 and GAP_BITS == 9
assert NROWS >= N + 1 + P and NCOLS >= N + P

WIDTHS = [
    ("kv1", 128), ("qq1", 96), ("comb1", 64), ("self1", 64),
    ("kv2", 128), ("qq2", 96), ("comb2", 64), ("self2", 64),
    ("skip_h1", 64), ("skip_h2", 64),
    ("root0", 64), ("root1", 64), ("root2", 64),
    ("w1", 128), ("w2", 64), ("b2", 64), ("ln_g", 128), ("ln_b", 128), ("eps", 1),
    ("w_l", 64), ("w_e", 64), ("w_r", 64),
    ("pick96", 64), ("pick64", 64),
    ("ident", 128), ("iota", 128), ("below", 128), ("minus_lane", 1), ("one", 1), ("trash", 1),
    ("q1_t", 65), ("e1_t", 32), ("q2_t", 65), ("e2_t", 32),
]
WCOL = {}
_at = 0
for _name, _w in WIDTHS:
    WCOL[_name] = (_at, _w)
    _at += _w
WTOTAL = _at


class Buffers:

    def __init__(self, nc, ctx):
        self.nc = nc

        def sb(name, shape, dt):
            return ctx.enter_context(nc.sbuf_tensor(name, shape, dt))

        self.places = sb("places", [1, TURNS * 2 * GROUPS], I32)
        self.node_a = sb("node_a", [P, NCOLS], F32)
        self.node_b = sb("node_b", [P, NCOLS], F32)
        self.query = sb("query", [P, NCOLS], F32)
        self.acc = sb("acc", [P, N + GROUP * P + 2], F32)
        self.x = sb("x", [P, NT * D], F32)
        self.weights = sb("weights", [P, WTOTAL], F32)
        self.rel_w = sb("rel_w", [D, LAYERS * RELS * D], F32)
        self.src_ids = sb("src_ids", [P, T + SLOTS], I32)
        self.rel_ids = sb("rel_ids", [P, T + SLOTS], I32)
        self.dst_off = sb("dst_off", [P, T + SLOTS], F32)
        self.rel_wt = sb("rel_wt", [P, T + SLOTS], F32)
        self.is_last = sb("is_last", [P, T], F32)
        self.score = sb("score", [P, T + SLOTS], F32)
        self.ring_hot = sb("ring_hot", [P, 18 * SLOTS], F32)
        self.ring = sb("ring", [P, SLOTS, P], F32)
        self.ids = sb("ids", [P, SLOTS], I32)
        self.edge_t = sb("edge_t", [P, ROW], F32)
        self.hot = sb("hot", [P, 4, P], F32)
        self.bcast_w = sb("bcast_w", [2, P], BF16)
        self.psum = ctx.enter_context(nc.psum_tensor("psum", [P, 8, 512], F32))

    def w(self, name, rows=P):
        a, n = WCOL[name]
        return self.weights[0:rows, a:a + n]

    def ident(self, n=P):
        a = WCOL["ident"][0]
        return self.weights[0:n, a:a + n]


@contextmanager
def stage(nc):
    before = nc.snapshot_sems()
    with ExitStack() as ctx:
        yield ctx
    nc.clear_and_free_semaphores(nc.allocated_since(before))
    nc.all_engine_barrier()


def tiles_of(g):
    return range(g * GROUP, (g + 1) * GROUP)


def load_places(eng, b, i, first, count):
    registers = [eng.alloc_register(name=f"place{k}_{b.nc.next_id()}") for k in range(count)]
    eng.load(registers, b.places[0:1, bass.ds(i * 2 * GROUPS + first, count)])
    return registers


def group_starts(eng, b, i):
    return [eng.snap(r, min_val=0, max_val=N, donate=True) for r in load_places(eng, b, i, 0, GROUPS)]


def gaps_of(packed):
    return [0] + [((packed >> (u * GAP_BITS)) & ((1 << GAP_BITS) - 1)).with_bounds(min_val=0, max_val=(GROUP - 1) * P)
                  for u in range(GROUP - 1)]


def packed_gaps(eng, registers):
    return [eng.snap(r, min_val=0, max_val=(1 << (GROUP - 1) * GAP_BITS) - 1, donate=True) for r in registers]


def group_gaps(eng, b, i):
    return packed_gaps(eng, load_places(eng, b, i, GROUPS, GROUPS))


def window_starts(eng, b, i):
    registers = load_places(eng, b, i, 0, 2 * GROUPS)
    firsts = [eng.snap(r, min_val=0, max_val=N, donate=True) for r in registers[:GROUPS]]
    gaps = packed_gaps(eng, registers[GROUPS:])
    return lambda g: [(firsts[g] + gap).with_bounds(min_val=0, max_val=N) if v else firsts[g]
                      for v, gap in enumerate(gaps_of(gaps[g]))]


def sems(nc, ctx, *names):
    return [nc.alloc_semaphore(name=f"{n}_{nc.next_id()}") for n in names]


def by_slot(columns):
    return columns[:, 0:T].rearrange("p (i u) -> p u i", u=SLOTS)


def load_inputs(nc, b, io):
    with stage(nc) as ctx:
        loaded, chain, folded, kept = sems(nc, ctx, "in_loaded", "in_chain", "in_folded", "in_kept")
        basis = b.acc[0:D, 0:LAYERS * BASES * D].rearrange("c (l b h) -> c l b h", l=LAYERS, b=BASES)
        comp = b.acc[0:D, LAYERS * BASES * D:LAYERS * BASES * D + LAYERS * RELS * BASES]
        windows = b.ring[0:1, :, :].rearrange("p u n -> p (u n)")[:, 0:T].bitcast(I32)
        block = ctx.enter_context(nc.Block())

        @block.sync
        def _(sp):
            sp.dma_start(b.weights[:, :], io["weights"]).then_inc(loaded, 16)
            sp.dma_start(b.acc[0:D, 0:LAYERS * BASES * D], io["basis"]).then_inc(loaded, 16)
            sp.dma_start(comp, io["comp"]).then_inc(loaded, 16)
            sp.dma_start(b.node_a[0:D + 1, :], io["x_t"]).then_inc(loaded, 16)
            sp.dma_start(b.x[:, :], io["x_rows"]).then_inc(loaded, 16)
            sp.dma_start(b.src_ids[:, :], io["src_lane"]).then_inc(loaded, 16)
            sp.dma_start(b.rel_ids[:, :], io["type_lane"]).then_inc(loaded, 16)
            sp.dma_start(windows, io["window"]).then_inc(loaded, 16)
            sp.wait_ge(loaded, 128)

        @block.tensor
        def _(pe):
            pe.wait_ge(loaded, 128)
            for n in (1, 2):
                pe.matmul(b.psum[0:65, n, 0:32], lhsT=b.w(f"q{n}_t", D), rhs=b.w(f"e{n}_t", D),
                          start=True, stop=True).then_inc(folded, 1)

        @block.vector
        def _(dve):
            done = [0]

            def link(ins):
                done[0] += 1
                ins.then_inc(chain, 1)
                dve.wait_ge(chain, done[0])

            dve.wait_ge(loaded, 128)
            factors = comp.rearrange("c (l r k) -> c l r k", l=LAYERS, r=RELS)
            product = b.query[0:D, 0:RELS * D].rearrange("c (r h) -> c r h", r=RELS)
            for l in range(LAYERS):
                out = b.rel_w[:, l * RELS * D:(l + 1) * RELS * D].rearrange("c (r h) -> c r h", r=RELS)
                for k in range(BASES):
                    link(dve.tensor_tensor(product if k else out, basis[:, l, k:k + 1, :].broadcast_to([D, RELS, D]),
                                           factors[:, l, :, k:k + 1].broadcast_to([D, RELS, D]), ALU.mult))
                    if k:
                        link(dve.tensor_tensor(out, out, product, ALU.add))
            starts = windows.rearrange("o (i g u) -> o i g u", g=GROUPS, u=GROUP)
            spare = b.edge_t[0:1, 0:T].bitcast(I32).rearrange("o (i g u) -> o i g u", g=GROUPS, u=GROUP)
            first, packed = (b.places[:, :].rearrange("o (i k g) -> o i k g", k=2, g=GROUPS)[:, :, k, :]
                             for k in range(2))
            link(dve.tensor_copy(first, starts[:, :, :, 0]))
            link(dve.tensor_tensor(packed, starts[:, :, :, 1], first, ALU.subtract))
            for u in range(2, GROUP):
                gap = spare[:, :, :, u]
                link(dve.tensor_tensor(gap, starts[:, :, :, u], first, ALU.subtract))
                link(dve.tensor_scalar(gap, gap, (u - 1) * GAP_BITS, None, ALU.logical_shift_left))
                link(dve.tensor_tensor(packed, packed, gap, ALU.bitwise_or))
            link(dve.scalar_tensor_tensor(out=b.rel_ids[:, :], in0=b.src_ids[:, :], scalar=float(RELS),
                                          in1=b.rel_ids[:, :], op0=ALU.mult, op1=ALU.add))
            for columns in (b.dst_off, b.rel_wt, b.score):
                link(dve.memset(columns[:, T:T + SLOTS], 0.0))
            dve.memset(b.node_b[64:65, :], 1.0).then_inc(kept, 1)
            dve.memset(b.bcast_w[0:2, :], 1.0).then_inc(kept, 1)
            dve.wait_ge(kept, 2)
            dve.memset(b.bcast_w[0:1, :], float(P)).then_inc(kept, 1)
            dve.wait_ge(folded, 2)
            for n in (1, 2):
                a = WCOL[f"qq{n}"][0] + D
                dve.tensor_copy(b.weights[0:65, a:a + 32], b.psum[0:65, n, 0:32]).then_inc(kept, 1)
            dve.wait_ge(kept, 5)


def turn_view(buffer, n):
    return buffer[0:TURNS, n * ROW:(n + 1) * ROW]


def carry_rows(pe, b, cols, n, carry_ready, carry_turned, k):
    pe.wait_ge(carry_ready, 2 * k + 1)
    for j in range(2):
        ins = pe.transpose(b.psum[0:n, 4 + j, 0:TURNS], cols[0:TURNS, j, 0:n], b.ident(TURNS))
    ins.then_inc(carry_turned, 1)
    pe.wait_ge(carry_ready, 2 * k + 2)
    pe.transpose(b.psum[0:TURNS, 7, 0:n], b.hot[0:n, 2, 0:TURNS], b.ident(n)).then_inc(carry_turned, 1)


def carry_scan(dve, link, b, n, ops, start, backward, into, carry_ready, carry_turned, k):
    lasts, flags, out = b.hot[0:n, 0, 0:TURNS], b.hot[0:n, 1, 0:TURNS], b.hot[0:n, 3, 0:TURNS]
    shifted = b.hot[0:n, 2, 0:TURNS]
    dve.wait_ge(carry_turned, 2 * k + 1)
    link(dve.tensor_copy(lasts, b.psum[0:n, 4, 0:TURNS]))
    link(dve.tensor_copy(flags, b.psum[0:n, 5, 0:TURNS]))
    link(dve.memset(shifted, start))
    if backward:
        link(dve.tensor_tensor_scan(out[:, ::-1], flags[:, ::-1], lasts[:, ::-1], start, *ops))
        link(dve.tensor_copy(shifted[:, 0:TURNS - 1], out[:, 1:TURNS]))
    else:
        link(dve.tensor_tensor_scan(out, flags, lasts, start, *ops))
        link(dve.tensor_copy(shifted[:, 1:TURNS], out[:, 0:TURNS - 1]))
    dve.sem_inc(carry_ready, 1)
    dve.wait_ge(carry_turned, 2 * k + 2)
    link(dve.tensor_copy(into, b.psum[0:TURNS, 7, 0:n]))


def lanes_from_turns(pe, b, source, ready, count, turned):
    pe.wait_ge(ready, count)
    for u in range(SLOTS):
        ins = pe.transpose(b.psum[:, u // 4, (u % 4) * P:(u % 4) * P + TURNS],
                           source[:, u * P:(u + 1) * P], b.ident(TURNS))
    ins.then_inc(turned, 1)


def copy_lanes(dve, link, b, columns):
    for q in range(4):
        link(dve.tensor_copy(by_slot(columns)[:, 4 * q:4 * q + 4, :],
                             b.psum[:, q, :].rearrange("p (u e) -> p u e", e=P)[:, :, 0:TURNS]))


def edge_tables(nc, b, io, rows_dram):
    with stage(nc) as ctx:
        loaded, chain, ready, turned, carry_ready, carry_turned, stored = sems(
            nc, ctx, "et_loaded", "et_chain", "et_ready", "et_turned", "et_carry_ready", "et_carry_turned",
            "et_stored")
        dst_i = b.query[0:TURNS, 0:ROW + 2].bitcast(I32)
        dst = b.query[0:TURNS, ROW + 2:2 * ROW + 4]
        dst_mid = dst[:, 1:ROW + 1]
        onward = turn_view(b.acc, 0)
        back = turn_view(b.acc, 1)
        kind_i = turn_view(b.acc, 2).bitcast(I32)
        kind = b.node_b[0:TURNS, 0:ROW]
        this = b.node_b[0:TURNS, ROW:2 * ROW]
        ahead = b.node_b[0:TURNS, 2 * ROW:3 * ROW]
        behind = b.query[0:TURNS, 2 * ROW + 4:3 * ROW + 4]
        total = b.edge_t[0:TURNS, :]
        src_i = turn_view(b.acc, 2).bitcast(I32)
        part_i = b.node_b[0:TURNS, 0:ROW].bitcast(I32)
        halves = b.ring[0:TURNS, :, :].rearrange("p u e -> p (u e)").bitcast(BF16)
        rows_hi, rows_lo = halves[:, 0:2 * ROW], b.node_b[0:TURNS, ROW:2 * ROW].bitcast(BF16)
        cols = b.score[0:TURNS, 0:2 * RELS * 2].rearrange("p (w j n) -> p w j n", w=2, j=2)
        carried = b.score[0:TURNS, 64:64 + 2 * RELS].rearrange("p (w n) -> p w n", w=2)
        block = ctx.enter_context(nc.Block())

        @block.sync
        def _(sp):
            sp.dma_start(dst_i, io["dst_turn"]).then_inc(loaded, 16)
            sp.dma_start(kind_i, io["type_turn"]).then_inc(loaded, 16)
            sp.wait_ge(ready, 1)
            sp.dma_start(src_i, io["src_turn"]).then_inc(loaded, 16)
            sp.wait_ge(ready, 5)
            sp.dma_start(rows_dram[0].rearrange("(i e) -> i e", i=TURNS), rows_hi).then_inc(stored, 16)
            sp.dma_start(rows_dram[1].rearrange("(i e) -> i e", i=TURNS), rows_lo).then_inc(stored, 16)
            sp.wait_ge(stored, 32)

        @block.tensor
        def _(pe):
            lanes_from_turns(pe, b, this, ready, 1, turned)
            lanes_from_turns(pe, b, ahead, ready, 2, turned)
            carry_rows(pe, b, cols[:, 0], RELS, carry_ready, carry_turned, 0)
            carry_rows(pe, b, cols[:, 1], RELS, carry_ready, carry_turned, 1)
            lanes_from_turns(pe, b, total, ready, 4, turned)

        @block.vector
        def _(dve):
            done = [0]

            def link(ins):
                done[0] += 1
                ins.then_inc(chain, 1)
                dve.wait_ge(chain, done[0])

            dve.wait_ge(loaded, 32)
            link(dve.tensor_copy(dst, dst_i))
            link(dve.tensor_copy(kind, kind_i))
            link(dve.tensor_tensor(onward, dst_mid, dst[:, 0:ROW], ALU.is_equal))
            link(dve.tensor_tensor(back, dst_mid, dst[:, 2:ROW + 2], ALU.is_equal))
            d3 = dst_mid.rearrange("p (u e) -> p u e", e=P)
            link(dve.tensor_tensor(this.rearrange("p (u e) -> p u e", e=P), d3,
                                   d3[:, :, 0:1].broadcast_to([TURNS, SLOTS, P]), ALU.subtract))
            dve.sem_inc(ready, 1)
            link(dve.tensor_scalar(ahead, back, -1.0, 1.0, ALU.mult, ALU.add))
            dve.wait_ge(turned, 1)
            copy_lanes(dve, link, b, b.dst_off)
            dve.sem_inc(ready, 1)
            hi3 = rows_hi.rearrange("p (u w e) -> p u w e", u=SLOTS, w=2)
            dve.wait_ge(turned, 2)
            copy_lanes(dve, link, b, b.is_last)

            scan = (ALU.mult, ALU.add)
            link(dve.tensor_reduce(cols[:, 0, 1, 0:1], onward, AX.X, ALU.min))
            link(dve.tensor_reduce(cols[:, 1, 1, 0:1], back, AX.X, ALU.min))
            for w in range(2):
                link(dve.tensor_copy(cols[:, w, 1, 1:RELS], cols[:, w, 1, 0:1].broadcast_to([TURNS, RELS - 1])))
            for r in range(RELS):
                link(dve.tensor_scalar(this, kind, float(r), None, ALU.is_equal))
                link(dve.tensor_tensor_scan(ahead, onward, this, 0.0, *scan))
                link(dve.tensor_tensor_scan(behind[:, ::-1], back[:, ::-1], this[:, ::-1], 0.0, *scan))
                link(dve.tensor_copy(cols[:, 0, 0, r:r + 1], ahead[:, ROW - 1:ROW]))
                link(dve.tensor_copy(cols[:, 1, 0, r:r + 1], behind[:, 0:1]))
            dve.sem_inc(carry_ready, 1)
            carry_scan(dve, link, b, RELS, scan, 0.0, False, carried[:, 0, :], carry_ready, carry_turned, 0)
            dve.sem_inc(carry_ready, 1)
            carry_scan(dve, link, b, RELS, scan, 0.0, True, carried[:, 1, :], carry_ready, carry_turned, 1)
            link(dve.memset(total, 0.0))
            for r in range(RELS):
                link(dve.tensor_scalar(this, kind, float(r), None, ALU.is_equal))
                link(dve.tensor_tensor_scan(ahead, onward, this, carried[:, 0, r:r + 1], *scan))
                link(dve.tensor_tensor_scan(behind[:, ::-1], back[:, ::-1], this[:, ::-1],
                                            carried[:, 1, r:r + 1], *scan))
                link(dve.tensor_tensor(ahead, ahead, behind, ALU.add))
                link(dve.scalar_tensor_tensor(out=ahead, in0=ahead, scalar=-1.0, in1=this,
                                              op0=ALU.add, op1=ALU.mult))
                link(dve.tensor_tensor(total, total, ahead, ALU.add))
            link(dve.reciprocal(total, total))
            dve.sem_inc(ready, 2)
            dve.wait_ge(turned, 3)
            copy_lanes(dve, link, b, b.rel_wt)

            dve.wait_ge(loaded, 48)
            link(dve.memset(rows_hi, 0.0))
            link(dve.tensor_scalar(part_i, src_i, 7, None, ALU.logical_shift_right))
            link(dve.tensor_copy(hi3[:, :, 0, :], part_i.rearrange("p (u e) -> p u e", e=P)))
            link(dve.tensor_scalar(part_i, src_i, P - 1, None, ALU.bitwise_and))
            lo3 = rows_lo.rearrange("p (u w e) -> p u w e", u=SLOTS, w=2)
            link(dve.tensor_copy(lo3[:, :, 0, :], part_i.rearrange("p (u e) -> p u e", e=P)))
            link(dve.tensor_tensor(lo3[:, :, 1, :], d3,
                                   d3[:, :, 0:1].broadcast_to([TURNS, SLOTS, P]), ALU.subtract))
            dve.sem_inc(ready, 1)
            dve.wait_ge(stored, 32)
            link(dve.memset(b.node_b[64:65, :], 1.0))


def node_rows(nc, b, source, weights, ncols, rows, table):
    tiles, sets = (NODE_SLOTS, 2) if ncols <= P else (1, NODE_SLOTS)
    banks = -(-tiles * ncols // BANK)
    with stage(nc) as ctx:
        staged, made, copied, gate = sems(nc, ctx, "nr_staged", "nr_made", "nr_copied", "nr_gate")
        stored = sems(nc, ctx, *[f"nr_stored{k}" for k in range(sets)])
        held = b.edge_t[:, 0:sets * tiles * P].rearrange("p (k n) -> p k n", k=sets)
        out = b.query[:, 0:sets * tiles * ncols].rearrange("p (k n) -> p k n", k=sets)
        table_rows = table.rearrange("(t p) n -> p t n", p=P)
        turns = NT // (tiles * sets)
        block = ctx.enter_context(nc.Block())

        def products(k):
            return b.psum[:, k * banks:(k + 1) * banks, :].rearrange("p a c -> p (a c)")

        @block.scalar
        def _(act):
            with act.Fori(0, turns) as i:
                for k in range(sets):
                    n = i * sets + k
                    act.wait_ge(made, n + 1)
                    act.sem_inc(gate, 1)
                    act.copy(held[0:rows, k, :], source[0:rows, bass.ds(n * tiles * P, tiles * P)]).then_inc(staged, 1)

        @block.tensor
        def _(pe):
            pe.sem_inc(made, sets)
            with pe.Fori(0, turns) as i:
                for k in range(sets):
                    n = i * sets + k
                    pe.wait_ge(staged, n + 1)
                    pe.wait_ge(copied, n + 1)
                    for t in range(tiles):
                        ins = pe.matmul(products(k)[:, t * ncols:(t + 1) * ncols],
                                        lhsT=held[0:rows, k, t * P:(t + 1) * P], rhs=weights, start=True, stop=True)
                    ins.then_inc(made, 1)

        @block.vector
        def _(dve):
            dve.sem_inc(copied, sets)
            with dve.Fori(0, turns) as i:
                for k in range(sets):
                    dve.wait_ge(made, sets + i * sets + k + 1)
                    dve.wait_ge(stored[k], 16 * i + 16)
                    dve.tensor_copy(out[:, k, :], products(k)[:, 0:tiles * ncols]).then_inc(copied, 1)

        @block.sync
        def _(sp):
            for k in range(sets):
                sp.sem_inc(stored[k], 16)
            with sp.Fori(0, turns) as i:
                for k in range(sets):
                    n = i * sets + k
                    sp.wait_ge(copied, sets + n + 1)
                    sp.dma_start(table_rows[:, bass.ds(n * tiles, tiles), :],
                                 out[:, k, :].rearrange("p (t n) -> p t n", t=tiles)).then_inc(stored[k], 16)
            for k in range(sets):
                sp.wait_ge(stored[k], 16 * turns + 16)


def node_query(nc, b, source, weights):
    with stage(nc) as ctx:
        made, copied, gate = sems(nc, ctx, "nq_made", "nq_copied", "nq_gate")
        block = ctx.enter_context(nc.Block())

        @block.tensor
        def _(pe):
            with pe.Fori(0, CHUNKS // 2) as i:
                for u in range(2):
                    pe.wait_ge(copied, 2 * i + u + 1)
                    pe.sem_inc(gate, 1)
                    pe.matmul(b.psum[0:96, u, 0:CW], lhsT=weights,
                              rhs=source[0:D + 1, bass.ds((2 * i + u) * CW, CW)],
                              start=True, stop=True).then_inc(made, 1)

        @block.scalar
        def _(act):
            act.sem_inc(copied, 2)
            with act.Fori(0, CHUNKS // 2) as i:
                for u in range(2):
                    act.wait_ge(made, 2 * i + u + 1)
                    act.sem_inc(gate, 1)
                    act.copy(b.query[0:96, bass.ds((2 * i + u) * CW, CW)],
                             b.psum[0:96, u, 0:CW]).then_inc(copied, 1)


def first_ids(act, b, index, ids):
    for g in range(GROUPS):
        mine = slice(g * GROUP, (g + 1) * GROUP)
        act.copy(b.ids[:, mine], index[:, mine]).then_inc(ids, 1)


def next_ids(act, b, index, ids, i, g):
    act.copy(b.ids[:, g * GROUP:(g + 1) * GROUP],
             index[:, bass.ds((i + 1) * SLOTS + g * GROUP, GROUP)]).then_inc(ids, 1)


def edge_scores(nc, b, io, table, values):
    with stage(nc) as ctx:
        ids, turned, keyed, scored, picked, gate, offs, kept = sems(
            nc, ctx, "sc_ids", "sc_turned", "sc_keyed", "sc_scored", "sc_picked", "sc_gate", "sc_offs", "sc_kept")
        got = sems(nc, ctx, *[f"sc_got{g}" for g in range(GROUPS)])
        spilled = sems(nc, ctx, "sc_spilled0", "sc_spilled1")
        feats = sems(nc, ctx, "sc_feats0", "sc_feats1")
        off16 = b.hot[:, 0, 0:SLOTS]
        score16 = b.hot[:, 0, SLOTS:2 * SLOTS]
        block = ctx.enter_context(nc.Block())

        @block.gpsimd
        def _(pool):
            with pool.Fori(0, TURNS) as i:
                for g in range(GROUPS):
                    h = g // 2
                    pool.wait_ge(ids, i * GROUPS + g + 1)
                    if g % 2 == 0:
                        pool.wait_ge(spilled[h], 16 * i + 16)
                    pool.wait_ge(turned, i * GROUPS + g + 1)
                    pool.sem_inc(gate, 1)
                    for u in tiles_of(g):
                        pool.indirect_dma_start(
                            out=b.ring[:, u, :], out_offset=None, in_=table,
                            in_offset=bass.IndirectOffsetOnAxis(ap=b.ids[:, u:u + 1], axis=0)).then_inc(got[g], 16)

        @block.sync
        def _(sp):
            for h in range(2):
                sp.sem_inc(spilled[h], 16)
            with sp.Fori(0, TURNS) as i:
                for h in range(2):
                    sp.wait_ge(scored, i * GROUPS + 2 * h + 2)
                    sp.dma_start(b.edge_t[D:D + 32, h * HALF * P:(h + 1) * HALF * P],
                                 io["ea32_t"][:, bass.ds(i * ROW + h * HALF * P, HALF * P)]).then_inc(feats[h], 16)
                    for g in (2 * h, 2 * h + 1):
                        sp.wait_ge(got[g], 16 * GROUP * (i + 1))
                    sp.dma_start(values[:, bass.ds(i * SLOTS + h * HALF, HALF), :],
                                 b.ring[:, h * HALF:(h + 1) * HALF, D:2 * D]).then_inc(spilled[h], 16)
            for h in range(2):
                sp.wait_ge(spilled[h], 16 * TURNS + 16)

        def turn_keys(pe, i, g):
            pe.wait_ge(got[g], 16 * GROUP * (i + 1))
            pe.wait_ge(keyed, i * GROUPS + g + 1)
            pe.sem_inc(gate, 1)
            for u in tiles_of(g):
                ins = pe.transpose(b.psum[0:D, g % 2, (u % GROUP) * P:(u % GROUP + 1) * P], b.ring[:, u, 0:D],
                                   b.ident())
            ins.then_inc(turned, 1)

        def score(pe, i, g, starts):
            pe.wait_ge(keyed, 2 + i * GROUPS + g + 1)
            if g % 2 == 0:
                pe.wait_ge(feats[g // 2], 16 * i + 16)
            pe.wait_ge(picked, i * GROUPS + g + 1)
            pe.sem_inc(gate, 1)
            for u in tiles_of(g):
                ins = pe.matmul(b.psum[:, 2 + g % 2, (u % GROUP) * P:(u % GROUP + 1) * P],
                                lhsT=b.edge_t[0:96, u * P:(u + 1) * P],
                                rhs=b.query[0:96, bass.ds(starts[u % GROUP], P)], start=True, stop=True)
            ins.then_inc(scored, 1)

        def pe_turn(pe, i, last):
            starts_of = window_starts(pe, b, i)
            for g in range(GROUPS):
                starts = starts_of(g)
                if g + 1 < GROUPS:
                    turn_keys(pe, i, g + 1)
                elif not last:
                    turn_keys(pe, i + 1, 0)
                score(pe, i, g, starts)

        @block.tensor
        def _(pe):
            pe.sem_inc(turned, GROUPS)
            pe.sem_inc(scored, GROUPS)
            turn_keys(pe, 0, 0)
            with pe.Fori(0, TURNS - 1) as i:
                pe_turn(pe, i, False)
            pe_turn(pe, TURNS - 1, True)

        @block.scalar
        def _(act):
            act.sem_inc(keyed, 2)
            first_ids(act, b, b.src_ids, ids)
            with act.Fori(0, TURNS) as i:
                for g in range(GROUPS):
                    act.wait_ge(turned, GROUPS + i * GROUPS + g + 1)
                    act.sem_inc(gate, 1)
                    next_ids(act, b, b.src_ids, ids, i, g)
                    act.wait_ge(scored, i * GROUPS + g + 1)
                    act.copy(b.edge_t[0:D, g * GROUP * P:(g + 1) * GROUP * P], b.psum[0:D, g % 2, :]).then_inc(keyed, 1)

        @block.vector
        def _(dve):
            dve.sem_inc(picked, 2)
            with dve.Fori(0, TURNS) as i:
                dve.tensor_copy(off16, b.dst_off[:, bass.ds(i * SLOTS, SLOTS)]).then_inc(offs, 1)
                dve.wait_ge(offs, i + 1)
                for g in range(GROUPS):
                    dve.wait_ge(scored, GROUPS + i * GROUPS + g + 1)
                    for u in tiles_of(g):
                        found = b.psum[:, 2 + g % 2, (u % GROUP) * P:(u % GROUP + 1) * P]
                        ins = dve.scalar_tensor_tensor(
                            out=found, in0=b.w("iota"), scalar=off16[:, u:u + 1], in1=found,
                            op0=ALU.is_equal, op1=ALU.mult, accum_out=score16[:, u:u + 1])
                    ins.then_inc(picked, 1)
                dve.wait_ge(picked, 2 + (i + 1) * GROUPS)
                dve.tensor_copy(b.score[:, bass.ds(i * SLOTS, SLOTS)], score16).then_inc(kept, 1)
                dve.wait_ge(kept, i + 1)


def softmax_parts(nc, b, io):
    with stage(nc) as ctx:
        loaded, chain, turned, carry_ready, carry_turned, shifted, raised = sems(
            nc, ctx, "sm_loaded", "sm_chain", "sm_turned", "sm_carry_ready", "sm_carry_turned", "sm_shifted",
            "sm_raised")
        dst = b.query[0:TURNS, 0:ROW + 2].bitcast(I32)
        by_turn = b.query[0:TURNS, ROW + 2:2 * ROW + 2]
        ahead = b.query[0:TURNS, 2 * ROW + 2:3 * ROW + 2]
        onward, back, behind = (turn_view(b.acc, k) for k in range(3))
        cols = b.ring[0:TURNS, 0, 0:4].rearrange("p (w j n) -> p w j n", w=2, j=2)
        carried = b.ring[0:TURNS, 1, 0:2]
        block = ctx.enter_context(nc.Block())

        @block.sync
        def _(sp):
            sp.dma_start(dst, io["dst_turn"]).then_inc(loaded, 16)

        @block.tensor
        def _(pe):
            for u in range(SLOTS):
                ins = pe.transpose(b.psum[0:TURNS, u // 4, (u % 4) * P:(u % 4 + 1) * P],
                                   by_slot(b.score)[:, u, :], b.ident())
            ins.then_inc(turned, 1)
            carry_rows(pe, b, cols[:, 0], 1, carry_ready, carry_turned, 0)
            carry_rows(pe, b, cols[:, 1], 1, carry_ready, carry_turned, 1)
            lanes_from_turns(pe, b, by_turn, raised, 1, turned)

        @block.scalar
        def _(act):
            act.wait_ge(shifted, 1)
            act.activation(by_turn, by_turn, ACT.Exp, scale=float(D) ** -0.5).then_inc(raised, 1)

        @block.vector
        def _(dve):
            done = [0]

            def link(ins):
                done[0] += 1
                ins.then_inc(chain, 1)
                dve.wait_ge(chain, done[0])

            dve.wait_ge(loaded, 16)
            for flag, lo in ((onward, 0), (back, 2)):
                link(dve.tensor_tensor(flag, dst[:, 1:ROW + 1], dst[:, lo:lo + ROW], ALU.is_equal))
                link(dve.tensor_scalar(flag, flag, 2 * BIG / 2, None, ALU.mult))
                link(dve.tensor_scalar(flag, flag, -BIG / 2, 2.0, ALU.add, ALU.mult))
            dve.wait_ge(turned, 1)
            for q in range(4):
                link(dve.tensor_copy(by_turn[:, q * 512:(q + 1) * 512], b.psum[0:TURNS, q, :]))
            scan = (ALU.min, ALU.max)
            link(dve.tensor_reduce(cols[:, 0, 1, :], onward, AX.X, ALU.min))
            link(dve.tensor_reduce(cols[:, 1, 1, :], back, AX.X, ALU.min))
            link(dve.tensor_tensor_scan(ahead, onward, by_turn, -BIG, *scan))
            link(dve.tensor_tensor_scan(behind[:, ::-1], back[:, ::-1], by_turn[:, ::-1], -BIG, *scan))
            link(dve.tensor_copy(cols[:, 0, 0, :], ahead[:, ROW - 1:ROW]))
            link(dve.tensor_copy(cols[:, 1, 0, :], behind[:, 0:1]))
            dve.sem_inc(carry_ready, 1)
            carry_scan(dve, link, b, 1, scan, -BIG, False, carried[:, 0:1], carry_ready, carry_turned, 0)
            dve.sem_inc(carry_ready, 1)
            carry_scan(dve, link, b, 1, scan, -BIG, True, carried[:, 1:2], carry_ready, carry_turned, 1)
            link(dve.tensor_tensor_scan(ahead, onward, by_turn, carried[:, 0:1], *scan))
            link(dve.tensor_tensor_scan(behind[:, ::-1], back[:, ::-1], by_turn[:, ::-1], carried[:, 1:2], *scan))
            link(dve.tensor_tensor(ahead, ahead, behind, ALU.max))
            dve.tensor_tensor(by_turn, by_turn, ahead, ALU.subtract).then_inc(shifted, 1)
            dve.wait_ge(turned, 2)
            copy_lanes(dve, link, b, b.score)


ATTEND, RELATE, AVERAGE = range(3)
SUM_ROWS = {ATTEND: 97, RELATE: 64, AVERAGE: 82}


def sum_edges(nc, b, io, what, source):
    rows = SUM_ROWS[what]
    weight = {ATTEND: b.score, RELATE: b.rel_wt, AVERAGE: None}[what]
    index = {ATTEND: None, RELATE: b.rel_ids, AVERAGE: b.src_ids}[what]
    with stage(nc) as ctx:
        ids, hot, summed, added, gate, offs, cleared, extra, zeroed = sems(
            nc, ctx, "su_ids", "su_hot", "su_summed", "su_added", "su_gate", "su_offs", "su_cleared", "su_extra",
            "su_zeroed")
        got = sems(nc, ctx, *[f"su_got{g}" for g in range(GROUPS)]) if index is not None else None
        rows_in = sems(nc, ctx, *[f"su_rows{k}" for k in range(GROUPS if what == ATTEND else 2)])
        off16, wt16 = b.ring_hot[:, 0:SLOTS], b.ring_hot[:, SLOTS:2 * SLOTS]
        feats16 = b.ring_hot[:, 2 * SLOTS:18 * SLOTS].rearrange("p (u f) -> p u f", u=SLOTS)
        hots = b.edge_t[:, :].rearrange("p (g u n) -> p g u n", g=GROUPS, u=GROUP)
        zeros = b.query[0:1, 0:320].bitcast(BF16)
        own = range(GROUP - 1, GROUP) if what == ATTEND else range(0)
        columns, shaped, act_hot = sems(nc, ctx, "su_columns", "su_shaped", "su_act_hot")
        away_hot = b.hot[:, 0:2, :]
        act_off, act_wt, act_minus = (b.hot[:, 2, k * SLOTS:(k + 1) * SLOTS] for k in range(3))
        block = ctx.enter_context(nc.Block())

        if what == ATTEND:
            @block.scalar
            def _(act):
                with act.Fori(0, TURNS) as i:
                    now = bass.ds(i * SLOTS, SLOTS)
                    act.copy(act_off, b.dst_off[:, now]).then_inc(columns, 1)
                    act.copy(act_wt, weight[:, now]).then_inc(columns, 1)
                    act.mul(act_minus, weight[:, now], -1.0).then_inc(columns, 1)
                    act.wait_ge(columns, 3 * i + 3)
                    for g in range(GROUPS):
                        for k, v in enumerate(own):
                            u = g * GROUP + v
                            act.activation(away_hot[:, k, :], b.w("iota"), ACT.Abs, bias=act_off[:, u:u + 1],
                                           scale=-1.0).then_inc(shaped, 1)
                        act.wait_ge(shaped, len(own) * (i * GROUPS + g + 1))
                        act.wait_ge(summed, i * GROUPS + g + 1)
                        for k, v in enumerate(own):
                            u = g * GROUP + v
                            ins = act.activation(hots[:, g, v, :], away_hot[:, k, :], ACT.Relu,
                                                 bias=act_wt[:, u:u + 1], scale=act_minus[:, u:u + 1])
                        ins.then_inc(act_hot, 1)
                        act.wait_ge(act_hot, i * GROUPS + g + 1)

        if index is not None:
            @block.gpsimd
            def _(pool):
                with pool.Fori(0, TURNS) as i:
                    for g in range(GROUPS):
                        pool.wait_ge(ids, i * GROUPS + g + 1)
                        pool.wait_ge(summed, i * GROUPS + g + 1)
                        pool.sem_inc(gate, 1)
                        for u in tiles_of(g):
                            pool.indirect_dma_start(
                                out=b.ring[:, u, 0:D], out_offset=None, in_=source,
                                in_offset=bass.IndirectOffsetOnAxis(ap=b.ids[:, u:u + 1], axis=0)
                            ).then_inc(got[g], 16)

            @block.scalar
            def _(act):
                first_ids(act, b, index, ids)
                with act.Fori(0, TURNS) as i:
                    for g in range(GROUPS):
                        act.wait_ge(summed, GROUPS + i * GROUPS + g + 1)
                        act.sem_inc(gate, 1)
                        next_ids(act, b, index, ids, i, g)

        if what != RELATE:
            @block.sync
            def _(sp):
                with sp.Fori(0, TURNS) as i:
                    if what == ATTEND:
                        for g in range(GROUPS):
                            mine, there = slice(g * GROUP, (g + 1) * GROUP), bass.ds(i * SLOTS + g * GROUP, GROUP)
                            sp.wait_ge(summed, i * GROUPS + g + 1)
                            sp.dma_start(b.ring[:, mine, 0:D], source[:, there, :]).then_inc(rows_in[g], 16)
                            sp.dma_start(b.ring[:, mine, D:D + 32], io["ea32"][:, there, :]).then_inc(rows_in[g], 16)
                    else:
                        for h in range(2):
                            sp.wait_ge(extra, 2 * (2 * i + h) + 2)
                            sp.dma_start(feats16[:, h * HALF:(h + 1) * HALF, :],
                                         io["ea16"][:, bass.ds(i * SLOTS + h * HALF, HALF), :]).then_inc(
                                             rows_in[h], 16)

        @block.tensor
        def _(pe):
            pe.sem_inc(summed, GROUPS)
            pe.wait_ge(zeroed, 1)
            with pe.Fori(0, TURNS) as i:
                gaps = group_gaps(pe, b, i)
                for g in range(GROUPS):
                    away = gaps_of(gaps[g])
                    pe.wait_ge(added, i * GROUPS + g + 1)
                    bank = b.psum[0:rows, g, :]
                    pe.matmul(bank, lhsT=zeros[:, 0:rows], rhs=zeros[:, P:P + 512], start=True, stop=False,
                              skip_group_check=True)
                    if index is not None:
                        pe.wait_ge(got[g], 16 * GROUP * (i + 1))
                    if what == ATTEND:
                        pe.wait_ge(rows_in[g], 32 * i + 32)
                    if what == AVERAGE and g % 2 == 0:
                        pe.wait_ge(extra, 4 + 2 * (2 * i + g // 2) + 2)
                    pe.wait_ge(hot, i * GROUPS + g + 1)
                    if own:
                        pe.wait_ge(act_hot, i * GROUPS + g + 1)
                    pe.sem_inc(gate, 1)
                    for v, u in enumerate(tiles_of(g)):
                        place = bank[:, 0:P] if v == 0 else b.psum[0:rows, g, bass.ds(away[v], P)]
                        ins = pe.matmul(place, lhsT=b.ring[:, u, 0:rows], rhs=hots[:, g, v, :],
                                        start=False, stop=(v == GROUP - 1), skip_group_check=True)
                    ins.then_inc(summed, 1)

        def make_hots(dve, i, g):
            dve.wait_ge(summed, i * GROUPS + g + 1)
            for v, u in enumerate(tiles_of(g)):
                if v in own:
                    continue
                if weight is None:
                    ins = dve.tensor_scalar(hots[:, g, v, :], b.w("iota"), off16[:, u:u + 1], None, ALU.is_equal)
                else:
                    ins = dve.tensor_scalar(hots[:, g, v, :], b.w("iota"), off16[:, u:u + 1],
                                            wt16[:, u:u + 1], ALU.is_equal, ALU.mult)
            ins.then_inc(hot, 1)

        def fetch(dve, i):
            dve.tensor_copy(off16, b.dst_off[:, bass.ds(i * SLOTS, SLOTS)]).then_inc(offs, 1)
            if weight is not None:
                dve.tensor_copy(wt16, weight[:, bass.ds(i * SLOTS, SLOTS)]).then_inc(offs, 1)
            else:
                dve.sem_inc(offs, 1)
            dve.wait_ge(offs, 2 * i + 2)

        def mark_last(dve, i, h):
            half = slice(h * HALF, (h + 1) * HALF)
            dve.wait_ge(rows_in[h], 16 * i + 16)
            dve.wait_ge(summed, i * GROUPS + 2 * h + 2)
            flag = b.is_last[:, bass.ds(i * SLOTS + h * HALF, HALF)].rearrange("p (u o) -> p u o", o=1)
            dve.tensor_tensor(b.ring[:, half, 65:81], feats16[:, half, :],
                              flag.broadcast_to([P, HALF, 16]), ALU.mult).then_inc(extra, 1)
            dve.tensor_copy(b.ring[:, half, 81:82], flag).then_inc(extra, 1)

        @block.vector
        def _(dve):
            dve.memset(zeros, 0.0).then_inc(zeroed, 1)
            dve.sem_inc(added, GROUPS)
            if what == AVERAGE:
                dve.sem_inc(extra, 4)
            dve.memset(b.acc[0:rows, :], 0.0).then_inc(cleared, 1)
            if what != RELATE:
                one = D if what == AVERAGE else 96
                dve.memset(b.ring[:, :, one:one + 1], 1.0).then_inc(cleared, 1)
                dve.wait_ge(cleared, 2)
            else:
                dve.wait_ge(cleared, 1)
            fetch(dve, 0)
            make_hots(dve, 0, 0)
            make_hots(dve, 0, 1)
            with dve.Fori(0, TURNS) as i:
                starts = group_starts(dve, b, i)
                for g in range(GROUPS):
                    if what == AVERAGE and g % 2 == 0:
                        mark_last(dve, i, g // 2)
                    if g == GROUPS - 2:
                        dve.wait_ge(hot, (i + 1) * GROUPS)
                        fetch(dve, i + 1)
                    make_hots(dve, i if g + 2 < GROUPS else i + 1, (g + 2) % GROUPS)
                    dve.wait_ge(summed, GROUPS + i * GROUPS + g + 1)
                    dve.wait_ge(added, GROUPS + i * GROUPS + g)
                    place = b.acc[0:rows, bass.ds(starts[g], GROUP * P)]
                    dve.tensor_tensor(place, place, b.psum[0:rows, g, :], ALU.add).then_inc(added, 1)


def divide_sums(nc, b, top, under, least, beside, relu, source, target):
    rows = top.shape[0]
    with stage(nc) as ctx:
        made, kept, gate, step = sems(nc, ctx, "ds_made", "ds_kept", "ds_gate", "ds_step")
        t = b.edge_t[0:D, 0:2 * CW].rearrange("p (u n) -> p u n", u=2)
        block = ctx.enter_context(nc.Block())

        @block.tensor
        def _(pe):
            with pe.Fori(0, CHUNKS // 2) as i:
                for u in range(2):
                    at = bass.ds((2 * i + u) * CW, CW)
                    pe.wait_ge(step, 4 * (2 * i + u) + 4)
                    pe.sem_inc(gate, 1)
                    pe.matmul(b.psum[0:D, 4 * u, 0:CW], lhsT=top, rhs=b.acc[0:rows, at], start=True, stop=True)
                    pe.matmul(b.psum[0:D, 4 * u + 1, 0:CW], lhsT=under, rhs=b.acc[0:rows, at],
                              start=True, stop=True)
                    for k, (w, array, r) in enumerate(beside):
                        ins = pe.matmul(b.psum[0:D, 4 * u + 2, 0:CW], lhsT=w, rhs=array[0:r, at],
                                        start=(k == 0), stop=(k == len(beside) - 1))
                    ins.then_inc(made, 1)

        @block.vector
        def _(dve):
            dve.sem_inc(step, 8)
            dve.sem_inc(kept, 2)
            with dve.Fori(0, CHUNKS // 2) as i:
                for u in range(2):
                    n = 2 * i + u
                    dve.wait_ge(made, n + 1)
                    dve.wait_ge(kept, n + 1)
                    dve.tensor_scalar(t[:, u, :], b.psum[0:D, 4 * u + 1, 0:CW], least, None,
                                      ALU.max).then_inc(step, 1)
                    dve.wait_ge(step, 8 + 4 * n + 1)
                    dve.reciprocal(t[:, u, :], t[:, u, :]).then_inc(step, 1)
                    dve.wait_ge(step, 8 + 4 * n + 2)
                    dve.tensor_tensor(t[:, u, :], b.psum[0:D, 4 * u, 0:CW], t[:, u, :], ALU.mult).then_inc(step, 1)
                    dve.wait_ge(step, 8 + 4 * n + 3)
                    dve.tensor_tensor(t[:, u, :], t[:, u, :], b.psum[0:D, 4 * u + 2, 0:CW],
                                      ALU.add).then_inc(step, 1)

        @block.scalar
        def _(act):
            with act.Fori(0, CHUNKS // 2) as i:
                for u in range(2):
                    n = 2 * i + u
                    act.wait_ge(step, 8 + 4 * n + 4)
                    act.sem_inc(gate, 1)
                    act.activation(target[0:D, bass.ds(n * CW, CW)], t[:, u, :], ACT.Relu if relu else ACT.Copy
                                   ).then_inc(kept, 1)


def add_root(nc, b, root, features):
    with stage(nc) as ctx:
        made, read, gate, step = sems(nc, ctx, "ar_made", "ar_read", "ar_gate", "ar_step")
        t = b.edge_t[0:D, 0:2 * CW].rearrange("p (u n) -> p u n", u=2)
        block = ctx.enter_context(nc.Block())

        @block.tensor
        def _(pe):
            with pe.Fori(0, CHUNKS // 2) as i:
                for u in range(2):
                    pe.wait_ge(read, 2 * i + u + 1)
                    pe.sem_inc(gate, 1)
                    pe.matmul(b.psum[0:D, u, 0:CW], lhsT=root, rhs=features[0:D + 1, bass.ds((2 * i + u) * CW, CW)],
                              start=True, stop=True).then_inc(made, 1)

        @block.vector
        def _(dve):
            dve.sem_inc(read, 2)
            with dve.Fori(0, CHUNKS // 2) as i:
                for u in range(2):
                    n = 2 * i + u
                    dve.wait_ge(made, n + 1)
                    dve.tensor_tensor(t[:, u, :], b.acc[0:D, bass.ds(n * CW, CW)], b.psum[0:D, u, 0:CW],
                                      ALU.add).then_inc(step, 1)
                    dve.wait_ge(step, n + 1)
                    dve.tensor_scalar(features[0:D, bass.ds(n * CW, CW)], t[:, u, :], 0.0, None,
                                      ALU.max).then_inc(read, 1)


def by_sets(nc, b, parts, width, finish):
    with stage(nc) as ctx:
        staged, made, read, gate = sems(nc, ctx, "bs_staged", "bs_made", "bs_read", "bs_gate")
        m = len(parts)
        turns = NT // (2 * NODE_SLOTS)
        held = [a.rearrange("p (m n) -> p m n", m=2) for a in
                (b.edge_t[:, 0:2 * NODE_SLOTS * P], b.ring.rearrange("p u n -> p (u n)")[:, 0:2 * NODE_SLOTS * P])]
        block = ctx.enter_context(nc.Block())

        def products(k):
            return b.psum[:, 2 * k:2 * k + 2, :].rearrange("p a c -> p (a c)")

        @block.scalar
        def _(act):
            with act.Fori(0, turns) as i:
                for k in range(2):
                    n = 2 * i + k
                    act.wait_ge(made, n + 1)
                    act.sem_inc(gate, 1)
                    for j, (array, rows, cols, _) in enumerate(parts):
                        size = NODE_SLOTS * cols
                        act.copy(held[k][0:rows, j, 0:size], array[0:rows, bass.ds(n * size, size)]
                                 ).then_inc(staged, 1)

        @block.tensor
        def _(pe):
            pe.sem_inc(made, 2)
            with pe.Fori(0, turns) as i:
                for k in range(2):
                    n = 2 * i + k
                    pe.wait_ge(staged, m * n + m)
                    pe.wait_ge(read, n + 1)
                    pe.sem_inc(gate, 1)
                    for t in range(NODE_SLOTS):
                        for j, (_, rows, cols, w) in enumerate(parts):
                            tile = held[k][0:rows, j, t * cols:(t + 1) * cols]
                            if w is None:
                                ins = pe.transpose(products(k)[0:cols, t * width:(t + 1) * width], tile, b.ident())
                            else:
                                ins = pe.matmul(products(k)[:, t * width:(t + 1) * width], lhsT=tile, rhs=w,
                                                start=(j == 0), stop=(j == m - 1))
                    ins.then_inc(made, 1)

        @block.vector
        def _(dve):
            dve.sem_inc(read, 2)
            with dve.Fori(0, turns) as i:
                for k in range(2):
                    n = 2 * i + k
                    dve.wait_ge(made, 2 + n + 1)
                    dve.sem_inc(gate, 1)
                    finish(dve, n, products(k)[:, 0:NODE_SLOTS * width]).then_inc(read, 1)


def add_norm(nc, b, parts, relu, out):
    with stage(nc) as ctx:
        staged, made, read, gate, chain, asked, rooted, normed, stored = sems(
            nc, ctx, "an_staged", "an_made", "an_read", "an_gate", "an_chain", "an_asked", "an_rooted", "an_normed",
            "an_stored")
        m = len(parts)
        size = NODE_SLOTS * P
        width = NODE_SLOTS * D
        turns = NT // (2 * NODE_SLOTS)
        held = [a.rearrange("p (m n) -> p m n", m=2) for a in
                (b.edge_t[:, 0:2 * size], b.ring.rearrange("p u n -> p (u n)")[:, 0:2 * size])]
        spare = b.hot.rearrange("p a n -> p (a n)")
        squares = spare[:, 0:width].rearrange("p (t d) -> p t d", d=D)
        mean = spare[:, width:width + NODE_SLOTS]
        var = spare[:, width + NODE_SLOTS:width + 2 * NODE_SLOTS]
        block = ctx.enter_context(nc.Block())

        def wide(column):
            return column.rearrange("p (t o) -> p t o", o=1).broadcast_to([P, NODE_SLOTS, D])

        @block.scalar
        def _(act):
            def stage_in(n, k):
                act.wait_ge(made, n + 1)
                act.sem_inc(gate, 1)
                for j, (array, rows, _) in enumerate(parts):
                    act.copy(held[k][0:rows, j, :], array[0:rows, bass.ds(n * size, size)]).then_inc(staged, 1)

            def root(n):
                act.wait_ge(asked, n + 1)
                act.sqrt(var, var).then_inc(rooted, 1)

            stage_in(0, 0)
            with act.Fori(0, turns - 1) as i:
                for k in range(2):
                    stage_in(2 * i + k + 1, 1 - k)
                    root(2 * i + k)
            stage_in(2 * turns - 1, 1)
            root(2 * turns - 2)
            root(2 * turns - 1)

        @block.tensor
        def _(pe):
            pe.sem_inc(made, 2)
            with pe.Fori(0, turns) as i:
                for k in range(2):
                    n = 2 * i + k
                    pe.wait_ge(staged, m * n + m)
                    pe.wait_ge(read, n + 1)
                    for t in range(NODE_SLOTS):
                        for j, (_, rows, w) in enumerate(parts):
                            ins = pe.matmul(b.psum[:, k, t * D:(t + 1) * D], lhsT=held[k][0:rows, j, t * P:(t + 1) * P],
                                            rhs=w, start=(j == 0), stop=(j == m - 1))
                    ins.then_inc(made, 1)

        @block.vector
        def _(dve):
            dve.sem_inc(read, 2)
            with dve.Fori(0, turns) as i:
                for k in range(2):
                    n = 2 * i + k
                    steps = [0]

                    def link(ins):
                        steps[0] += 1
                        ins.then_inc(chain, 1)
                        dve.wait_ge(chain, 5 * n + steps[0])

                    x = b.x[:, bass.ds(n * width, width)]
                    rows = x.rearrange("p (t d) -> p t d", d=D)
                    dve.wait_ge(made, 2 + n + 1)
                    dve.scalar_tensor_tensor(out=x, in0=b.psum[:, k, 0:width], scalar=0.0 if relu else -BIG, in1=x,
                                             op0=ALU.max, op1=ALU.add).then_inc(read, 1)
                    dve.wait_ge(read, 2 + n + 1)
                    dve.sem_inc(gate, 1)
                    link(dve.tensor_reduce(mean, rows, AX.X, ALU.add))
                    link(dve.scalar_tensor_tensor(out=rows, in0=wide(mean), scalar=-1.0 / D, in1=rows,
                                                  op0=ALU.mult, op1=ALU.add))
                    link(dve.tensor_tensor(squares, rows, rows, ALU.mult))
                    link(dve.tensor_reduce(var, squares, AX.X, ALU.add))
                    dve.tensor_scalar(var, var, 1.0 / D, EPS, ALU.mult, ALU.add).then_inc(asked, 1)
                    dve.wait_ge(rooted, n + 1)
                    link(dve.reciprocal(var, var))
                    dve.tensor_tensor(rows, rows, wide(var), ALU.mult).then_inc(normed, 1)
                    dve.wait_ge(normed, n + 1)

        @block.sync
        def _(sp):
            whole = 2 * turns - 1
            tiles = out[0:whole * size, :].rearrange("(t p) d -> p t d", p=P)
            with sp.Fori(0, whole) as n:
                sp.wait_ge(normed, n + 1)
                sp.dma_start(tiles[:, bass.ds(n * NODE_SLOTS, NODE_SLOTS), :],
                             b.x[:, bass.ds(n * width, width)].rearrange("p (t d) -> p t d", d=D)).then_inc(stored, 16)
            sp.wait_ge(normed, 2 * turns)
            full = out.shape[0] // P
            rest = out.shape[0] - full * P
            sp.dma_start(out[whole * size:full * P, :].rearrange("(t p) d -> p t d", p=P),
                         b.x[:, whole * width:full * D].rearrange("p (t d) -> p t d", d=D)).then_inc(stored, 16)
            if rest:
                sp.dma_start(out[full * P:, :], b.x[0:rest, full * D:(full + 1) * D]).then_inc(stored, 16)
            sp.wait_ge(stored, 16 * (whole + (2 if rest else 1)))


def normalize(dve, link, rows, width, spare, stats, root):
    mean, var = stats[:, 0:NT], stats[:, NT:2 * NT]

    def wide(column):
        return column.rearrange("p (t o) -> p t o", o=1).broadcast_to([P, NT, width])

    link(dve.tensor_reduce(mean, rows, AX.X, ALU.add))
    link(dve.tensor_scalar(mean, mean, 1.0 / width, None, ALU.mult))
    link(dve.tensor_tensor(rows, rows, wide(mean), ALU.subtract))
    link(dve.tensor_tensor(spare, rows, rows, ALU.mult))
    link(dve.tensor_reduce(var, spare, AX.X, ALU.add))
    link(dve.tensor_scalar(var, var, 1.0 / width, EPS, ALU.mult, ALU.add))
    root()
    link(dve.reciprocal(var, var))
    link(dve.tensor_tensor(rows, rows, wide(var), ALU.mult))


def turn_nodes(nc, b, rows, width, turned_to):
    def finish(dve, n, turned):
        return dve.tensor_copy(turned_to[0:width, bass.ds(n * NODE_SLOTS * P, NODE_SLOTS * P)], turned[0:width, :])

    by_sets(nc, b, [(rows, P, width, None)], P, finish)


def split_x(nc, b, out):
    with stage(nc) as ctx:
        chain, split, stored = sems(nc, ctx, "sx_chain", "sx_split", "sx_stored")
        x = b.x[:, :].rearrange("p (t d) -> p t d", d=D)
        rest = b.acc[:, 0:NT * D].rearrange("p (t d) -> p t d", d=D)
        parts = b.query[:, 0:NT * PARTS * D // 2].bitcast(BF16).rearrange("p (t k d) -> p t k d", t=NT, k=PARTS)
        block = ctx.enter_context(nc.Block())

        @block.vector
        def _(dve):
            done = [0]

            def link(ins):
                done[0] += 1
                ins.then_inc(chain, 1)
                dve.wait_ge(chain, done[0])

            link(dve.tensor_copy(parts[:, :, 0, :], x))
            link(dve.tensor_tensor(rest, x, parts[:, :, 0, :], ALU.subtract))
            link(dve.tensor_copy(parts[:, :, 1, :], rest))
            link(dve.tensor_tensor(rest, rest, parts[:, :, 1, :], ALU.subtract))
            dve.tensor_copy(parts[:, :, 2, :], rest).then_inc(split, 1)

        @block.sync
        def _(sp):
            sp.wait_ge(split, 1)
            sp.dma_start(out.rearrange("(t p) w -> p t w", p=P), parts.rearrange("p t k d -> p t (k d)")
                         ).then_inc(stored, 16)
            sp.wait_ge(stored, 16)


def scatter_messages(nc, b, io, table, rows_dram, partial):
    with stage(nc) as ctx:
        broadcast, spread, apart, hot, moved, joined, ordered, offs = sems(
            nc, ctx, "me_broadcast", "me_spread", "me_apart", "me_hot", "me_moved", "me_joined", "me_ordered",
            "me_offs")
        message, relued, copied, zeroed, cleared, freed = sems(
            nc, ctx, "me_message", "me_relued", "me_copied", "me_zeroed", "me_cleared", "me_freed")
        key_rows = sems(nc, ctx, "me_key_rows0", "me_key_rows1")
        feats = sems(nc, ctx, "me_feats0", "me_feats1")
        windows = sems(nc, ctx, *[f"me_windows{g}" for g in range(GROUPS)])
        sent = sems(nc, ctx, *[f"me_sent{k}" for k in range(COPIES)])
        big = b.query
        o = [0]

        def take(n):
            o[0] += n
            return big[:, o[0] - n:o[0]]

        win = take(SLOTS * PARTS * D // 2).bitcast(BF16).rearrange("p (u k d) -> p u k d", u=SLOTS, k=PARTS)
        feat = take(SLOTS * D).rearrange("p (u d) -> p u d", u=SLOTS)
        keys = take(ROW)[0:2, :].bitcast(BF16).rearrange("p (u w) -> p u w", u=SLOTS)
        apart_hot = b.hot[:, 0:2, :].bitcast(BF16).rearrange("p a (v e) -> p (a v) e", e=P)
        out_hot = b.hot[:, 2:4, :].bitcast(BF16).rearrange("p a (v e) -> p (a v) e", e=P)
        same, before = (b.edge_t[:, k * 2 * GROUP * P:(k + 1) * 2 * GROUP * P].rearrange(
            "p (g u n) -> p g u n", g=2, u=GROUP) for k in range(2))
        msg = take(2 * GROUP * D).rearrange("p (g u d) -> p g u d", g=2, u=GROUP)
        total = take(GROUPS * GROUP * D).rearrange("p (g u d) -> p g u d", g=GROUPS, u=GROUP)
        src_all, row_all, spare_all = b.rel_wt, b.node_b[:, 0:T + SLOTS], b.score
        high_all = b.node_b[:, T + SLOTS:2 * (T + SLOTS)]
        src_f = take(SLOTS)
        row_f = take(SLOTS)
        spare = take(SLOTS)
        earlier = take(SLOTS)
        moves = take(SLOTS)
        ids = b.ids
        of_src, of_dst = (b.psum[:, 2 * w:2 * w + 2, :].rearrange("p g (v e) -> p g v e", v=GROUP) for w in range(2))
        block = ctx.enter_context(nc.Block())

        @block.sync
        def _(sp):
            with sp.Fori(0, TURNS) as i:
                starts_of = window_starts(sp, b, i)
                for g in range(GROUPS):
                    starts = starts_of(g)
                    sp.wait_ge(message, i * GROUPS + g + 1)
                    for v, u in enumerate(tiles_of(g)):
                        sp.dma_start(win[:, u, :, :].rearrange("p k d -> p (k d)"),
                                     table[bass.ds(starts[v], P), :]).then_inc(windows[g], 16)

        def load_keys(act, i, h):
            half = slice(h * HALF, (h + 1) * HALF)
            act.dma_start(keys[:, half, :].rearrange("o u w -> o (u w)"),
                          rows_dram[:, bass.ds((i * SLOTS + h * HALF) * 2 * P, HALF * 2 * P)]
                          ).then_inc(key_rows[h], 16)

        def load_feats(act, i, h):
            act.dma_start(feat[:, h * HALF:(h + 1) * HALF, :],
                          io["ea64"][:, bass.ds(i * SLOTS + h * HALF, HALF), :]).then_inc(feats[h], 16)

        def bcast(pe, i, g):
            if g % 2 == 0:
                pe.wait_ge(key_rows[g // 2], 16 * i + 16)
            pe.wait_ge(spread, i * GROUPS + g + 1)
            pe.wait_ge(hot, i * GROUPS + g + 1)
            for w, to in enumerate((of_src, of_dst)):
                ins = pe.matmul(to[:, g % 2, :, :], lhsT=b.bcast_w[0:2, :],
                                rhs=keys[0:2, g * GROUP:(g + 1) * GROUP, w * P:(w + 1) * P], start=True, stop=True)
            ins.then_inc(broadcast, 1)

        def pick_rows(pe, i, g):
            pe.wait_ge(windows[g], 16 * GROUP * (i + 1))
            pe.wait_ge(hot, 2 + i * GROUPS + g + 1)
            pe.wait_ge(message, GROUPS - 2 + i * GROUPS + g + 1)
            for v, u in enumerate(tiles_of(g)):
                for k in range(PARTS):
                    ins = pe.matmul(b.psum[:, 4 + g % 2, v * D:(v + 1) * D], lhsT=out_hot[:, v, :],
                                    rhs=win[:, u, k, :], start=(k == 0), stop=(k == PARTS - 1))
            ins.then_inc(moved, 1)

        def join(pe, i, g):
            pe.wait_ge(relued, i * GROUPS + g + 1)
            pe.wait_ge(copied, i * GROUPS + g + 1)
            for v in range(GROUP):
                ins = pe.matmul(b.psum[:, 6 + g % 2, v * D:(v + 1) * D], lhsT=same[:, g % 2, v, :],
                                rhs=msg[:, g % 2, v, :], start=True, stop=True)
            ins.then_inc(joined, 1)

        def pe_turn(pe, i, last, first=False):
            for g in range(GROUPS):
                if g + 1 < GROUPS:
                    bcast(pe, i, g + 1)
                elif not last:
                    bcast(pe, i + 1, 0)
                pick_rows(pe, i, g)
                if g >= 1:
                    join(pe, i, g - 1)
                elif not first:
                    join(pe, i - 1, GROUPS - 1)

        @block.tensor
        def _(pe):
            pe.sem_inc(moved, 1)
            pe.sem_inc(joined, 2)
            bcast(pe, 0, 0)
            pe_turn(pe, 0, False, True)
            with pe.Fori(1, TURNS - 1) as i:
                pe_turn(pe, i, False)
            pe_turn(pe, TURNS - 1, True)
            join(pe, TURNS - 1, GROUPS - 1)

        @block.scalar
        def _(act):
            act.sem_inc(copied, 2)
            act.sem_inc(hot, 2)

            def make_hots(i, g):
                act.wait_ge(broadcast, i * GROUPS + g + 1)
                act.wait_ge(moved, 1 + i * GROUPS + g)
                act.activation(apart_hot, of_dst[:, g % 2, :, :], ACT.Abs, bias=b.w("minus_lane")).then_inc(
                    apart, 1)
                act.wait_ge(apart, i * GROUPS + g + 1)
                act.activation(out_hot, apart_hot, ACT.Relu, bias=b.w("one"),
                               scale=-1.0).then_inc(hot, 1)

            def relu(i, g):
                act.wait_ge(message, GROUPS + i * GROUPS + g + 1)
                act.activation(msg[:, g % 2, :, :], msg[:, g % 2, :, :], ACT.Relu).then_inc(relued, 1)

            def copy(i, g):
                act.wait_ge(joined, 2 + i * GROUPS + g + 1)
                act.wait_ge(freed, i * SLOTS + g * GROUP + GROUP)
                act.copy(total[:, g, :, :], b.psum[:, 6 + g % 2, 0:GROUP * D].rearrange(
                    "p (u d) -> p u d", u=GROUP)).then_inc(copied, 1)

            def act_turn(i, first, last):
                for g in range(GROUPS):
                    relu(i, g)
                    if g % 2 == 1 and not last:
                        load_feats(act, i + 1, g // 2)
                    if g + 1 < GROUPS:
                        make_hots(i, g + 1)
                        if g % 2 == 0 and not last:
                            load_keys(act, i + 1, g // 2)
                    elif not last:
                        make_hots(i + 1, 0)
                    if g >= 1:
                        copy(i, g - 1)
                    elif not first:
                        copy(i - 1, GROUPS - 1)

            for h in range(2):
                load_keys(act, 0, h)
                load_feats(act, 0, h)
            make_hots(0, 0)
            act_turn(0, True, False)
            with act.Fori(1, TURNS - 1) as i:
                act_turn(i, False, False)
            act_turn(TURNS - 1, False, True)
            copy(TURNS - 1, GROUPS - 1)

        @block.vector
        def _(dve):
            dve.memset(b.acc[:, 0:NT * D], 0.0).then_inc(zeroed, 1)
            dve.sem_inc(spread, 2)
            dve.sem_inc(message, GROUPS)

            def add_feats(i, g):
                dve.wait_ge(moved, 1 + i * GROUPS + g + 1)
                if g % 2 == 0:
                    dve.wait_ge(feats[g // 2], 16 * i + 16)
                dve.tensor_tensor(msg[:, g % 2, :, :].rearrange("p u d -> p (u d)"),
                                  b.psum[:, 4 + g % 2, 0:GROUP * D],
                                  feat[:, g * GROUP:(g + 1) * GROUP, :].rearrange("p u d -> p (u d)"),
                                  ALU.add).then_inc(message, 1)

            def fetch(i):
                dve.tensor_copy(src_f, src_all[:, bass.ds(i * SLOTS, SLOTS)]).then_inc(offs, 1)
                dve.tensor_copy(row_f, row_all[:, bass.ds(i * SLOTS, SLOTS)]).then_inc(offs, 1)
                dve.tensor_copy(spare, spare_all[:, bass.ds(i * SLOTS, SLOTS)]).then_inc(offs, 1)

            high_i = high_all.bitcast(I32)
            dve.tensor_scalar(high_i, b.src_ids[:, :], 7, None, ALU.logical_shift_right).then_inc(offs, 1)
            dve.tensor_copy(src_all[:, :], b.src_ids[:, :]).then_inc(offs, 1)
            dve.wait_ge(offs, 2)
            dve.tensor_scalar(row_all, src_all[:, :], float(NT), None, ALU.mult).then_inc(offs, 1)
            dve.wait_ge(offs, 3)
            dve.scalar_tensor_tensor(out=row_all, in0=high_i, scalar=float(1 - P * NT), in1=row_all,
                                     op0=ALU.mult, op1=ALU.add).then_inc(offs, 1)
            dve.wait_ge(offs, 4)
            dve.tensor_scalar(spare_all[:, :], row_all, -1.0, b.w("trash"), ALU.mult, ALU.add).then_inc(offs, 1)
            dve.wait_ge(offs, 5)
            with dve.Fori(0, TURNS) as i:
                fetch(i)
                dve.wait_ge(offs, 5 + 3 * i + 3)
                for g in range(GROUPS):
                    n = i * GROUPS + g
                    dve.wait_ge(broadcast, n + 1)
                    dve.wait_ge(joined, n + 1)
                    dve.tensor_tensor(same[:, g % 2, :, :], of_src[:, g % 2, :, :],
                                      src_f[:, g * GROUP:(g + 1) * GROUP].rearrange("p (u o) -> p u o", o=1)
                                      .broadcast_to([P, GROUP, P]), ALU.is_equal)
                    for v, u in enumerate(tiles_of(g)):
                        ins = dve.scalar_tensor_tensor(
                            out=before[:, g % 2, v, :], in0=of_src[:, g % 2, v, :], scalar=src_f[:, u:u + 1],
                            in1=b.w("below"), op0=ALU.is_equal, op1=ALU.mult, accum_out=earlier[:, u:u + 1])
                    ins.then_inc(spread, 1)
                    add_feats(i, g)
                    mine = slice(g * GROUP, (g + 1) * GROUP)
                    dve.wait_ge(spread, 2 + n + 1)
                    dve.scalar_tensor_tensor(out=moves[:, mine], in0=earlier[:, mine], scalar=0.0, in1=spare[:, mine],
                                             op0=ALU.is_gt, op1=ALU.mult).then_inc(ordered, 1)
                    dve.wait_ge(ordered, 2 * n + 1)
                    dve.wait_ge(freed, i * SLOTS + g * GROUP + GROUP)
                    dve.tensor_tensor(ids[:, mine], moves[:, mine], row_f[:, mine], ALU.add).then_inc(ordered, 1)
                dve.wait_ge(ordered, 2 * GROUPS * (i + 1))

        @block.gpsimd
        def _(pool):
            pool.wait_ge(zeroed, 1)
            for c in range(COPIES):
                pool.dma_start(partial[c].rearrange("(p t) d -> p (t d)", p=P),
                               b.acc[:, 0:NT * D]).then_inc(cleared, 16)
            pool.wait_ge(cleared, 16 * COPIES)
            pool.sem_inc(freed, SLOTS - COPIES)

            def pool_turn(i, first):
                for g in range(GROUPS):
                    pool.wait_ge(copied, 2 + i * GROUPS + g + 1)
                    pool.wait_ge(ordered, 2 * (i * GROUPS + g) + 2)
                    for v, u in enumerate(tiles_of(g)):
                        if not first or u >= COPIES:
                            pool.wait_ge(sent[u % COPIES], 16 * (i * (SLOTS // COPIES) + u // COPIES))
                        pool.sem_inc(freed, 1)
                        pool.indirect_dma_start(
                            out=partial[u % COPIES],
                            out_offset=bass.IndirectOffsetOnAxis(ap=ids[:, u:u + 1], axis=0),
                            in_=total[:, g, v, :], in_offset=None,
                            compute_op=ALU.add).then_inc(sent[u % COPIES], 16)

            pool_turn(0, True)
            with pool.Fori(1, TURNS) as i:
                pool_turn(i, False)
            for c in range(COPIES):
                pool.wait_ge(sent[c], 16 * (SLOTS // COPIES) * TURNS)


def gather_partials(nc, b, partial):
    with stage(nc) as ctx:
        loaded, chain = sems(nc, ctx, "gp_loaded", "gp_chain")
        total = b.acc[:, 0:NT * D]
        parts = [b.query[:, 0:NT * D], b.query[:, NT * D:2 * NT * D],
                 b.node_b[:, 0:NT * D], b.node_b[:, NT * D:2 * NT * D]]
        block = ctx.enter_context(nc.Block())

        @block.sync
        def _(sp):
            for k in range(COPIES):
                sp.dma_start(parts[k], partial[k].rearrange("(p t) d -> p (t d)", p=P)).then_inc(loaded, 16)
            sp.wait_ge(loaded, 16 * COPIES)

        @block.vector
        def _(dve):
            done = [0]

            def link(ins):
                done[0] += 1
                ins.then_inc(chain, 1)
                dve.wait_ge(chain, done[0])

            dve.wait_ge(loaded, 16 * COPIES)
            link(dve.tensor_tensor(parts[0], parts[0], parts[1], ALU.add))
            link(dve.tensor_tensor(parts[2], parts[2], parts[3], ALU.add))
            link(dve.tensor_tensor(parts[0], parts[0], parts[2], ALU.add))
            link(dve.scalar_tensor_tensor(out=total, in0=b.x[:, :], scalar=b.w("eps"), in1=b.x[:, :],
                                          op0=ALU.mult, op1=ALU.add))
            link(dve.tensor_tensor(total, total, parts[0], ALU.add))


def widen(nc, b):
    def finish(dve, n, wide):
        return dve.tensor_copy(b.query[:, bass.ds(n * NODE_SLOTS * P, NODE_SLOTS * P)], wide)

    by_sets(nc, b, [(b.node_b, D + 1, P, b.w("w1", D + 1))], P, finish)


def norm_wide(nc, b):
    with stage(nc) as ctx:
        chain, asked, rooted = sems(nc, ctx, "nw_chain", "nw_asked", "nw_rooted")
        z = b.query[:, 0:NT * P].rearrange("p (t d) -> p t d", d=P)
        spare = b.acc[:, 0:NT * P].rearrange("p (t d) -> p t d", d=P)
        stats = b.hot[:, 0, :]
        var = stats[:, NT:2 * NT]
        block = ctx.enter_context(nc.Block())

        def each_node(w):
            return w.rearrange("p (o d) -> p o d", o=1).broadcast_to([P, NT, P])

        @block.vector
        def _(dve):
            done = [0]

            def link(ins):
                done[0] += 1
                ins.then_inc(chain, 1)
                dve.wait_ge(chain, done[0])

            def root():
                dve.sem_inc(asked, 1)
                dve.wait_ge(rooted, 1)

            normalize(dve, link, z, P, spare, stats, root)
            link(dve.tensor_tensor(z, z, each_node(b.w("ln_g")), ALU.mult))
            link(dve.tensor_tensor(z, z, each_node(b.w("ln_b")), ALU.add))
            link(dve.tensor_scalar(z, z, 0.0, None, ALU.max))

        @block.scalar
        def _(act):
            act.wait_ge(asked, 1)
            act.sqrt(var, var).then_inc(rooted, 1)


def program(nc, io, out):
    def dram(name, shape, dt=F32):
        return nc.dram_tensor(name, shape, dt, kind="Internal").ap()

    kv_table = dram("kv_table", (NROWS, 2 * D))
    values = dram("values", (P, T, D))
    rel_table = dram("rel_table", (NROWS, RELS * D))
    x_table = dram("x_table", (NROWS, D))
    x_parts = dram("x_parts", (NROWS, PARTS * D), BF16)
    rows_dram = dram("rows_dram", (2, T * 2 * P), BF16)
    partial = [dram(f"partial{k}", (NROWS, D)) for k in range(COPIES)]

    with ExitStack() as ctx:
        b = Buffers(nc, ctx)
        load_inputs(nc, b, io)
        edge_tables(nc, b, io, rows_dram)

        for n, source, target in ((1, b.node_a, b.node_b), (2, b.node_b, b.node_a)):
            node_rows(nc, b, source, b.w(f"kv{n}", 65), 2 * D, 65, kv_table)
            node_query(nc, b, source, b.w(f"qq{n}", 65))
            edge_scores(nc, b, io, kv_table, values)
            softmax_parts(nc, b, io)
            sum_edges(nc, b, io, ATTEND, values)
            divide_sums(nc, b, b.w(f"comb{n}", 97), b.w("pick96", 97), 1e-30,
                        [(b.w(f"self{n}", 65), source, 65)], True, source, target)
        add_norm(nc, b, [(b.node_b, 64, b.w("skip_h1", 64)), (b.node_a, 65, b.w("skip_h2", 65))], True, x_table)
        turn_nodes(nc, b, b.x, D, b.node_a)

        for l in range(LAYERS):
            node_rows(nc, b, b.node_a, b.rel_w[:, l * RELS * D:(l + 1) * RELS * D], RELS * D, 64, rel_table)
            sum_edges(nc, b, io, RELATE, rel_table.rearrange("n (r d) -> (n r) d", d=D))
            if l < LAYERS - 1:
                add_root(nc, b, b.w(f"root{l}", 65), b.node_a)
        add_norm(nc, b, [(b.acc, 64, b.ident(64)), (b.node_a, 65, b.w("root2", 65))], False, x_table)

        split_x(nc, b, x_parts)
        scatter_messages(nc, b, io, x_parts, rows_dram, partial)
        gather_partials(nc, b, partial)
        restore_one(nc, b)
        turn_nodes(nc, b, b.acc, D, b.node_b)
        widen(nc, b)
        norm_wide(nc, b)
        turn_nodes(nc, b, b.query, P, b.acc)
        add_norm(nc, b, [(b.acc, P, b.w("w2", P)), (b.node_b, 65, b.w("b2", 65))], False, x_table)
        turn_nodes(nc, b, b.x, D, b.node_a)

        sum_edges(nc, b, io, AVERAGE, x_table)
        divide_sums(nc, b, b.w("w_l", 82), b.w("pick64", 82), 1.0,
                    [(b.w("w_r", 65), b.node_a, 65), (b.w("w_e", 82), b.acc, 82)], False, b.node_a, b.node_b)
        add_norm(nc, b, [(b.node_b, 64, b.ident(64))], False, out)


def restore_one(nc, b):
    with stage(nc) as ctx:
        (set_,) = sems(nc, ctx, "ro_set")
        block = ctx.enter_context(nc.Block())

        @block.vector
        def _(dve):
            dve.memset(b.node_b[64:65, :], 1.0).then_inc(set_, 1)


def kernel(**inputs):
    import numpy as np
    import concourse.bacc as _bacc
    from concourse import mybir as _mybir
    from concourse.bass_utils import run_bass_kernel_spmd as _run

    a = {k: np.asarray(v) for k, v in inputs.items()}
    f4, i4 = np.float32, np.int32

    def lane(values, fill, extra=0):
        out = np.full(((T + extra) * P,) + values.shape[1:], fill, values.dtype)
        out[:E] = values
        out = out.reshape((T + extra, P) + values.shape[1:])
        return np.ascontiguousarray(np.swapaxes(out, 0, 1))

    def turn(values, fill):
        out = np.full(T * P, fill, values.dtype)
        out[:E] = values
        return out

    weights = np.zeros((P, WTOTAL), f4)

    def put(name, block, row=0, col=0):
        at = WCOL[name][0] + col
        block = np.atleast_2d(block)
        weights[row:row + block.shape[0], at:at + block.shape[1]] = block

    for n in (1, 2):
        w = {k: a[f"L0_gnn_{k[0]}{n}{k[1:]}"] for k in ("q_w", "q_b", "k_w", "k_b", "v_w", "v_b", "e_w", "s_w", "s_b")}
        put(f"kv{n}", w["k_w"])
        put(f"kv{n}", w["v_w"], 0, D)
        put(f"kv{n}", w["k_b"], 64)
        put(f"kv{n}", w["v_b"], 64, D)
        put(f"qq{n}", w["q_w"])
        put(f"qq{n}", w["q_b"], 64)
        put(f"q{n}_t", w["q_w"].T)
        put(f"q{n}_t", w["q_b"][:, None], 0, 64)
        put(f"e{n}_t", w["e_w"].T)
        put(f"comb{n}", np.eye(D, dtype=f4))
        put(f"comb{n}", w["e_w"], 64)
        put(f"self{n}", w["s_w"])
        put(f"self{n}", w["s_b"], 64)
    put("skip_h1", a["L0_gnn_skip_w"][:D])
    put("skip_h2", a["L0_gnn_skip_w"][D:])
    put("skip_h2", a["L0_gnn_skip_b"], 64)
    for l in range(LAYERS):
        put(f"root{l}", a["L1_gnn_root"][l])
        put(f"root{l}", a["L1_gnn_bias"][l], 64)
    put("w1", a["L2_gnn_W1"])
    put("w1", a["L2_gnn_b1"], 64)
    put("w2", a["L2_gnn_W2"])
    put("b2", a["L2_gnn_b2"], 64)
    put("ln_g", np.broadcast_to(a["L2_gnn_ln_g"], (P, P)))
    put("ln_b", np.broadcast_to(a["L2_gnn_ln_b"], (P, P)))
    put("eps", np.broadcast_to(a["L2_gnn_eps"], (P, 1)))
    put("w_l", a["L3_gnn_W_l"])
    put("w_r", a["L3_gnn_W_r"])
    put("w_r", a["L3_gnn_b_l"], 64)
    put("w_e", a["L3_gnn_W_e"], 65)
    put("w_e", a["L3_gnn_b_e"], 81)
    lanes = np.arange(P, dtype=f4)
    put("pick96", np.ones((1, D), f4), 96)
    put("pick64", np.ones((1, D), f4), 64)
    put("ident", np.eye(P, dtype=f4))
    put("iota", np.broadcast_to(lanes, (P, P)))
    put("below", np.tril(np.ones((P, P), f4), -1))
    put("minus_lane", -lanes[:, None])
    put("one", np.ones((P, 1), f4))
    spare = np.arange(N + 1, N + 1 + P)
    put("trash", (spare % P * NT + spare // P).astype(f4)[:, None])

    x = a["x"]
    x_pad = np.zeros((NROWS, D), f4)
    x_pad[:N] = x
    x_t = np.zeros((D + 1, NCOLS), f4)
    x_t[:D, :N] = x.T
    x_t[D] = 1.0
    dst = turn(a["dst"], N)
    ext = np.concatenate([np.full(1, -1, i4), dst, np.full(1, -1, i4)])
    dst_turn = np.stack([ext[i * ROW:i * ROW + ROW + 2] for i in range(TURNS)])
    ea32_t = np.zeros((32, T * P), f4)
    ea32_t[:, :E] = a["edge_attr_32"].T

    arrays = {
        "weights": weights,
        "basis": np.ascontiguousarray(a["L1_gnn_basis"].transpose(2, 0, 1, 3).reshape(D, -1)),
        "comp": np.ascontiguousarray(np.broadcast_to(a["L1_gnn_comp"].reshape(1, -1), (D, LAYERS * RELS * BASES))),
        "x_t": x_t,
        "x_rows": np.ascontiguousarray(x_pad.reshape(NT, P, D).transpose(1, 0, 2).reshape(P, NT * D)),
        "src_lane": lane(a["src"], N, SLOTS),
        "type_lane": lane(a["edge_type_8"], 0, SLOTS),
        "window": np.ascontiguousarray(dst.reshape(T, P)[:, 0].reshape(1, T)),
        "dst_turn": dst_turn,
        "type_turn": turn(a["edge_type_8"], 0).reshape(TURNS, ROW),
        "src_turn": turn(a["src"], N).reshape(TURNS, ROW),
        "ea32_t": ea32_t,
        "ea32": lane(a["edge_attr_32"], 0),
        "ea16": lane(a["edge_attr_16"], 0),
        "ea64": lane(a["edge_attr_64"], 0),
    }
    nc = _bacc.Bacc("TRN2", target_bir_lowering=False, num_devices=1)
    io = {k: nc.dram_tensor(f"in_{k}", v.shape, _mybir.dt.from_np(v.dtype), kind="ExternalInput").ap()
          for k, v in arrays.items()}
    out = nc.dram_tensor("out", (N, D), _mybir.dt.float32, kind="ExternalOutput").ap()
    program(nc, io, out)
    r = _run(nc, [{f"in_{k}": v for k, v in arrays.items()}], core_ids=[0])
    return r.results[0]["out"]
```
